# Optimizing a Trainium2 kernel written in Bass

```python
import numpy as np
import jax
import jax.numpy as jnp

def _softmax(x, axis=-1):
    return jax.nn.softmax(x, axis=axis)

def _gelu(x):
    return jax.nn.gelu(x, approximate=True)

def _silu(x):
    return jax.nn.silu(x)

def _sigmoid(x):
    return jax.nn.sigmoid(x)

def _layernorm(x, axis=-1, eps=1e-05):
    m = jnp.mean(x, axis=axis, keepdims=True)
    v = jnp.var(x, axis=axis, keepdims=True)
    return (x - m) / jnp.sqrt(v + eps)

def _scatter_add(tgt, idx, src, axis=0):
    return tgt.at[idx].add(src)

def _segment_sum(src, seg, n):
    return jax.ops.segment_sum(src, seg, n)
kernel_name = 'mk_decoder_postln_d4_seqx_r8_eefd1d'

def setup_inputs(seed: int=0):
    np.random.seed(seed)
    _w = jnp.asarray

    def _rec_inputs():
        import jax
        import jax.numpy as jnp
        _rk = jax.random.key(seed)
        x = -0.0002928 + 1 * jax.random.normal(jax.random.fold_in(_rk, 1), (4, 256, 128), jnp.float32)
        _lenS = 256 - jax.random.randint(jax.random.fold_in(_rk, 7), (4,), 0, max(1, 256 // 4) + 1, jnp.int32)
        _lenS2 = 64 - jax.random.randint(jax.random.fold_in(_rk, 8), (4,), 0, max(1, 64 // 4) + 1, jnp.int32)
        _ctx_1024P = jax.random.normal(jax.random.fold_in(_rk, 11), (4, 16, 128), jnp.float32)
        _ctx_1024c = jax.random.dirichlet(jax.random.fold_in(_rk, 511), 0.3 * jnp.ones((16,), jnp.float32), (4, 64))
        _ctx_1024t = jnp.einsum('bsk,bkd->bsd', _ctx_1024c, _ctx_1024P)
        _ctx_1024t = _ctx_1024t * jax.lax.rsqrt(jnp.mean(jnp.square(_ctx_1024t)) + 1e-12) * 0.953939
        ctx_1024 = -1.39393e-06 + 0.999914 * (_ctx_1024t + 0.3 * jax.random.normal(jax.random.fold_in(_rk, 611), (4, 64, 128), jnp.float32))
        _validS = jnp.arange(256)[None, :] < _lenS[:, None]
        _validS2 = jnp.arange(64)[None, :] < _lenS2[:, None]
        _causal = jnp.tril(jnp.ones((256, 256), dtype=bool))
        mask_1x1xSxS2_ik1 = jnp.where(jnp.broadcast_to(_validS2[0:1, None, None, :], (1, 1, 256, 64)), 1, 0).astype(jnp.int32)
        mask_BxSxS2_bk1 = jnp.broadcast_to(_validS2[:, None, :], (4, 256, 64))
        return (x, ctx_1024, mask_1x1xSxS2_ik1, mask_BxSxS2_bk1)
    x, ctx_1024, mask_1x1xSxS2_ik1, mask_BxSxS2_bk1 = _rec_inputs()

    def _L0_attn_setup():
        import jax, jax.numpy as jnp
        import numpy as np
        EMBED = 128
        H = 16
        KV = 4
        D = 64
        K_NODES = 4
        TOP_K = 2
        MAXLEN = 1024
        BASE = 10000.0
        SCALE = D ** (-0.5)
        NEG = -1000000000.0

        def _rotate_half(t):
            h = t.shape[-1] // 2
            return jnp.concatenate([-t[..., h:], t[..., :h]], axis=-1)

        def _rope_cache():
            inv_freq = 1.0 / BASE ** (jnp.arange(0, D, 2, dtype=jnp.float32) / D)
            t = jnp.arange(MAXLEN, dtype=jnp.float32)
            freqs = t[:, None] * inv_freq[None, :]
            emb = jnp.concatenate([freqs, freqs], axis=-1)
            return (jnp.cos(emb), jnp.sin(emb))
        key = jax.random.key(seed)
        ks = jax.random.split(key, 6)
        B, N = (1, 256)
        x = jax.random.normal(ks[0], (B, N, EMBED), jnp.float32)
        wq = 0.02 * jax.random.normal(ks[1], (EMBED, H * D), jnp.float32)
        wk = 0.02 * jax.random.normal(ks[2], (EMBED, KV * D), jnp.float32)
        wv = 0.02 * jax.random.normal(ks[3], (EMBED, KV * D), jnp.float32)
        wr = 0.02 * jax.random.normal(ks[4], (EMBED, H * K_NODES), jnp.float32)
        wo = 0.02 * jax.random.normal(ks[5], (H * D, EMBED), jnp.float32)
        return {'x': x, 'wq': wq, 'wk': wk, 'wv': wv, 'wr': wr, 'wo': wo}
    _L0_attn_all = _L0_attn_setup()
    _L0_attn_in = {k: v for k, v in _L0_attn_all.items() if k in ('wq', 'wk', 'wv', 'wr', 'wo')}
    del _L0_attn_all

    def _L0_xattn_setup():
        import jax, jax.numpy as jnp
        import numpy as np
        D_MODEL = 128
        N_HEAD = 16
        D_K = D_MODEL // N_HEAD
        B, S = (2, 256)
        NEG = -1000000000.0
        key = jax.random.key(seed)
        ks = jax.random.split(key, 9)
        inp = {'input_q': jax.random.normal(ks[0], (B, S, D_MODEL), dtype=jnp.float32), 'input_k': jax.random.normal(ks[1], (B, S, D_MODEL), dtype=jnp.float32), 'input_v': jax.random.normal(ks[2], (B, S, D_MODEL), dtype=jnp.float32), 'mask': jax.random.randint(ks[3], (1, 1, S, S), 0, 2, dtype=jnp.int32), 'w_q': jax.random.normal(ks[4], (D_MODEL, D_MODEL), dtype=jnp.float32) / np.sqrt(D_MODEL), 'w_k': jax.random.normal(ks[5], (D_MODEL, D_MODEL), dtype=jnp.float32) / np.sqrt(D_MODEL), 'w_v': jax.random.normal(ks[6], (D_MODEL, D_MODEL), dtype=jnp.float32) / np.sqrt(D_MODEL), 'w_o': jax.random.normal(ks[7], (D_MODEL, D_MODEL), dtype=jnp.float32) / np.sqrt(D_MODEL), 'b_o': jax.random.normal(ks[8], (D_MODEL,), dtype=jnp.float32) * 0.01}
        return inp
    _L0_xattn_all = _L0_xattn_setup()
    _L0_xattn_in = {k: v for k, v in _L0_xattn_all.items() if k in ('w_q', 'w_k', 'w_v', 'w_o', 'b_o')}
    del _L0_xattn_all

    def _L0_ffn_setup():
        import jax, jax.numpy as jnp
        import numpy as np
        DIM, HEADS, FFN, E = (128, 16, 512, 8)
        B, S = (2, 128)
        EPS = 1e-05

        def _ln(x, g, b):
            mu = jnp.mean(x, axis=-1, keepdims=True)
            var = jnp.mean((x - mu) ** 2, axis=-1, keepdims=True)
            return (x - mu) * jax.lax.rsqrt(var + EPS) * g + b
        key = jax.random.key(seed)
        ks = jax.random.split(key, 20)
        sd = 0.02
        d, f = (DIM, FFN)
        return {'x': jax.random.normal(ks[0], (B, S, d), jnp.float32), 'ln1_g': jnp.ones((d,), jnp.float32), 'ln1_b': jnp.zeros((d,), jnp.float32), 'Wqkv': jax.random.normal(ks[1], (d, 3 * d), jnp.float32) * sd, 'bqkv': jnp.zeros((3 * d,), jnp.float32), 'Wo': jax.random.normal(ks[2], (d, d), jnp.float32) * sd, 'bo': jnp.zeros((d,), jnp.float32), 'ln2_g': jnp.ones((d,), jnp.float32), 'ln2_b': jnp.zeros((d,), jnp.float32), 'gate_w': jax.random.normal(ks[3], (d, E), jnp.float32) * sd, 'W1': jax.random.normal(ks[4], (E, d, f), jnp.float32) * sd, 'b1': jnp.zeros((E, f), jnp.float32), 'W2': jax.random.normal(ks[5], (E, f, d), jnp.float32) * sd, 'b2': jnp.zeros((E, d), jnp.float32), 'rW1': jax.random.normal(ks[6], (d, f), jnp.float32) * sd, 'rb1': jnp.zeros((f,), jnp.float32), 'rW2': jax.random.normal(ks[7], (f, d), jnp.float32) * sd, 'rb2': jnp.zeros((d,), jnp.float32), 'coef_w': jax.random.normal(ks[8], (d, 2), jnp.float32) * sd, 'coef_b': jnp.zeros((2,), jnp.float32)}
    _L0_ffn_all = _L0_ffn_setup()
    _L0_ffn_in = {k: v for k, v in _L0_ffn_all.items() if k in ('ln1_g', 'ln1_b', 'Wqkv', 'bqkv', 'Wo', 'bo', 'ln2_g', 'ln2_b', 'gate_w', 'W1', 'b1', 'W2', 'b2', 'rW1', 'rb1', 'rW2', 'rb2', 'coef_w', 'coef_b')}
    del _L0_ffn_all

    def _L1_attn_setup():
        import jax, jax.numpy as jnp
        import numpy as np
        B, S, DIM, SDIM = (4, 512, 128, 32)
        key = jax.random.key(seed)
        ks = jax.random.split(key, 10)

        def lin(k, din, dout):
            return jax.random.normal(k, (din, dout), jnp.float32) / np.float32(np.sqrt(din))
        return {'x': jax.random.normal(ks[0], (B, S, DIM), jnp.float32), 'ln_g': jnp.ones((DIM,), jnp.float32), 'ln_b': jnp.zeros((DIM,), jnp.float32), 'mix_w': jax.random.normal(ks[1], (DIM, 1, 3), jnp.float32) * 0.3, 'mix_b': jnp.zeros((DIM,), jnp.float32), 'Wi': lin(ks[2], DIM, DIM), 'bi': jnp.zeros((DIM,), jnp.float32), 'Wsin': lin(ks[3], DIM, SDIM), 'bsin': jnp.zeros((SDIM,), jnp.float32), 'Wd': lin(ks[4], DIM, SDIM), 'bd': jnp.zeros((SDIM,), jnp.float32), 'Wsel': lin(ks[5], DIM, SDIM), 'bsel': jnp.zeros((SDIM,), jnp.float32), 'Wso': lin(ks[6], SDIM, DIM), 'bso': jnp.zeros((DIM,), jnp.float32), 'Wg': lin(ks[7], DIM, DIM), 'bg': jnp.zeros((DIM,), jnp.float32), 'Wout': lin(ks[8], DIM, DIM), 'bout': jnp.zeros((DIM,), jnp.float32)}
    _L1_attn_all = _L1_attn_setup()
    _L1_attn_in = {k: v for k, v in _L1_attn_all.items() if k in ('ln_g', 'ln_b', 'mix_w', 'mix_b', 'Wi', 'bi', 'Wsin', 'bsin', 'Wd', 'bd', 'Wsel', 'bsel', 'Wso', 'bso', 'Wg', 'bg', 'Wout', 'bout')}
    del _L1_attn_all

    def _L1_xattn_setup():
        import jax, jax.numpy as jnp
        import numpy as np
        E = 128
        H = 16
        N, S, T = (4, 256, 256)
        key = jax.random.key(seed)
        ks = jax.random.split(key, 11)
        scale = 1.0 / np.sqrt(E)
        inp = {'query': jax.random.normal(ks[0], (N, S, E), jnp.float32), 'key': jax.random.normal(ks[1], (N, T, E), jnp.float32), 'value': jax.random.normal(ks[2], (N, T, E), jnp.float32), 'Wq': jax.random.normal(ks[3], (E, E), jnp.float32) * scale, 'bq': jax.random.normal(ks[4], (E,), jnp.float32) * 0.01, 'Wk': jax.random.normal(ks[5], (E, E), jnp.float32) * scale, 'bk': jax.random.normal(ks[6], (E,), jnp.float32) * 0.01, 'Wv': jax.random.normal(ks[7], (E, E), jnp.float32) * scale, 'bv': jax.random.normal(ks[8], (E,), jnp.float32) * 0.01, 'Wp': jax.random.normal(ks[9], (E, E), jnp.float32) * scale, 'bp': jax.random.normal(ks[10], (E,), jnp.float32) * 0.01}
        return inp
    _L1_xattn_all = _L1_xattn_setup()
    _L1_xattn_in = {k: v for k, v in _L1_xattn_all.items() if k in ('Wq', 'bq', 'Wk', 'bk', 'Wv', 'bv', 'Wp', 'bp')}
    del _L1_xattn_all

    def _L1_ffn_setup():
        import jax, jax.numpy as jnp
        import numpy as np
        E = 16
        F_C = 2.0
        D = 128
        I = 4 * D
        IS = 2 * D
        B, S = (4, 128)
        key = jax.random.key(seed)
        ks = jax.random.split(key, 8)
        w = 0.02
        return {'hidden_states': jax.random.normal(ks[0], (B, S, D), dtype=jnp.float32), 'gate_w': jax.random.normal(ks[1], (E, D), dtype=jnp.float32) * w, 'Wg': jax.random.normal(ks[2], (E, I, D), dtype=jnp.float32) * w, 'Wu': jax.random.normal(ks[3], (E, I, D), dtype=jnp.float32) * w, 'Wd': jax.random.normal(ks[4], (E, D, I), dtype=jnp.float32) * w, 'Sg': jax.random.normal(ks[5], (IS, D), dtype=jnp.float32) * w, 'Su': jax.random.normal(ks[6], (IS, D), dtype=jnp.float32) * w, 'Sd': jax.random.normal(ks[7], (D, IS), dtype=jnp.float32) * w}
    _L1_ffn_all = _L1_ffn_setup()
    _L1_ffn_in = {k: v for k, v in _L1_ffn_all.items() if k in ('gate_w', 'Wg', 'Wu', 'Wd', 'Sg', 'Su', 'Sd')}
    del _L1_ffn_all

    def _L2_attn_setup():
        import jax, jax.numpy as jnp
        import numpy as np
        B, T, D_MODEL, N_HEADS = (2, 256, 128, 16)
        HS = D_MODEL // N_HEADS
        key = jax.random.key(seed)
        k1, k2, k3 = jax.random.split(key, 3)
        x = jax.random.normal(k1, (B, T, D_MODEL), dtype=jnp.float32)
        W_qkv = jax.random.normal(k2, (3 * D_MODEL, D_MODEL), dtype=jnp.float32) * D_MODEL ** (-0.5)
        W_out = jax.random.normal(k3, (D_MODEL, D_MODEL), dtype=jnp.float32) * D_MODEL ** (-0.5)
        return {'x': x, 'W_qkv': W_qkv, 'W_out': W_out}
    _L2_attn_all = _L2_attn_setup()
    _L2_attn_in = {k: v for k, v in _L2_attn_all.items() if k in ('W_qkv', 'W_out')}
    del _L2_attn_all

    def _L2_xattn_setup():
        import jax, jax.numpy as jnp
        import numpy as np
        B, L_ENC, L_DEC, D = (16, 64, 128, 128)
        key = jax.random.key(seed)
        k1, k2, k3, k4, k5, k6 = jax.random.split(key, 6)
        encoder_hc = jax.random.normal(k1, (B, L_ENC, D), dtype=jnp.float32)
        decoder_hq = jax.random.normal(k2, (B, L_DEC, D), dtype=jnp.float32)
        w_sim = jax.random.normal(k3, (3 * D,), dtype=jnp.float32) * 0.02
        b_sim = jax.random.normal(k4, (1,), dtype=jnp.float32) * 0.02
        W_qv = jax.random.normal(k5, (4 * D, D), dtype=jnp.float32) * 0.02
        b_qv = jax.random.normal(k6, (D,), dtype=jnp.float32) * 0.02
        return {'encoder_hc': encoder_hc, 'decoder_hq': decoder_hq, 'w_sim': w_sim, 'b_sim': b_sim, 'W_qv': W_qv, 'b_qv': b_qv}
    _L2_xattn_all = _L2_xattn_setup()
    _L2_xattn_in = {k: v for k, v in _L2_xattn_all.items() if k in ('w_sim', 'b_sim', 'W_qv', 'b_qv')}
    del _L2_xattn_all

    def _L2_ffn_setup():
        import jax, jax.numpy as jnp
        import numpy as np
        EPS = 1e-12

        def rms_norm(t, gamma):
            n = jnp.maximum(jnp.linalg.norm(t, axis=-1, keepdims=True), EPS)
            scale = jnp.sqrt(jnp.asarray(t.shape[-1], t.dtype))
            return t / n * scale * gamma
        key = jax.random.key(seed)
        ks = jax.random.split(key, 4)
        b, s, d = (4, 512, 128)
        e, t = (8, 64)
        hidden = 4 * d
        return {'x': jax.random.normal(ks[0], (b, s, d), dtype=jnp.float32), 'gamma_x': jnp.ones((d,), dtype=jnp.float32), 'gamma_slot': jnp.ones((d,), dtype=jnp.float32), 'slot_embeds': jax.random.normal(ks[1], (e, t, d), dtype=jnp.float32), 'w1': jax.random.normal(ks[2], (d, hidden), dtype=jnp.float32) * (1.0 / np.sqrt(d)), 'w2': jax.random.normal(ks[3], (hidden, d), dtype=jnp.float32) * (1.0 / np.sqrt(hidden))}
    _L2_ffn_all = _L2_ffn_setup()
    _L2_ffn_in = {k: v for k, v in _L2_ffn_all.items() if k in ('gamma_x', 'gamma_slot', 'slot_embeds', 'w1', 'w2')}
    del _L2_ffn_all

    def _L3_attn_setup():
        import jax, jax.numpy as jnp
        import numpy as np
        NUM_HEADS = 16
        LN_EPS = 1e-05

        def _layernorm(x, gamma, beta):
            mu = jnp.mean(x, axis=-1, keepdims=True)
            var = jnp.var(x, axis=-1, keepdims=True)
            return (x - mu) * jax.lax.rsqrt(var + LN_EPS) * gamma + beta
        key = jax.random.key(seed)
        ks = jax.random.split(key, 6)
        B, N, D = (4, 512, 128)
        s = 1.0 / np.sqrt(D)
        return {'x': jax.random.normal(ks[0], (B, N, D), dtype=jnp.float32), 'Wq': jax.random.normal(ks[1], (D, D), dtype=jnp.float32) * s, 'Wk': jax.random.normal(ks[2], (D, D), dtype=jnp.float32) * s, 'Wv': jax.random.normal(ks[3], (D, D), dtype=jnp.float32) * s, 'Wo': jax.random.normal(ks[4], (D, D), dtype=jnp.float32) * s, 'bo': jnp.zeros((D,), dtype=jnp.float32), 'alpha': jax.random.uniform(ks[5], (1,), dtype=jnp.float32), 'temperature': jnp.float32(1.0), 'gamma': jnp.ones((D,), dtype=jnp.float32), 'beta': jnp.zeros((D,), dtype=jnp.float32)}
    _L3_attn_all = _L3_attn_setup()
    _L3_attn_in = {k: v for k, v in _L3_attn_all.items() if k in ('Wq', 'Wk', 'Wv', 'Wo', 'bo', 'alpha', 'temperature', 'gamma', 'beta')}
    del _L3_attn_all

    def _L3_xattn_setup():
        import jax, jax.numpy as jnp
        import numpy as np
        NEG = -1000000000.0
        key0 = jax.random.key(seed)
        ks = jax.random.split(key0, 12)
        N, K, M = (4, 256, 128)
        H, D = (16, 64)
        query = jax.random.normal(ks[0], (N, K, M), dtype=jnp.float32)
        key = jax.random.normal(ks[1], (N, K, M), dtype=jnp.float32)
        value = jax.random.normal(ks[2], (N, K, M), dtype=jnp.float32)
        mask = jax.random.randint(ks[3], (N, K, K), 0, 2).astype(jnp.bool_)
        c_qk = (6.0 / (M + D)) ** 0.5
        c_v = (6.0 / (M + D)) ** 0.5
        c_o = (6.0 / (H * D + M)) ** 0.5
        Wq = jax.random.uniform(ks[4], (H, M, D), minval=-c_qk, maxval=c_qk, dtype=jnp.float32)
        Wk = jax.random.uniform(ks[5], (H, M, D), minval=-c_qk, maxval=c_qk, dtype=jnp.float32)
        Wv = jax.random.uniform(ks[6], (H, M, D), minval=-c_v, maxval=c_v, dtype=jnp.float32)
        bq = jax.random.uniform(ks[7], (H, D), minval=-0.01, maxval=0.01, dtype=jnp.float32)
        bk = jax.random.uniform(ks[8], (H, D), minval=-0.01, maxval=0.01, dtype=jnp.float32)
        bv = jax.random.uniform(ks[9], (H, D), minval=-0.01, maxval=0.01, dtype=jnp.float32)
        Wo = jax.random.uniform(ks[10], (H * D, M), minval=-c_o, maxval=c_o, dtype=jnp.float32)
        bo = jax.random.uniform(ks[11], (M,), minval=-0.01, maxval=0.01, dtype=jnp.float32)
        return {'query': query, 'key': key, 'value': value, 'mask': mask, 'Wq': Wq, 'Wk': Wk, 'Wv': Wv, 'bq': bq, 'bk': bk, 'bv': bv, 'Wo': Wo, 'bo': bo}
    _L3_xattn_all = _L3_xattn_setup()
    _L3_xattn_in = {k: v for k, v in _L3_xattn_all.items() if k in ('Wq', 'Wk', 'Wv', 'bq', 'bk', 'bv', 'Wo', 'bo')}
    del _L3_xattn_all

    def _L3_ffn_setup():
        import jax, jax.numpy as jnp
        import numpy as np
        DIM = 128
        DEPTH = 2
        HEADS = 8
        DIM_HEAD = 64
        WINDOW = 64
        INNER = HEADS * DIM_HEAD
        HID = int(DIM * 4 * 2 / 3)
        B, N = (2, 1024)
        QK_SCALE = 8.0

        def shift_token(t):
            t1, t2 = jnp.split(t, 2, axis=-1)
            t2 = jnp.pad(t2, ((0, 0), (1, 0), (0, 0)))[:, :-1]
            return jnp.concatenate([t1, t2], axis=-1)

        def l2norm(t):
            return t / jnp.clip(jnp.linalg.norm(t, axis=-1, keepdims=True), 1e-12)

        def rotate_half(x):
            x1, x2 = jnp.split(x, 2, axis=-1)
            return jnp.concatenate([-x2, x1], axis=-1)

        def rotary_xpos(q, k):
            n = q.shape[-2]
            half_idx = jnp.arange(0, DIM_HEAD, 2, dtype=jnp.float32)
            inv_freq = 1.0 / 10000.0 ** (half_idx / DIM_HEAD)
            t = jnp.arange(n, dtype=jnp.float32)
            freqs = t[:, None] * inv_freq[None, :]
            freqs = jnp.concatenate([freqs, freqs], axis=-1)
            base = (half_idx + 0.4 * DIM_HEAD) / (1.4 * DIM_HEAD)
            power = (t - n // 2) / float(WINDOW // 2)
            scale = base[None, :] ** power[:, None]
            scale = jnp.concatenate([scale, scale], axis=-1)
            cos, sin = (jnp.cos(freqs), jnp.sin(freqs))
            q = q * cos * scale + rotate_half(q) * sin * scale
            k = k * cos / scale + rotate_half(k) * sin / scale
            return (q, k)

        def local_attention(q, k, v):
            b, h, n, d = q.shape
            w = n // WINDOW
            bq = q.reshape(b, h, w, WINDOW, d) * QK_SCALE
            bk = k.reshape(b, h, w, WINDOW, d)
            bv = v.reshape(b, h, w, WINDOW, d)

            def look_around(t):
                p = jnp.pad(t, ((0, 0), (0, 0), (1, 0), (0, 0), (0, 0)))
                return jnp.concatenate([p[:, :, :w], p[:, :, 1:]], axis=3)
            bk, bv = (look_around(bk), look_around(bv))
            bt = jnp.arange(n).reshape(w, WINDOW)
            btp = jnp.pad(bt, ((1, 0), (0, 0)), constant_values=-1)
            btk = jnp.concatenate([btp[:w], btp[1:]], axis=1)
            sim = jnp.einsum('bhwid,bhwjd->bhwij', bq, bk)
            i = bt[:, :, None]
            j = btk[:, None, :]
            mask = (i < j) | (i > j + WINDOW) | (j == -1)
            sim = jnp.where(mask, -jnp.finfo(sim.dtype).max, sim)
            attn = jax.nn.softmax(sim, axis=-1)
            out = jnp.einsum('bhwij,bhwjd->bhwid', attn, bv)
            return out.reshape(b, h, n, d)

        def _layer(x, wqkv, qs, ksc, wo, lg, lb, w1, b1, w2, b2):
            b, n, _ = x.shape
            h = shift_token(x)
            qkv = h @ wqkv
            q, k, v = jnp.split(qkv, 3, axis=-1)
            to_heads = lambda t: t.reshape(b, n, HEADS, DIM_HEAD).transpose(0, 2, 1, 3)
            q, k, v = (to_heads(q), to_heads(k), to_heads(v))
            q = l2norm(q) * qs
            k = l2norm(k) * ksc
            q, k = rotary_xpos(q, k)
            o = local_attention(q, k, v)
            o = o.transpose(0, 2, 1, 3).reshape(b, n, INNER)
            x = x + o @ wo
            h = shift_token(x)
            mu = h.mean(-1, keepdims=True)
            var = h.var(-1, keepdims=True)
            h = (h - mu) / jnp.sqrt(var + 1e-05) * lg + lb
            h = h @ w1 + b1
            a, g = jnp.split(h, 2, axis=-1)
            h = a * jax.nn.gelu(g, approximate=False)
            x = x + h @ w2 + b2
            return x
        key = jax.random.key(seed)
        ks = jax.random.split(key, 6)
        return {'x': jax.random.normal(ks[0], (B, N, DIM), jnp.float32), 'wqkv': jax.random.normal(ks[1], (DEPTH, DIM, 3 * INNER), jnp.float32) * 0.02, 'q_scale': jnp.ones((DEPTH, DIM_HEAD), jnp.float32), 'k_scale': jnp.ones((DEPTH, DIM_HEAD), jnp.float32), 'wo': jax.random.normal(ks[2], (DEPTH, INNER, DIM), jnp.float32) * 0.02, 'ln_g': jnp.ones((DEPTH, DIM), jnp.float32), 'ln_b': jnp.zeros((DEPTH, DIM), jnp.float32), 'w1': jax.random.normal(ks[3], (DEPTH, DIM, 2 * HID), jnp.float32) * 0.02, 'b1': jnp.zeros((DEPTH, 2 * HID), jnp.float32), 'w2': jax.random.normal(ks[4], (DEPTH, HID, DIM), jnp.float32) * 0.02, 'b2': jnp.zeros((DEPTH, DIM), jnp.float32)}
    _L3_ffn_all = _L3_ffn_setup()
    _L3_ffn_in = {k: v for k, v in _L3_ffn_all.items() if k in ('wqkv', 'q_scale', 'k_scale', 'wo', 'ln_g', 'ln_b', 'w1', 'b1', 'w2', 'b2')}
    del _L3_ffn_all
    return {'x': x, 'ctx_1024': ctx_1024, 'mask_1x1xSxS2_ik1': mask_1x1xSxS2_ik1, 'mask_BxSxS2_bk1': mask_BxSxS2_bk1, 'L0_attn_wq': _L0_attn_in['wq'], 'L0_attn_wk': _L0_attn_in['wk'], 'L0_attn_wv': _L0_attn_in['wv'], 'L0_attn_wr': _L0_attn_in['wr'], 'L0_attn_wo': _L0_attn_in['wo'], 'L0_xattn_w_q': _L0_xattn_in['w_q'], 'L0_xattn_w_k': _L0_xattn_in['w_k'], 'L0_xattn_w_v': _L0_xattn_in['w_v'], 'L0_xattn_w_o': _L0_xattn_in['w_o'], 'L0_xattn_b_o': _L0_xattn_in['b_o'], 'L0_ffn_ln1_g': _L0_ffn_in['ln1_g'], 'L0_ffn_ln1_b': _L0_ffn_in['ln1_b'], 'L0_ffn_Wqkv': _L0_ffn_in['Wqkv'], 'L0_ffn_bqkv': _L0_ffn_in['bqkv'], 'L0_ffn_Wo': _L0_ffn_in['Wo'], 'L0_ffn_bo': _L0_ffn_in['bo'], 'L0_ffn_ln2_g': _L0_ffn_in['ln2_g'], 'L0_ffn_ln2_b': _L0_ffn_in['ln2_b'], 'L0_ffn_gate_w': _L0_ffn_in['gate_w'], 'L0_ffn_W1': _L0_ffn_in['W1'], 'L0_ffn_b1': _L0_ffn_in['b1'], 'L0_ffn_W2': _L0_ffn_in['W2'], 'L0_ffn_b2': _L0_ffn_in['b2'], 'L0_ffn_rW1': _L0_ffn_in['rW1'], 'L0_ffn_rb1': _L0_ffn_in['rb1'], 'L0_ffn_rW2': _L0_ffn_in['rW2'], 'L0_ffn_rb2': _L0_ffn_in['rb2'], 'L0_ffn_coef_w': _L0_ffn_in['coef_w'], 'L0_ffn_coef_b': _L0_ffn_in['coef_b'], 'L1_attn_ln_g': _L1_attn_in['ln_g'], 'L1_attn_ln_b': _L1_attn_in['ln_b'], 'L1_attn_mix_w': _L1_attn_in['mix_w'], 'L1_attn_mix_b': _L1_attn_in['mix_b'], 'L1_attn_Wi': _L1_attn_in['Wi'], 'L1_attn_bi': _L1_attn_in['bi'], 'L1_attn_Wsin': _L1_attn_in['Wsin'], 'L1_attn_bsin': _L1_attn_in['bsin'], 'L1_attn_Wd': _L1_attn_in['Wd'], 'L1_attn_bd': _L1_attn_in['bd'], 'L1_attn_Wsel': _L1_attn_in['Wsel'], 'L1_attn_bsel': _L1_attn_in['bsel'], 'L1_attn_Wso': _L1_attn_in['Wso'], 'L1_attn_bso': _L1_attn_in['bso'], 'L1_attn_Wg': _L1_attn_in['Wg'], 'L1_attn_bg': _L1_attn_in['bg'], 'L1_attn_Wout': _L1_attn_in['Wout'], 'L1_attn_bout': _L1_attn_in['bout'], 'L1_xattn_Wq': _L1_xattn_in['Wq'], 'L1_xattn_bq': _L1_xattn_in['bq'], 'L1_xattn_Wk': _L1_xattn_in['Wk'], 'L1_xattn_bk': _L1_xattn_in['bk'], 'L1_xattn_Wv': _L1_xattn_in['Wv'], 'L1_xattn_bv': _L1_xattn_in['bv'], 'L1_xattn_Wp': _L1_xattn_in['Wp'], 'L1_xattn_bp': _L1_xattn_in['bp'], 'L1_ffn_gate_w': _L1_ffn_in['gate_w'], 'L1_ffn_Wg': _L1_ffn_in['Wg'], 'L1_ffn_Wu': _L1_ffn_in['Wu'], 'L1_ffn_Wd': _L1_ffn_in['Wd'], 'L1_ffn_Sg': _L1_ffn_in['Sg'], 'L1_ffn_Su': _L1_ffn_in['Su'], 'L1_ffn_Sd': _L1_ffn_in['Sd'], 'L2_attn_W_qkv': _L2_attn_in['W_qkv'], 'L2_attn_W_out': _L2_attn_in['W_out'], 'L2_xattn_w_sim': _L2_xattn_in['w_sim'], 'L2_xattn_b_sim': _L2_xattn_in['b_sim'], 'L2_xattn_W_qv': _L2_xattn_in['W_qv'], 'L2_xattn_b_qv': _L2_xattn_in['b_qv'], 'L2_ffn_gamma_x': _L2_ffn_in['gamma_x'], 'L2_ffn_gamma_slot': _L2_ffn_in['gamma_slot'], 'L2_ffn_slot_embeds': _L2_ffn_in['slot_embeds'], 'L2_ffn_w1': _L2_ffn_in['w1'], 'L2_ffn_w2': _L2_ffn_in['w2'], 'L3_attn_Wq': _L3_attn_in['Wq'], 'L3_attn_Wk': _L3_attn_in['Wk'], 'L3_attn_Wv': _L3_attn_in['Wv'], 'L3_attn_Wo': _L3_attn_in['Wo'], 'L3_attn_bo': _L3_attn_in['bo'], 'L3_attn_alpha': _L3_attn_in['alpha'], 'L3_attn_temperature': _L3_attn_in['temperature'], 'L3_attn_gamma': _L3_attn_in['gamma'], 'L3_attn_beta': _L3_attn_in['beta'], 'L3_xattn_Wq': _L3_xattn_in['Wq'], 'L3_xattn_Wk': _L3_xattn_in['Wk'], 'L3_xattn_Wv': _L3_xattn_in['Wv'], 'L3_xattn_bq': _L3_xattn_in['bq'], 'L3_xattn_bk': _L3_xattn_in['bk'], 'L3_xattn_bv': _L3_xattn_in['bv'], 'L3_xattn_Wo': _L3_xattn_in['Wo'], 'L3_xattn_bo': _L3_xattn_in['bo'], 'L3_ffn_wqkv': _L3_ffn_in['wqkv'], 'L3_ffn_q_scale': _L3_ffn_in['q_scale'], 'L3_ffn_k_scale': _L3_ffn_in['k_scale'], 'L3_ffn_wo': _L3_ffn_in['wo'], 'L3_ffn_ln_g': _L3_ffn_in['ln_g'], 'L3_ffn_ln_b': _L3_ffn_in['ln_b'], 'L3_ffn_w1': _L3_ffn_in['w1'], 'L3_ffn_b1': _L3_ffn_in['b1'], 'L3_ffn_w2': _L3_ffn_in['w2'], 'L3_ffn_b2': _L3_ffn_in['b2']}

def reference(x, ctx_1024, mask_1x1xSxS2_ik1, mask_BxSxS2_bk1, L0_attn_wq, L0_attn_wk, L0_attn_wv, L0_attn_wr, L0_attn_wo, L0_xattn_w_q, L0_xattn_w_k, L0_xattn_w_v, L0_xattn_w_o, L0_xattn_b_o, L0_ffn_ln1_g, L0_ffn_ln1_b, L0_ffn_Wqkv, L0_ffn_bqkv, L0_ffn_Wo, L0_ffn_bo, L0_ffn_ln2_g, L0_ffn_ln2_b, L0_ffn_gate_w, L0_ffn_W1, L0_ffn_b1, L0_ffn_W2, L0_ffn_b2, L0_ffn_rW1, L0_ffn_rb1, L0_ffn_rW2, L0_ffn_rb2, L0_ffn_coef_w, L0_ffn_coef_b, L1_attn_ln_g, L1_attn_ln_b, L1_attn_mix_w, L1_attn_mix_b, L1_attn_Wi, L1_attn_bi, L1_attn_Wsin, L1_attn_bsin, L1_attn_Wd, L1_attn_bd, L1_attn_Wsel, L1_attn_bsel, L1_attn_Wso, L1_attn_bso, L1_attn_Wg, L1_attn_bg, L1_attn_Wout, L1_attn_bout, L1_xattn_Wq, L1_xattn_bq, L1_xattn_Wk, L1_xattn_bk, L1_xattn_Wv, L1_xattn_bv, L1_xattn_Wp, L1_xattn_bp, L1_ffn_gate_w, L1_ffn_Wg, L1_ffn_Wu, L1_ffn_Wd, L1_ffn_Sg, L1_ffn_Su, L1_ffn_Sd, L2_attn_W_qkv, L2_attn_W_out, L2_xattn_w_sim, L2_xattn_b_sim, L2_xattn_W_qv, L2_xattn_b_qv, L2_ffn_gamma_x, L2_ffn_gamma_slot, L2_ffn_slot_embeds, L2_ffn_w1, L2_ffn_w2, L3_attn_Wq, L3_attn_Wk, L3_attn_Wv, L3_attn_Wo, L3_attn_bo, L3_attn_alpha, L3_attn_temperature, L3_attn_gamma, L3_attn_beta, L3_xattn_Wq, L3_xattn_Wk, L3_xattn_Wv, L3_xattn_bq, L3_xattn_bk, L3_xattn_bv, L3_xattn_Wo, L3_xattn_bo, L3_ffn_wqkv, L3_ffn_q_scale, L3_ffn_k_scale, L3_ffn_wo, L3_ffn_ln_g, L3_ffn_ln_b, L3_ffn_w1, L3_ffn_b1, L3_ffn_w2, L3_ffn_b2):
    import jax
    import jax.numpy as jnp

    def _L0_attn_ref(x, wq, wk, wv, wr, wo):
        import jax, jax.numpy as jnp
        import numpy as np
        EMBED = 128
        H = 16
        KV = 4
        D = 64
        K_NODES = 4
        TOP_K = 2
        MAXLEN = 1024
        BASE = 10000.0
        SCALE = D ** (-0.5)
        NEG = -1000000000.0

        def _rotate_half(t):
            h = t.shape[-1] // 2
            return jnp.concatenate([-t[..., h:], t[..., :h]], axis=-1)

        def _rope_cache():
            inv_freq = 1.0 / BASE ** (jnp.arange(0, D, 2, dtype=jnp.float32) / D)
            t = jnp.arange(MAXLEN, dtype=jnp.float32)
            freqs = t[:, None] * inv_freq[None, :]
            emb = jnp.concatenate([freqs, freqs], axis=-1)
            return (jnp.cos(emb), jnp.sin(emb))
        B, N, _ = x.shape
        G = H // KV
        q = (x @ wq).reshape(B, N, H, D).transpose(0, 2, 1, 3)
        k = (x @ wk).reshape(B, N, KV, D).transpose(0, 2, 1, 3)
        v = (x @ wv).reshape(B, N, KV, D).transpose(0, 2, 1, 3)
        k = jnp.repeat(k, G, axis=1)
        v = jnp.repeat(v, G, axis=1)
        logits = (x @ wr).reshape(B, N, H, K_NODES).transpose(0, 2, 1, 3)
        tk_vals, tk_idx = jax.lax.top_k(logits, TOP_K)
        tk_w = jax.nn.softmax(tk_vals, axis=-1)
        member = jax.nn.one_hot(tk_idx, K_NODES, dtype=jnp.float32).sum(axis=-2) > 0
        m_i = member.astype(jnp.int32)
        pos = jnp.cumsum(m_i, axis=2) - m_i
        cos_c, sin_c = _rope_cache()
        causal = jnp.tril(jnp.ones((N, N), dtype=bool))
        outs = []
        for n in range(K_NODES):
            p = pos[..., n]
            c = cos_c[p]
            s = sin_c[p]
            qr = q * c + _rotate_half(q) * s
            kr = k * c + _rotate_half(k) * s
            scores = jnp.einsum('bhid,bhjd->bhij', qr, kr) * SCALE
            mk = member[..., n][:, :, None, :]
            scores = jnp.where(causal[None, None] & mk, scores, NEG)
            probs = jax.nn.softmax(scores, axis=-1)
            outs.append(jnp.einsum('bhij,bhjd->bhid', probs, v))
        outs = jnp.stack(outs, axis=3)
        gathered = jnp.take_along_axis(outs, tk_idx[..., None], axis=3)
        y = (tk_w[..., None] * gathered).sum(axis=3)
        y = y.transpose(0, 2, 1, 3).reshape(B, N, H * D)
        return y @ wo

    def _L0_xattn_ref(input_q, input_k, input_v, mask, w_q, w_k, w_v, w_o, b_o):
        import jax, jax.numpy as jnp
        import numpy as np
        D_MODEL = 128
        N_HEAD = 16
        D_K = D_MODEL // N_HEAD
        B, S = (2, 256)
        NEG = -1000000000.0
        b = input_q.shape[0]

        def split_heads(x):
            return x.reshape(b, -1, N_HEAD, D_K).transpose(0, 2, 1, 3)
        q = split_heads(input_q @ w_q)
        k = split_heads(input_k @ w_k)
        v = split_heads(input_v @ w_v)
        scores = jnp.einsum('bhqd,bhkd->bhqk', q, k) / jnp.sqrt(jnp.float32(D_K))
        scores = jnp.where(mask == 0, jnp.float32(NEG), scores)
        attn = jax.nn.softmax(scores, axis=-1)
        per_head = jnp.einsum('bhqk,bhkd->bhqd', attn, v)
        concat = per_head.transpose(0, 2, 1, 3).reshape(b, -1, N_HEAD * D_K)
        return concat @ w_o + b_o

    def _L0_ffn_ref(x, ln1_g, ln1_b, Wqkv, bqkv, Wo, bo, ln2_g, ln2_b, gate_w, W1, b1, W2, b2, rW1, rb1, rW2, rb2, coef_w, coef_b):
        import jax, jax.numpy as jnp
        import numpy as np
        DIM, HEADS, FFN, E = (128, 16, 512, 8)
        B, S = (2, 128)
        EPS = 1e-05

        def _ln(x, g, b):
            mu = jnp.mean(x, axis=-1, keepdims=True)
            var = jnp.mean((x - mu) ** 2, axis=-1, keepdims=True)
            return (x - mu) * jax.lax.rsqrt(var + EPS) * g + b
        b, s, d = x.shape
        h, dh = (HEADS, d // HEADS)
        xn = _ln(x, ln1_g, ln1_b)
        qkv = xn @ Wqkv + bqkv
        q, k, v = jnp.split(qkv, 3, axis=-1)
        q = q.reshape(b, s, h, dh)
        k = k.reshape(b, s, h, dh)
        v = v.reshape(b, s, h, dh)
        scores = jnp.einsum('bqhd,bkhd->bhqk', q, k) / jnp.sqrt(jnp.float32(dh))
        attn = jax.nn.softmax(scores, axis=-1)
        ctx = jnp.einsum('bhqk,bkhd->bqhd', attn, v).reshape(b, s, d)
        x = x + ctx @ Wo + bo
        xn2 = _ln(x, ln2_g, ln2_b)
        xt = xn2.reshape(b * s, d)
        probs = jax.nn.softmax(xt @ gate_w, axis=-1)
        gate_val = jnp.max(probs, axis=-1, keepdims=True)
        expert_idx = jnp.argmax(probs, axis=-1)
        oh = jax.nn.one_hot(expert_idx, E, dtype=xt.dtype)
        xe = jnp.einsum('te,td->etd', oh, xt)
        he = jax.nn.gelu(jnp.einsum('etd,edf->etf', xe, W1) + b1[:, None, :], approximate=False)
        ye = jnp.einsum('etf,efd->etd', he, W2) + b2[:, None, :]
        moe_out = jnp.einsum('te,etd->td', oh, ye) * gate_val
        rm = jax.nn.gelu(xt @ rW1 + rb1, approximate=False) @ rW2 + rb2
        coef = jax.nn.softmax(xt @ coef_w + coef_b, axis=-1)
        ff = moe_out * coef[:, 0:1] + rm * coef[:, 1:2]
        return x + ff.reshape(b, s, d)

    def _L1_attn_ref(x, ln_g, ln_b, mix_w, mix_b, Wi, bi, Wsin, bsin, Wd, bd, Wsel, bsel, Wso, bso, Wg, bg, Wout, bout):
        import jax, jax.numpy as jnp
        import numpy as np
        B, S, DIM, SDIM = (4, 512, 128, 32)
        eps = 1e-05
        mu = jnp.mean(x, axis=-1, keepdims=True)
        var = jnp.mean(jnp.square(x - mu), axis=-1, keepdims=True)
        h = (x - mu) * jax.lax.rsqrt(var + eps) * ln_g + ln_b
        hc = jnp.transpose(h, (0, 2, 1))
        mixed = jax.lax.conv_general_dilated(hc, mix_w, window_strides=(1,), padding=[(1, 1)], dimension_numbers=('NCH', 'OIH', 'NCH'), feature_group_count=hc.shape[1])
        mixed = jnp.transpose(mixed + mix_b[None, :, None], (0, 2, 1))
        u = jnp.tanh(mixed @ Wi + bi)
        x_state = jnp.tanh(mixed @ Wsin + bsin)
        decay = jax.nn.sigmoid(mixed @ Wd + bd)
        select = jax.nn.sigmoid(mixed @ Wsel + bsel)

        def step(state, inp):
            dt, xt = inp
            state = dt * state + (1.0 - dt) * xt
            return (state, state)
        init = jnp.zeros((x.shape[0], x_state.shape[-1]), x.dtype)
        _, states = jax.lax.scan(step, init, (jnp.swapaxes(decay, 0, 1), jnp.swapaxes(x_state, 0, 1)))
        states = jnp.swapaxes(states, 0, 1)
        y = select * states @ Wso + bso
        g = jax.nn.sigmoid(mixed @ Wg + bg)
        out = (g * y + (1.0 - g) * u) @ Wout + bout
        return x + out

    def _L1_xattn_ref(query, key, value, Wq, bq, Wk, bk, Wv, bv, Wp, bp):
        import jax, jax.numpy as jnp
        import numpy as np
        E = 128
        H = 16
        N, S, T = (4, 256, 256)
        n, s, e = query.shape
        t = value.shape[1]
        hd = e // H
        Q = (query @ Wq.T + bq).reshape(n, s, H, hd).transpose(0, 2, 1, 3)
        K = (key @ Wk.T + bk).reshape(n, t, H, hd).transpose(0, 2, 1, 3)
        V = (value @ Wv.T + bv).reshape(n, t, H, hd).transpose(0, 2, 1, 3)
        scale = 1.0 / jnp.sqrt(jnp.asarray(hd, Q.dtype))
        attn = jnp.einsum('nhsd,nhtd->nhst', Q, K) * scale
        A = jax.nn.softmax(attn, axis=-1)
        Y = jnp.einsum('nhst,nhtd->nhsd', A, V)
        Y = Y.transpose(0, 2, 1, 3).reshape(n, s, e)
        return Y @ Wp.T + bp

    def _L1_ffn_ref(hidden_states, gate_w, Wg, Wu, Wd, Sg, Su, Sd):
        import jax, jax.numpy as jnp
        import numpy as np
        E = 16
        F_C = 2.0
        D = 128
        I = 4 * D
        IS = 2 * D
        B, S = (4, 128)
        b, s, d = hidden_states.shape
        T = b * s
        C = int(T * F_C / E)
        flat_x = hidden_states.reshape(T, d)
        logits = flat_x @ gate_w.T
        scores = jax.nn.softmax(logits, axis=-1).T
        topk_weight, topk_idx = jax.lax.top_k(scores, C)
        xg = flat_x[topk_idx]
        g = jnp.einsum('ecd,eid->eci', xg, Wg)
        u = jnp.einsum('ecd,eid->eci', xg, Wu)
        h = jax.nn.gelu(g, approximate=False) * u
        eo = jnp.einsum('eci,edi->ecd', h, Wd)
        eo = eo * topk_weight[..., None]
        flat_out = jnp.zeros_like(flat_x).at[topk_idx.reshape(-1)].add(eo.reshape(-1, d))
        out = flat_out.reshape(b, s, d)
        sg = hidden_states @ Sg.T
        su = hidden_states @ Su.T
        shared = jax.nn.gelu(sg, approximate=False) * su @ Sd.T
        return out + shared

    def _L2_attn_ref(x, W_qkv, W_out):
        import jax, jax.numpy as jnp
        import numpy as np
        B, T, D_MODEL, N_HEADS = (2, 256, 128, 16)
        HS = D_MODEL // N_HEADS
        Bx, Tx, Dm = x.shape
        nH, Hs = (N_HEADS, HS)
        qkv = x @ W_qkv.T
        qkv = qkv.reshape(Bx, Tx, 3 * nH, Hs).transpose(0, 2, 1, 3)
        q, k, v = (qkv[:, :nH], qkv[:, nH:2 * nH], qkv[:, 2 * nH:])
        q = jax.nn.softmax(q, axis=-1) * Hs ** (-0.5)
        k_exp = jnp.exp(k - jnp.max(k, axis=2, keepdims=True))
        k_exp_cumsum = jnp.cumsum(k_exp, axis=2)
        kv_outer = jnp.einsum('bhtc,bhtd->bhtcd', k_exp, v)
        kv_cumsum = jnp.cumsum(kv_outer, axis=2)
        kv = kv_cumsum / (k_exp_cumsum[..., None] + 1e-09)
        xo = jnp.einsum('bhtc,bhtcd->bhtd', q, kv)
        xo = xo.transpose(0, 2, 1, 3).reshape(Bx, Tx, Dm)
        return xo @ W_out.T

    def _L2_xattn_ref(encoder_hc, decoder_hq, w_sim, b_sim, W_qv, b_qv):
        import jax, jax.numpy as jnp
        import numpy as np
        B, L_ENC, L_DEC, D = (16, 64, 128, 128)
        d = encoder_hc.shape[-1]
        w1, w2, w3 = (w_sim[:d], w_sim[d:2 * d], w_sim[2 * d:])
        Sim = (encoder_hc @ w1)[:, :, None] + (decoder_hq @ w2)[:, None, :] + jnp.einsum('bid,bjd->bij', encoder_hc * w3, decoder_hq) + b_sim[0]
        A = jax.nn.softmax(Sim, axis=2)
        hq_hat = jnp.einsum('bij,bjd->bid', A, decoder_hq)
        Batt = jax.nn.softmax(jnp.max(Sim, axis=2), axis=1)
        hc_bar = jnp.einsum('bi,bid->bd', Batt, encoder_hc)[:, None, :]
        hc_hat = jnp.broadcast_to(hc_bar, encoder_hc.shape)
        feats = jnp.concatenate([encoder_hc, hq_hat, encoder_hc * hq_hat, encoder_hc * hc_hat], axis=-1)
        hcq = feats @ W_qv + b_qv
        return hcq

    def _L2_ffn_ref(x, gamma_x, gamma_slot, slot_embeds, w1, w2):
        import jax, jax.numpy as jnp
        import numpy as np
        EPS = 1e-12

        def rms_norm(t, gamma):
            n = jnp.maximum(jnp.linalg.norm(t, axis=-1, keepdims=True), EPS)
            scale = jnp.sqrt(jnp.asarray(t.shape[-1], t.dtype))
            return t / n * scale * gamma
        b, s, d = x.shape
        e, t, _ = slot_embeds.shape
        xn = rms_norm(x, gamma_x)
        se = rms_norm(slot_embeds, gamma_slot)
        logits = jnp.einsum('bsd,etd->bset', xn, se)
        dispatch = jax.nn.softmax(logits, axis=1)
        slots = jnp.einsum('bsd,bset->betd', xn, dispatch)
        h = jax.nn.gelu(slots @ w1, approximate=False)
        processed = h @ w2
        combine = jax.nn.softmax(logits.reshape(b, s, e * t), axis=-1)
        out = jnp.einsum('bnd,bsn->bsd', processed.reshape(b, e * t, d), combine)
        return out

    def _L3_attn_ref(x, Wq, Wk, Wv, Wo, bo, alpha, temperature, gamma, beta):
        import jax, jax.numpy as jnp
        import numpy as np
        NUM_HEADS = 16
        LN_EPS = 1e-05

        def _layernorm(x, gamma, beta):
            mu = jnp.mean(x, axis=-1, keepdims=True)
            var = jnp.var(x, axis=-1, keepdims=True)
            return (x - mu) * jax.lax.rsqrt(var + LN_EPS) * gamma + beta
        B, N, D = x.shape
        H = NUM_HEADS
        hd = D // H
        residual = x
        q = (x @ Wq.T).reshape(B, N, H, hd).transpose(0, 2, 1, 3)
        k = (x @ Wk.T).reshape(B, N, H, hd).transpose(0, 2, 1, 3)
        v = (x @ Wv.T).reshape(B, N, H, hd).transpose(0, 2, 1, 3)
        kk = jnp.einsum('bhnd,bhne->bhde', k, k)
        kk = kk + alpha[0] * jnp.eye(hd, dtype=x.dtype)
        kk_inv = jnp.linalg.inv(kk)
        ktv = jnp.einsum('bhnd,bhne->bhde', k, v)
        attn_map = kk_inv @ ktv
        attn_map = jax.nn.softmax(attn_map / temperature, axis=-2)
        out = q @ attn_map
        out = out.transpose(0, 2, 1, 3).reshape(B, N, D)
        out = out @ Wo.T + bo
        return _layernorm(out + residual, gamma, beta)

    def _L3_xattn_ref(query, key, value, mask, Wq, Wk, Wv, bq, bk, bv, Wo, bo):
        import jax, jax.numpy as jnp
        import numpy as np
        NEG = -1000000000.0
        q = jnp.einsum('nkm,hmd->nhkd', query, Wq) + bq[None, :, None, :]
        k = jnp.einsum('nkm,hmd->nhkd', key, Wk) + bk[None, :, None, :]
        v = jnp.einsum('nkm,hmd->nhkd', value, Wv) + bv[None, :, None, :]
        D = q.shape[-1]
        scores = jnp.einsum('nhkd,nhjd->nhkj', q, k) / jnp.sqrt(jnp.float32(D))
        scores = jnp.where(mask[:, None, :, :], NEG, scores)
        attn = jax.nn.softmax(scores, axis=-1)
        y = jnp.einsum('nhkj,nhjd->nhkd', attn, v)
        N, H, K, _ = y.shape
        concat = jnp.transpose(y, (0, 2, 1, 3)).reshape(N, K, H * D)
        return concat @ Wo + bo

    def _L3_ffn_ref(x, wqkv, q_scale, k_scale, wo, ln_g, ln_b, w1, b1, w2, b2):
        import jax, jax.numpy as jnp
        import numpy as np
        DIM = 128
        DEPTH = 2
        HEADS = 8
        DIM_HEAD = 64
        WINDOW = 64
        INNER = HEADS * DIM_HEAD
        HID = int(DIM * 4 * 2 / 3)
        B, N = (2, 1024)
        QK_SCALE = 8.0

        def shift_token(t):
            t1, t2 = jnp.split(t, 2, axis=-1)
            t2 = jnp.pad(t2, ((0, 0), (1, 0), (0, 0)))[:, :-1]
            return jnp.concatenate([t1, t2], axis=-1)

        def l2norm(t):
            return t / jnp.clip(jnp.linalg.norm(t, axis=-1, keepdims=True), 1e-12)

        def rotate_half(x):
            x1, x2 = jnp.split(x, 2, axis=-1)
            return jnp.concatenate([-x2, x1], axis=-1)

        def rotary_xpos(q, k):
            n = q.shape[-2]
            half_idx = jnp.arange(0, DIM_HEAD, 2, dtype=jnp.float32)
            inv_freq = 1.0 / 10000.0 ** (half_idx / DIM_HEAD)
            t = jnp.arange(n, dtype=jnp.float32)
            freqs = t[:, None] * inv_freq[None, :]
            freqs = jnp.concatenate([freqs, freqs], axis=-1)
            base = (half_idx + 0.4 * DIM_HEAD) / (1.4 * DIM_HEAD)
            power = (t - n // 2) / float(WINDOW // 2)
            scale = base[None, :] ** power[:, None]
            scale = jnp.concatenate([scale, scale], axis=-1)
            cos, sin = (jnp.cos(freqs), jnp.sin(freqs))
            q = q * cos * scale + rotate_half(q) * sin * scale
            k = k * cos / scale + rotate_half(k) * sin / scale
            return (q, k)

        def local_attention(q, k, v):
            b, h, n, d = q.shape
            w = n // WINDOW
            bq = q.reshape(b, h, w, WINDOW, d) * QK_SCALE
            bk = k.reshape(b, h, w, WINDOW, d)
            bv = v.reshape(b, h, w, WINDOW, d)

            def look_around(t):
                p = jnp.pad(t, ((0, 0), (0, 0), (1, 0), (0, 0), (0, 0)))
                return jnp.concatenate([p[:, :, :w], p[:, :, 1:]], axis=3)
            bk, bv = (look_around(bk), look_around(bv))
            bt = jnp.arange(n).reshape(w, WINDOW)
            btp = jnp.pad(bt, ((1, 0), (0, 0)), constant_values=-1)
            btk = jnp.concatenate([btp[:w], btp[1:]], axis=1)
            sim = jnp.einsum('bhwid,bhwjd->bhwij', bq, bk)
            i = bt[:, :, None]
            j = btk[:, None, :]
            mask = (i < j) | (i > j + WINDOW) | (j == -1)
            sim = jnp.where(mask, -jnp.finfo(sim.dtype).max, sim)
            attn = jax.nn.softmax(sim, axis=-1)
            out = jnp.einsum('bhwij,bhwjd->bhwid', attn, bv)
            return out.reshape(b, h, n, d)

        def _layer(x, wqkv, qs, ksc, wo, lg, lb, w1, b1, w2, b2):
            b, n, _ = x.shape
            h = shift_token(x)
            qkv = h @ wqkv
            q, k, v = jnp.split(qkv, 3, axis=-1)
            to_heads = lambda t: t.reshape(b, n, HEADS, DIM_HEAD).transpose(0, 2, 1, 3)
            q, k, v = (to_heads(q), to_heads(k), to_heads(v))
            q = l2norm(q) * qs
            k = l2norm(k) * ksc
            q, k = rotary_xpos(q, k)
            o = local_attention(q, k, v)
            o = o.transpose(0, 2, 1, 3).reshape(b, n, INNER)
            x = x + o @ wo
            h = shift_token(x)
            mu = h.mean(-1, keepdims=True)
            var = h.var(-1, keepdims=True)
            h = (h - mu) / jnp.sqrt(var + 1e-05) * lg + lb
            h = h @ w1 + b1
            a, g = jnp.split(h, 2, axis=-1)
            h = a * jax.nn.gelu(g, approximate=False)
            x = x + h @ w2 + b2
            return x
        for l in range(DEPTH):
            x = _layer(x, wqkv[l], q_scale[l], k_scale[l], wo[l], ln_g[l], ln_b[l], w1[l], b1[l], w2[l], b2[l])
        return x
    x = _layernorm(x + _L0_attn_ref(x, L0_attn_wq, L0_attn_wk, L0_attn_wv, L0_attn_wr, L0_attn_wo), axis=-1)
    x = _layernorm(x + _L0_xattn_ref(x, ctx_1024, ctx_1024, mask_1x1xSxS2_ik1, L0_xattn_w_q, L0_xattn_w_k, L0_xattn_w_v, L0_xattn_w_o, L0_xattn_b_o), axis=-1)
    x = _layernorm(x + _L0_ffn_ref(x, L0_ffn_ln1_g, L0_ffn_ln1_b, L0_ffn_Wqkv, L0_ffn_bqkv, L0_ffn_Wo, L0_ffn_bo, L0_ffn_ln2_g, L0_ffn_ln2_b, L0_ffn_gate_w, L0_ffn_W1, L0_ffn_b1, L0_ffn_W2, L0_ffn_b2, L0_ffn_rW1, L0_ffn_rb1, L0_ffn_rW2, L0_ffn_rb2, L0_ffn_coef_w, L0_ffn_coef_b), axis=-1)
    x = _layernorm(x + _L1_attn_ref(x, L1_attn_ln_g, L1_attn_ln_b, L1_attn_mix_w, L1_attn_mix_b, L1_attn_Wi, L1_attn_bi, L1_attn_Wsin, L1_attn_bsin, L1_attn_Wd, L1_attn_bd, L1_attn_Wsel, L1_attn_bsel, L1_attn_Wso, L1_attn_bso, L1_attn_Wg, L1_attn_bg, L1_attn_Wout, L1_attn_bout), axis=-1)
    x = _layernorm(x + _L1_xattn_ref(x, ctx_1024, ctx_1024, L1_xattn_Wq, L1_xattn_bq, L1_xattn_Wk, L1_xattn_bk, L1_xattn_Wv, L1_xattn_bv, L1_xattn_Wp, L1_xattn_bp), axis=-1)
    x = _layernorm(x + _L1_ffn_ref(x, L1_ffn_gate_w, L1_ffn_Wg, L1_ffn_Wu, L1_ffn_Wd, L1_ffn_Sg, L1_ffn_Su, L1_ffn_Sd), axis=-1)
    x = _layernorm(x + _L2_attn_ref(x, L2_attn_W_qkv, L2_attn_W_out), axis=-1)
    x = _layernorm(x + _L2_xattn_ref(x, ctx_1024, L2_xattn_w_sim, L2_xattn_b_sim, L2_xattn_W_qv, L2_xattn_b_qv), axis=-1)
    x = _layernorm(x + _L2_ffn_ref(x, L2_ffn_gamma_x, L2_ffn_gamma_slot, L2_ffn_slot_embeds, L2_ffn_w1, L2_ffn_w2), axis=-1)
    x = _layernorm(x + _L3_attn_ref(x, L3_attn_Wq, L3_attn_Wk, L3_attn_Wv, L3_attn_Wo, L3_attn_bo, L3_attn_alpha, L3_attn_temperature, L3_attn_gamma, L3_attn_beta), axis=-1)
    x = _layernorm(x + _L3_xattn_ref(x, ctx_1024, ctx_1024, mask_BxSxS2_bk1, L3_xattn_Wq, L3_xattn_Wk, L3_xattn_Wv, L3_xattn_bq, L3_xattn_bk, L3_xattn_bv, L3_xattn_Wo, L3_xattn_bo), axis=-1)
    x = _layernorm(x + _L3_ffn_ref(x, L3_ffn_wqkv, L3_ffn_q_scale, L3_ffn_k_scale, L3_ffn_wo, L3_ffn_ln_g, L3_ffn_ln_b, L3_ffn_w1, L3_ffn_b1, L3_ffn_w2, L3_ffn_b2), axis=-1)
    return x

_drawn_inputs = setup_inputs


def setup_inputs(seed=0):
    import zlib

    import numpy as np

    out = dict(_drawn_inputs(seed))
    spreads = {'L0_ffn_ln1_g': (1.0, 0.6),
     'L0_ffn_ln1_b': (0.0, 0.8),
     'L0_ffn_bqkv': (0.0, 0.747),
     'L0_ffn_bo': (0.0, 0.1),
     'L0_ffn_ln2_g': (1.0, 0.6),
     'L0_ffn_ln2_b': (0.0, 0.8),
     'L0_ffn_b1': (0.0, 0.8),
     'L0_ffn_b2': (0.0, 0.8),
     'L0_ffn_rb1': (0.0, 0.8),
     'L0_ffn_rb2': (0.0, 0.309),
     'L0_ffn_coef_b': (0.0, 0.8),
     'L1_attn_ln_g': (1.0, 0.6),
     'L1_attn_ln_b': (0.0, 0.765),
     'L1_attn_mix_b': (0.0, 0.37),
     'L1_attn_bi': (0.0, 0.432),
     'L1_attn_bsin': (0.0, 0.745),
     'L1_attn_bd': (0.0, 0.8),
     'L1_attn_bsel': (0.0, 0.8),
     'L1_attn_bso': (0.0, 0.371),
     'L1_attn_bg': (0.0, 0.8),
     'L1_attn_bout': (0.0, 0.1),
     'L2_ffn_gamma_x': (1.0, 0.2),
     'L2_ffn_gamma_slot': (1.0, 0.2),
     'L3_attn_bo': (0.0, 0.1),
     'L3_attn_gamma': (1.0, 0.2),
     'L3_attn_beta': (0.0, 0.1),
     'L3_ffn_q_scale': (1.0, 0.6),
     'L3_ffn_k_scale': (1.0, 0.6),
     'L3_ffn_ln_g': (1.0, 0.6),
     'L3_ffn_ln_b': (0.0, 0.8),
     'L3_ffn_b1': (0.0, 0.8),
     'L3_ffn_b2': (0.0, 0.585)}
    factors = {'L0_attn_wq': 8.0,
     'L0_attn_wk': 8.0,
     'L0_attn_wr': 3.858,
     'L0_xattn_b_o': 5.901,
     'L0_ffn_Wqkv': 4.954,
     'L0_ffn_Wo': 3.379,
     'L0_ffn_gate_w': 8.0,
     'L0_ffn_W1': 8.0,
     'L0_ffn_W2': 8.0,
     'L0_ffn_rW1': 4.085,
     'L0_ffn_rW2': 3.636,
     'L0_ffn_coef_w': 8.0,
     'L1_attn_Wd': 6.481,
     'L1_attn_Wsel': 5.112,
     'L1_xattn_bq': 8.0,
     'L1_xattn_bk': 64.0,
     'L1_xattn_bv': 5.906,
     'L1_xattn_bp': 5.442,
     'L1_ffn_gate_w': 8.0,
     'L1_ffn_Wg': 8.0,
     'L1_ffn_Wu': 8.0,
     'L1_ffn_Wd': 8.0,
     'L1_ffn_Sg': 6.123,
     'L1_ffn_Su': 5.957,
     'L1_ffn_Sd': 5.998,
     'L3_xattn_bq': 8.0,
     'L3_xattn_bk': 64.0,
     'L3_xattn_bv': 8.0,
     'L3_xattn_bo': 8.0,
     'L3_ffn_w1': 6.463,
     'L3_ffn_w2': 6.446}
    for name, (base, spread) in spreads.items():
        noise = np.random.default_rng([zlib.crc32(name.encode()), seed]).standard_normal(out[name].shape)
        drawn = base * np.exp(spread * noise) if base else spread * noise
        out[name] = jnp.asarray(drawn.astype(out[name].dtype))
    for name, factor in factors.items():
        out[name] = (out[name] * factor).astype(out[name].dtype)
    return out
```

```python
from contextlib import ExitStack

import numpy as np

import concourse.bass as bass
from concourse import mybir
from concourse.alu_op_type import AluOpType as ALU

ACT = mybir.ActivationFunctionType
F32 = mybir.dt.float32
BF16 = mybir.dt.bfloat16
I32 = mybir.dt.int32
AX = mybir.AxisListType

P = 128
B = 4
S = 256
SC = 64
T = B * S // P
TB = S // P
N = B * S
BANK = 512
MASKED = -2.0 ** 30
EPS = 1e-5


class Chain:

    def __init__(self, sem):
        self.sem, self.base, self.n = sem, 0, 0

    def __call__(self, eng, ins):
        self.n += 1
        ins.then_inc(self.sem, 1)
        eng.wait_ge(self.sem, self.base + self.n)

    def enter(self, turn, per_turn):
        self.kept, self.per_turn = self.n, per_turn
        self.base, self.n = self.n + turn * per_turn, 0

    def leave(self, turns):
        assert self.n == self.per_turn, (self.n, self.per_turn)
        self.base, self.n = 0, self.kept + turns * self.per_turn


class Counted:

    def __init__(self, sem):
        self.sem, self.base = sem, 0


class Core:

    def __init__(self, nc, ctx, dram):
        self.nc, self.ctx, self.dram, self.shared = nc, ctx, dram, {}
        self.X = self.sb("X", [P, T, P])
        self.XT = self.sb("XT", [P, N])
        self.centred = self.sb("centred", [P, T, P])
        self.squared = self.sb("squared", [P, T, P])
        self.stat = self.sb("stat", [P, 4, T])
        self.vchain = Chain(self.sem("vector_chain"))
        self.achain = Chain(self.sem("scalar_chain"))
        self.gchain = Chain(self.sem("gpsimd_chain"))

    def sb(self, name, shape, dt=F32, ctx=None):
        return (ctx or self.ctx).enter_context(self.nc.sbuf_tensor(name, shape, dt))

    def ps(self, name, shape, ctx, dt=F32):
        return ctx.enter_context(self.nc.psum_tensor(name, shape, dt))

    def sem(self, name):
        return self.ctx.enter_context(self.nc.semaphore(name))

    def counted(self, tag, names):
        for n in names.split():
            if (tag, n) not in self.shared:
                self.shared[tag, n] = Counted(self.sem(f"{tag}_{n}"))
        return [self.shared[tag, n] for n in names.split()]

    def sems(self, tag, names):
        return [self.sem(f"{tag}_{n}") for n in names.split()]


def bc(ap, shape):
    return ap.broadcast_to(shape)



class Pack:

    def __init__(self, name):
        self.name, self.at, self.width = name, {}, 0

    def put(self, key, width):
        self.at[key] = (self.width, width)
        self.width += width

    def build(self, parts):
        out = np.zeros((P, self.width), np.float32)
        for key, a in parts.items():
            start, width = self.at[key]
            a = np.asarray(a)
            assert a.ndim == 2 and a.shape[1] == width and a.shape[0] <= P, (key, a.shape, width)
            out[:a.shape[0], start:start + width] = a
        return out

    def view(self, tile, key):
        start, width = self.at[key]
        return tile[:, start:start + width]


def tile_rows(a, rows=P):
    n = a.shape[0] // rows
    return a.reshape(n, rows, a.shape[1]).transpose(1, 0, 2).reshape(rows, -1)


def on_all(v):
    return np.broadcast_to(np.asarray(v).reshape(1, -1), (P, np.asarray(v).size))


def column(v):
    return np.asarray(v).reshape(-1, 1)



def norm_vector(k, v, src, dst, var_ready, rstd_ready, n, gain=None, shift=None, copy_to=None):
    link, full = k.vchain, [P, T, P]
    mean, var = k.stat[:, 0, :], k.stat[:, 2, :]
    link(v, k.nc.vector.tensor_reduce(mean, src, AX.X, ALU.add))
    link(v, k.nc.vector.tensor_scalar(k.stat[:, 1, :], mean, 1.0 / P, None, ALU.mult))
    link(v, k.nc.vector.tensor_tensor(k.centred[:], src, bc(k.stat[:, 1, :].unsqueeze(2), full), ALU.subtract))
    link(v, k.nc.vector.tensor_tensor(k.squared[:], k.centred[:], k.centred[:], ALU.mult))
    link(v, k.nc.vector.tensor_reduce(var, k.squared[:], AX.X, ALU.add))
    k.nc.vector.tensor_scalar(k.stat[:, 3, :], var, 1.0 / P, EPS, ALU.mult, ALU.add).then_inc(var_ready.sem, 1)
    v.wait_ge(rstd_ready.sem, rstd_ready.base + n)
    link(v, k.nc.vector.tensor_tensor(dst, k.centred[:], bc(k.rstd[:].unsqueeze(2), full), ALU.mult))
    if gain is not None:
        link(v, k.nc.vector.tensor_tensor(dst, dst, bc(gain.unsqueeze(1), full), ALU.mult))
        link(v, k.nc.vector.tensor_tensor(dst, dst, bc(shift.unsqueeze(1), full), ALU.add))


def norm_gpsimd(k, g, var_ready, rstd_ready, n):
    g.wait_ge(var_ready.sem, var_ready.base + n)
    k.nc.gpsimd.tensor_tensor(k.rstd[:], k.stat[:, 3, :], k.minus_half[:], ALU.pow).then_inc(rstd_ready.sem, 1)


def constants(k):
    k.ident = k.sb("ident", [P, P])
    k.identb = k.sb("identb", [P, P], BF16)
    k.masker = k.sb("masker", [P, P], BF16)
    k.above = k.sb("above", [P, P], BF16)
    k.ones = k.sb("ones", [P, P])
    k.rstd = k.sb("rstd", [P, T])
    k.minus_half = k.sb("minus_half", [P, T])
    filled, = k.sems("const", "filled")
    with k.nc.Block() as block:

        @block.gpsimd
        def _(g):
            nc = k.nc
            nc.gpsimd.memset(k.ident[:], 0.0).then_inc(filled, 1)
            nc.gpsimd.memset(k.masker[:], 0.0).then_inc(filled, 1)
            nc.gpsimd.memset(k.above[:], 0.0).then_inc(filled, 1)
            nc.gpsimd.memset(k.ones[:], 1.0)
            nc.gpsimd.memset(k.quarter[:], 0.25)
            nc.gpsimd.memset(k.identb[:], 0.0).then_inc(filled, 1)
            nc.gpsimd.memset(k.minus_half[:], -0.5)
            g.wait_ge(filled, 4)
            for m, value in ((k.ident, 1.0), (k.identb, 1.0), (k.masker, MASKED)):
                nc.gpsimd.affine_select(out=m[:], in_=m[:], compare_op=ALU.not_equal, fill=value, base=0,
                                        pattern=[[-1, P]], channel_multiplier=1)
            nc.gpsimd.affine_select(out=k.above[:], in_=k.above[:], compare_op=ALU.is_ge, fill=1.0, base=0,
                                    pattern=[[1, P]], channel_multiplier=-1)


SCALAR, VECTOR = "scalar", "vector"


def products(k, tag, table):
    nc = k.nc
    ring = 4
    with ExitStack() as ctx:
        areas = k.ps(f"{tag}_areas", [P, ring, 2 * BANK], ctx)
        ready, by_scalar, by_vector = k.counted("products", "ready taken_by_scalar taken_by_vector")
        taken = {SCALAR: by_scalar, VECTOR: by_vector}
        upto = lambda n: sum(1 for who, _, _ in table[:n] if who == table[n - 1][0])
        with nc.Block() as block:

            @block.tensor
            def _(pe):
                for n, (who, issue, _) in enumerate(table):
                    if n >= ring:
                        last = taken[table[n - ring][0]]
                        pe.wait_ge(last.sem, last.base + upto(n - ring + 1))
                    issue(pe, areas[:, n % ring, :]).then_inc(ready.sem, 1)

            def take_out(eng, me):
                for n, (who, _, take) in enumerate(table):
                    if who == me:
                        eng.wait_ge(ready.sem, ready.base + n + 1)
                        take(eng, areas[:, n % ring, :]).then_inc(taken[me].sem, 1)
                        eng.wait_ge(taken[me].sem, taken[me].base + upto(n + 1))

            @block.scalar
            def _(act):
                take_out(act, SCALAR)

            @block.vector
            def _(v):
                take_out(v, VECTOR)
        ready.base += len(table)
        for who in taken:
            taken[who].base += sum(1 for entry in table if entry[0] == who)


def wide(k, lhsT, rhs, rows=P):
    def issue(pe, out):
        for c in range(2):
            mm = k.nc.tensor.matmul(out[0:rows, c * BANK:(c + 1) * BANK], lhsT, rhs[:, c * BANK:(c + 1) * BANK],
                                    start=True, stop=True)
        return mm
    return issue


def narrow(k, lhsT, rhs, cols, rows=P):
    return lambda pe, out: k.nc.tensor.matmul(out[0:rows, 0:cols], lhsT, rhs, start=True, stop=True)


def by_tile(k, source_t, rhs, width):
    def issue(pe, out):
        for t in range(T):
            mm = k.nc.tensor.matmul(out[:, t * width:(t + 1) * width], source_t[:, t * P:(t + 1) * P], rhs,
                                    start=True, stop=True)
        return mm
    return issue


def activated(k, dst, func=ACT.Identity, bias=0.0, rows=P, cols=N, scale=1.0):
    return lambda act, out: k.nc.scalar.activation(dst, out[0:rows, 0:cols], func, bias=bias, scale=scale)


def attention(k, tag, units, scale, wide_out=False):
    nc = k.nc
    with ExitStack() as ctx:
        scores = k.ps(f"{tag}_scores", [P, 2, 2, BANK], ctx)
        turned = k.ps(f"{tag}_turned", [P, 2 * BANK], ctx)
        outs = k.ps(f"{tag}_outs", [P, 2, BANK], ctx)
        probs = k.sb(f"{tag}_probs", [P, 2, 2 * BANK], ctx=ctx)
        probs_t = k.sb(f"{tag}_probs_t", [P, 2 * BANK], ctx=ctx)
        top = k.sb(f"{tag}_top", [P, 2, 16], ctx=ctx)
        total = k.sb(f"{tag}_total", [P, 2, 16], ctx=ctx)
        (scores_ready, shifted, exp_ready, turned_ready, turned_copied, out_ready, out_used) = k.counted(
            "attention", "scores_ready shifted exp_ready turned_ready turned_copied out_ready out_used")
        area = lambda u: outs[:].rearrange("p a b -> p (a b)") if wide_out else outs[:, u % 2]
        outs_in_turn = 1 if wide_out else 2
        with nc.Block() as block:

            @block.tensor
            def _(pe):
                def score(u):
                    if u >= 2:
                        pe.wait_ge(shifted.sem, shifted.base + u - 1)
                    units[u][2](scores[:, u % 2]).then_inc(scores_ready.sem, 1)

                def weigh(u):
                    pe.wait_ge(turned_copied.sem, turned_copied.base + u + 1)
                    if u >= outs_in_turn:
                        pe.wait_ge(out_used.sem, out_used.base + u + 1 - outs_in_turn)
                    units[u][3](area(u), probs_t).then_inc(out_ready.sem, 1)

                score(0)
                for u, (columns, *_) in enumerate(units):
                    if u + 1 < len(units):
                        score(u + 1)
                    if u >= 1:
                        weigh(u - 1)
                    pe.wait_ge(exp_ready.sem, exp_ready.base + u + 1)
                    for x in range(columns // P):
                        mm = nc.tensor.transpose(turned[:, x * P:(x + 1) * P], probs[:, u % 2, x * P:(x + 1) * P],
                                                 k.ident[:])
                    mm.then_inc(turned_ready.sem, 1)
                weigh(len(units) - 1)

            @block.scalar
            def _(act):
                for u, (columns, *_) in enumerate(units):
                    act.wait_ge(shifted.sem, shifted.base + u + 1)
                    nc.scalar.activation(probs[:, u % 2, 0:columns], probs[:, u % 2, 0:columns], ACT.Exp,
                                         scale=scale).then_inc(exp_ready.sem, 1)
                    act.wait_ge(turned_ready.sem, turned_ready.base + u + 1)
                    nc.scalar.copy(probs_t[:, 0:columns], turned[:, 0:columns]).then_inc(turned_copied.sem, 1)

            @block.vector
            def _(v):
                link = k.vchain
                lag = 1 if wide_out else min(2, len(units))

                def finish(u):
                    columns, groups, _, _, dest, _ = units[u]
                    sums = total[:, u % 2, 0:groups]
                    if wide_out:
                        out = area(u)[:, 0:columns].rearrange("p (g d) -> p g d", g=groups)
                        v.wait_ge(exp_ready.sem, exp_ready.base + u + 1)
                        link(v, nc.vector.tensor_reduce(sums, probs[:, u % 2, 0:columns].rearrange(
                            "p (g w) -> p g w", g=groups), AX.X, ALU.add))
                        v.wait_ge(out_ready.sem, out_ready.base + u + 1)
                        link(v, nc.vector.reciprocal(sums, sums))
                    else:
                        width = dest.shape[-1]
                        out = area(u)[:, 0:groups * (width + 1)].rearrange("p (g d) -> p g d", g=groups)
                        v.wait_ge(out_ready.sem, out_ready.base + u + 1)
                        link(v, nc.vector.reciprocal(sums, out[:, :, width]))
                        out = out[:, :, 0:width]
                    sums = sums.unsqueeze(2)
                    if len(dest.shape) == 4:
                        out, sums = (x.rearrange("p (o g) d -> p o g d", o=2) for x in (out, sums))
                    nc.vector.tensor_tensor(dest, out, bc(sums, list(dest.shape)), ALU.mult)\
                        .then_inc(out_used.sem, 1)

                for u, (columns, groups, _, _, dest, mask) in enumerate(units):
                    split = lambda x: x.rearrange("p o (g w) -> p o g w", g=groups // 2)
                    banks = split(scores[:, u % 2, :, 0:columns // 2])
                    packed = split(probs[:, u % 2, 0:columns].rearrange("p (o c) -> p o c", o=2))
                    tops = top[:, u % 2, 0:groups].rearrange("p (o g) -> p o g", o=2)
                    full = [P, 2, groups // 2, columns // groups]
                    v.wait_ge(scores_ready.sem, scores_ready.base + u + 1)
                    if u >= 2:
                        v.wait_ge(turned_ready.sem, turned_ready.base + u - 1)
                    if mask:
                        packed_groups = probs[:, u % 2, 0:columns].rearrange("p (g w) -> p g w", g=groups)
                        flat = [P, groups, columns // groups]
                        for o in range(2):
                            link(v, nc.vector.tensor_tensor(packed[:, o], banks[:, o],
                                                            bc(mask[0].unsqueeze(1), full[:1] + full[2:]), ALU.mult))
                        link(v, nc.vector.tensor_tensor(packed_groups, packed_groups, bc(mask[1].unsqueeze(1), flat),
                                                        ALU.add))
                        source = packed
                    else:
                        source = banks
                    link(v, nc.vector.tensor_reduce(tops, source, AX.X, ALU.max))
                    nc.vector.tensor_tensor(packed, source, bc(tops.unsqueeze(3), full), ALU.subtract)\
                        .then_inc(shifted.sem, 1)
                    v.wait_ge(shifted.sem, shifted.base + u + 1)
                    if u >= lag:
                        finish(u - lag)
                for u in range(len(units) - lag, len(units)):
                    finish(u)
        for counted in (scores_ready, shifted, exp_ready, turned_ready, turned_copied, out_ready, out_used):
            counted.base += len(units)


def close_sublayer(k, tag, features, weights, chunks, bias=None, doubled=False, extra_norm=None,
                   features_t=None, addend=None, to=None, gain=None, shift=None, norm=True):
    normed_to, turned_to = to or (k.X[:], k.XT[:])
    nc = k.nc
    with ExitStack() as ctx:
        width = chunks * P
        turned = k.ps(f"{tag}_turned", [P, 2, 2, BANK], ctx)
        product = k.ps(f"{tag}_product", [P, T, P], ctx)
        xt = k.ps(f"{tag}_xt", [P, 2, BANK], ctx)
        turned_sb = k.sb(f"{tag}_turned_sb", [P, 2, width], ctx=ctx)
        (turned_ready, turned_copied, product_ready, var_ready, rstd_ready, normed, xt_ready) = k.counted(
            "close", "turned_ready turned_copied product_ready var_ready rstd_ready normed xt_ready")
        flat = lambda t: turned[:, t % 2].rearrange("p a b -> p (a b)")[:, 0:width]
        with nc.Block() as block:

            @block.tensor
            def _(pe):
                def turn(t):
                    if t >= 2:
                        pe.wait_ge(turned_copied.sem, turned_copied.base + t - 1)
                    for c in range(chunks):
                        last_one = nc.tensor.transpose(flat(t)[:, c * P:(c + 1) * P],
                                                       features[:, t, c * P:(c + 1) * P], k.ident[:])
                    last_one.then_inc(turned_ready.sem, 1)

                if not features_t:
                    turn(0)
                for t in range(T):
                    if not features_t:
                        if t + 1 < T:
                            turn(t + 1)
                        pe.wait_ge(turned_copied.sem, turned_copied.base + t + 1)
                    for c in range(chunks):
                        rows = features_t[c][:, t * P:(t + 1) * P] if features_t else \
                            turned_sb[:, t % 2, c * P:(c + 1) * P]
                        last_one = nc.tensor.matmul(product[:, t, :], rows, weights[c], start=(c == 0),
                                                    stop=(c == chunks - 1))
                    last_one.then_inc(product_ready.sem, 1)
                pe.wait_ge(normed.sem, normed.base + 1)
                for t in range(T):
                    last_one = nc.tensor.transpose(xt[:, t // 4, (t % 4) * P:(t % 4 + 1) * P], normed_to[:, t, :],
                                                   k.ident[:])
                last_one.then_inc(xt_ready.sem, 1)

            @block.scalar
            def _(act):
                for t in range(0 if features_t else T):
                    act.wait_ge(turned_ready.sem, turned_ready.base + t + 1)
                    if t >= 2:
                        act.wait_ge(product_ready.sem, product_ready.base + t - 1)
                    nc.scalar.copy(turned_sb[:, t % 2, :], flat(t)).then_inc(turned_copied.sem, 1)
                act.wait_ge(xt_ready.sem, xt_ready.base + 1)
                nc.scalar.copy(turned_to, xt[:].rearrange("p a b -> p (a b)"))

            @block.vector
            def _(v):
                link = k.vchain
                if doubled:
                    link(v, nc.vector.tensor_scalar(k.X[:], k.X[:], 2.0, None, ALU.mult))
                if bias is not None:
                    link(v, nc.vector.tensor_tensor(k.X[:], k.X[:], bc(bias.unsqueeze(1), [P, T, P]), ALU.add))
                if addend is not None:
                    link(v, nc.vector.tensor_tensor(k.X[:], k.X[:], addend, ALU.add))
                v.wait_ge(product_ready.sem, product_ready.base + T)
                link(v, nc.vector.tensor_tensor(k.X[:], k.X[:], product[:], ALU.add))
                n = 1
                if extra_norm:
                    norm_vector(k, v, k.X[:], k.X[:], var_ready, rstd_ready, n, *extra_norm)
                    n += 1
                if norm:
                    norm_vector(k, v, k.X[:], normed_to, var_ready, rstd_ready, n, gain, shift)
                nc.vector.engine_nop().then_inc(normed.sem, 1)

            @block.gpsimd
            def _(g):
                for n in range(2 if extra_norm else 1 if norm else 0):
                    norm_gpsimd(k, g, var_ready, rstd_ready, n + 1)
        norms = 2 if extra_norm else 1 if norm else 0
        for counted, signals in ((turned_ready, 0 if features_t else T), (turned_copied, 0 if features_t else T),
                                 (product_ready, T), (var_ready, norms), (rstd_ready, norms), (normed, 1),
                                 (xt_ready, 1)):
            counted.base += signals


def norm_and_turn(k, tag, src, dst, dst_t, gain=None, shift=None, addends=(), copy_to=None, on_turned=None):
    nc = k.nc
    with ExitStack() as ctx:
        xt = k.ps(f"{tag}_xt", [P, 2 * BANK], ctx)
        var_ready, rstd_ready, normed, xt_ready = k.counted("norm", "var_ready rstd_ready normed xt_ready")
        with nc.Block() as block:

            @block.tensor
            def _(pe):
                pe.wait_ge(normed.sem, normed.base + 1)
                for t in range(T):
                    mm = nc.tensor.transpose(xt[:, t * P:(t + 1) * P], dst[:, t, :], k.ident[:])
                mm.then_inc(xt_ready.sem, 1)

            @block.scalar
            def _(act):
                act.wait_ge(xt_ready.sem, xt_ready.base + 1)
                if on_turned:
                    on_turned(act, xt[:])
                else:
                    nc.scalar.copy(dst_t, xt[:])

            @block.vector
            def _(v):
                if copy_to is not None:
                    k.vchain(v, nc.vector.tensor_copy(copy_to, src))
                for a in addends:
                    k.vchain(v, nc.vector.tensor_tensor(src, src, a, ALU.add))
                norm_vector(k, v, src, dst, var_ready, rstd_ready, 1, gain, shift)
                nc.vector.engine_nop().then_inc(normed.sem, 1)

            @block.gpsimd
            def _(g):
                norm_gpsimd(k, g, var_ready, rstd_ready, 1)
        for counted in (var_ready, rstd_ready, normed, xt_ready):
            counted.base += 1



H0, KV0, D0, NODES = 16, 4, 64, 4
G0 = H0 // KV0
SINES_AFTER = 6
ROUND = 1.5 * 2.0 ** 23
TWO_PI = 6.283185

L0A = Pack("l0_attn")
for _key, _width in (("wq", (H0 + 1) * 2 * D0), ("wk", (H0 + 1) * 2 * D0), ("wv", KV0 * D0), ("wr", H0 * NODES),
                     ("wo", 8 * P), ("freq", 1), ("sin_scale", 1), ("earlier", NODES * NODES)):
    L0A.put(_key, _width)


def l0_attn_layout(i):
    swap = np.r_[D0 // 2:D0, 0:D0 // 2]

    def heads(w, n):
        w = np.asarray(w).reshape(P, n, D0)
        return np.stack([w, w[:, :, swap]], axis=2).reshape(P, n * 2 * D0)
    none = np.zeros((P, 2 * D0), np.float32)
    wq = np.concatenate([heads(i["L0_attn_wq"], H0), none], axis=1)
    wk = heads(i["L0_attn_wk"], KV0).reshape(P, KV0, 1, 2 * D0).repeat(G0, axis=2).reshape(P, H0 * 2 * D0)
    inv_freq = (1.0 / 10000.0 ** (np.arange(0, D0, 2, dtype=np.float32) / D0)).astype(np.float64)
    freq = np.tile(inv_freq / (2 * np.pi), 4).astype(np.float32).reshape(P, 1)
    sign = np.tile(np.r_[-np.ones(D0 // 2), np.ones(D0 // 2)], 2).reshape(P, 1)
    earlier = np.tril(np.ones((NODES, NODES)), -1).reshape(1, -1)
    return L0A.build({"wq": wq, "wk": np.concatenate([wk, none], axis=1), "wv": i["L0_attn_wv"], "wr": i["L0_attn_wr"],
                      "wo": tile_rows(np.asarray(i["L0_attn_wo"])), "freq": freq, "sin_scale": sign * TWO_PI,
                      "earlier": np.broadcast_to(earlier, (P, NODES * NODES))})


def l0_attn(k):
    nc = k.nc
    with ExitStack() as ctx:
        sb = lambda name, shape, dt=F32: k.sb("l0a_" + name, shape, dt, ctx)
        w = k.weights["l0_attn"]
        W = lambda key: L0A.view(w, key)
        values = sb("values", [P, T, KV0, D0 + 1])
        member = sb("member", [P, T, H0 + 2, NODES], BF16)
        absent = sb("absent", [P, T, H0 + 1, NODES], BF16)
        mix = sb("mix", [P, T, H0, NODES])
        before = sb("before", [P, 2, P], BF16)
        heads_out = sb("heads_out", [P, T, H0 * D0])
        l0_attn_route(k, W, values, member, absent, mix, before)
        l0_attn_heads(k, W, values, member, absent, mix, before, heads_out)
        close_sublayer(k, "l0a_close", heads_out[:], [W("wo")[:, c * P:(c + 1) * P] for c in range(8)], 8)


def l0_attn_route(k, W, values, member, absent, mix, before):
    nc = k.nc
    pairs = [P, T * H0, NODES, NODES]
    with ExitStack() as ctx:
        sb = lambda name, shape, dt=F32: k.sb("l0r_" + name, shape, dt, ctx)
        logits_ps = k.ps("l0r_logits_ps", [P, T * H0, NODES], ctx)
        values_ps = k.ps("l0r_values_ps", [P, T, KV0, D0], ctx)
        logits = sb("logits", [P, T * H0, NODES])
        greater = sb("greater", [P, T * H0, NODES, NODES])
        tied = sb("tied", [P, T * H0, NODES, NODES])
        rank = sb("rank", [P, T * H0, NODES])
        top = sb("top", [P, T * H0])
        exps = sb("exps", [P, T * H0, NODES])
        logits_ready, values_ready, shifted, exps_ready = k.sems("l0r", "logits_ready values_ready shifted exps_ready")
        with nc.Block() as block:

            @block.tensor
            def _(pe):
                for t in range(T):
                    mm = nc.tensor.matmul(logits_ps[:, t * H0:(t + 1) * H0, :], k.XT[:, t * P:(t + 1) * P], W("wr"),
                                          start=True, stop=True)
                mm.then_inc(logits_ready, 1)
                for t in range(T):
                    mm = nc.tensor.matmul(values_ps[:, t], k.XT[:, t * P:(t + 1) * P], W("wv"), start=True, stop=True)
                mm.then_inc(values_ready, 1)

            @block.gpsimd
            def _(g):
                nc.gpsimd.memset(values[:, :, :, D0:D0 + 1], 1.0)
                nc.gpsimd.memset(member[:, :, H0:, :], 0.0)
                nc.gpsimd.memset(absent[:, :, H0, :], 0.0)
                nc.gpsimd.memset(before[:, 1, :], 1.0)
                k.gchain(g, nc.gpsimd.memset(before[:, 0, :], 1.0))
                nc.gpsimd.affine_select(out=before[:, 0, :], in_=before[:, 0, :], compare_op=ALU.is_gt, fill=0.0,
                                        base=0, pattern=[[1, P]], channel_multiplier=-1)

            @block.scalar
            def _(act):
                act.wait_ge(shifted, 1)
                nc.scalar.activation(exps[:], exps[:], ACT.Exp).then_inc(exps_ready, 1)
                act.wait_ge(values_ready, 1)
                for t in range(0, T, 2):
                    nc.scalar.copy(values[:, t:t + 2, :, 0:D0].rearrange("p t c d -> p (t c) d"),
                                   values_ps[:, t:t + 2].rearrange("p t c d -> p (t c) d"))

            @block.vector
            def _(v):
                link = k.vchain
                v.wait_ge(logits_ready, 1)
                link(v, nc.vector.tensor_copy(logits[:], logits_ps[:]))
                link(v, nc.vector.tensor_reduce(top[:], logits[:], AX.X, ALU.max))
                nc.vector.tensor_tensor(exps[:], logits[:], bc(top[:].unsqueeze(2), [P, T * H0, NODES]),
                                        ALU.subtract).then_inc(shifted, 1)
                one = bc(logits[:].unsqueeze(3), pairs)
                other = bc(logits[:].unsqueeze(2), pairs)
                link(v, nc.vector.tensor_tensor(greater[:], other, one, ALU.is_gt))
                link(v, nc.vector.tensor_tensor(tied[:], other, one, ALU.is_equal))
                flat = "p a n m -> p a (n m)"
                link(v, nc.vector.tensor_tensor(tied[:].rearrange(flat), tied[:].rearrange(flat),
                                                bc(W("earlier").unsqueeze(1), [P, T * H0, NODES * NODES]), ALU.mult))
                link(v, nc.vector.tensor_tensor(greater[:], greater[:], tied[:], ALU.add))
                link(v, nc.vector.tensor_reduce(rank[:], greater[:], AX.X, ALU.add))
                ranks = rank[:].rearrange("p (t h) n -> p t h n", t=T)
                link(v, nc.vector.tensor_scalar(absent[:, :, 0:H0, :], ranks, 1.5, None, ALU.is_gt))
                link(v, nc.vector.tensor_scalar(member[:, :, 0:H0, :], ranks, 1.5, None, ALU.is_lt))
                link(v, nc.vector.tensor_scalar(rank[:], rank[:], 1.5, None, ALU.is_lt))
                v.wait_ge(exps_ready, 1)
                link(v, nc.vector.tensor_tensor(exps[:], exps[:], rank[:], ALU.mult))
                link(v, nc.vector.tensor_reduce(top[:], exps[:], AX.X, ALU.add))
                link(v, nc.vector.reciprocal(top[:], top[:]))
                link(v, nc.vector.tensor_tensor(
                    mix[:].rearrange("p t h (odd pair) -> p (t h) pair odd", odd=2),
                    exps[:].rearrange("p a (pair odd) -> p a pair odd", odd=2),
                    bc(top[:].unsqueeze(2).unsqueeze(3), [P, T * H0, 2, 2]), ALU.mult))


def l0_attn_heads(k, W, values, member, absent, mix, before, heads_out):
    nc = k.nc
    U = T
    AHEAD = 1
    CHUNKS = [("q", 0), ("k", 0), ("q", 1), ("k", 1)]
    assert U == B + len(CHUNKS)
    LO, HI = slice(0, D0), slice(D0, P)
    with ExitStack() as ctx:
        sb = lambda name, shape, dt=F32: k.sb("l0h_" + name, shape, dt, ctx)
        scores = k.ps("l0h_scores", [P, 2, 2 * BANK], ctx)
        turned = k.ps("l0h_turned", [P, 2 * BANK], ctx)
        out_ps = k.ps("l0h_out_ps", [P, BANK], ctx)
        side_ps = k.ps("l0h_side_ps", [P, BANK], ctx)
        weights = {x: sb("w" + x, [P, P]) for x in "qk"}
        member_next = sb("member_next", [P, T, NODES, D0], BF16)
        absent_now = sb("absent_now", [P, T, NODES], BF16)
        now = {x: sb(x + "_now", [P, 2, N]) for x in "qk"}
        turns = sb("turns", [P, B, 2, BANK])
        nearest = sb("nearest", [P, 2, BANK])
        touched = sb("touched", [1, 1])
        trig = sb("trig", [P, B, 2, BANK])
        rotated_now = {x: sb(x + "_rot", [P, 2, 2, S]) for x in "qk"}
        parts = {x: sb(x + "_part", [P, 2, S]) for x in "qk"}
        q_rot, k_rot = rotated_now["q"], rotated_now["k"]
        probs = sb("probs", [P, 2, NODES * S])
        probs_t = sb("probs_t", [P, NODES * S])
        top = sb("top", [P, 2, NODES])
        share = sb("share", [P, NODES])
        weighted = sb("weighted", [P, NODES, D0])
        (weights_ready, rows_next, rows_now, pos_ready, turns_copied, turns_ready, trig_ready, chunk_ready,
         chunk_copied, rotated, scores_ready, shifted, exp_ready, turned_ready, turned_copied, out_ready,
         out_used) = k.sems(
            "l0h", "weights_ready rows_next rows_now pos_ready turns_copied turns_ready trig_ready chunk_ready "
            "chunk_copied rotated scores_ready shifted exp_ready turned_ready turned_copied out_ready out_used")
        both = [P, 2, S]


        def load_weights_of(g, head):
            for x in "qk":
                nc.gpsimd.tensor_copy(weights[x][:], W("w" + x)[:, bass.ds(head * P, P)]).then_inc(weights_ready, 1)

        def load_rows_next(g, head):
            nc.gpsimd.tensor_copy(member_next[:], bc(member[:].rearrange("p t h n -> p t (h n)")
                                                     [:, :, bass.ds(head * NODES, NODES)].unsqueeze(3),
                                                     [P, T, NODES, D0])).then_inc(rows_next, 1)

        def load_rows_now(g, head, tiles):
            nc.gpsimd.tensor_copy(absent_now[:, tiles], absent[:].rearrange("p t h n -> p t (h n)")
                                  [:, tiles, bass.ds(head * NODES, NODES)]).then_inc(rows_now, 1)

        def reduce_angles(g, b, before_it):
            if before_it is not None:
                g.wait_ge(turns_ready, before_it)
            nc.gpsimd.tensor_tensor(touched[:], k.ones[0:1, 0:1], k.ones[0:1, 0:1], ALU.mult)
            k.gchain(g, nc.gpsimd.tensor_scalar(nearest[:], turns[:, b], ROUND, ROUND, ALU.add, ALU.subtract))
            nc.gpsimd.tensor_tensor(turns[:, b], turns[:, b], nearest[:], ALU.subtract).then_inc(turns_ready, 1)


        def positions(pe, b):
            for pair in range(2):
                at = side_ps[:, pair * S:(pair + 1) * S]
                rows = lambda t: member_next[:, t, 2 * pair:2 * pair + 2, :].rearrange("p n d -> p (n d)")
                nc.tensor.matmul(at, rows(TB * b), before[:].rearrange("p a b -> p (a b)"), start=True, stop=False,
                                 skip_group_check=True)
                mm = nc.tensor.matmul(at[:, P:S], rows(TB * b + 1), before[:, 0, :], start=False, stop=True,
                                      skip_group_check=True)
            mm.then_inc(pos_ready, 1)

        def project(pe, c):
            x, half = CHUNKS[c]
            nc.tensor.matmul(side_ps[:], weights[x][:], k.XT[:, half * BANK:(half + 1) * BANK], start=True, stop=True)\
                .then_inc(chunk_ready, 1)

        def score(pe, h, u):
            b, i = divmod(u, TB)
            width = (i + 1) * P
            for n in range(NODES):
                first = (n % 2) * BANK + (n // 2) * width
                at = scores[:, u % 2, first:first + width]
                for c in range(i + 1):
                    nc.tensor.matmul(at[:, c * P:(c + 1) * P], bc(absent_now[:, TB * b + c, n:n + 1], [P, P]),
                                     k.masker[:], start=(c == 0), stop=False, skip_group_check=True)
                nc.tensor.matmul(at[:, i * P:(i + 1) * P], k.above[:], k.masker[:], start=False, stop=False,
                                 skip_group_check=True)
                part = (LO, HI)[n % 2]
                mm = nc.tensor.matmul(at, q_rot[part, b % 2, n // 2, i * P:(i + 1) * P],
                                      k_rot[part, b % 2, n // 2, 0:width], start=False, stop=True,
                                      skip_group_check=True)
            mm.then_inc(scores_ready, 1)


        def angles(act, b):
            nc.scalar.activation(turns[:, b, 0, :], side_ps[:], ACT.Identity, scale=W("freq"))
            nc.scalar.activation(turns[:, b, 1, :], side_ps[:], ACT.Identity, scale=W("freq"),
                                 bias=k.quarter[:]).then_inc(turns_copied, 1)

        def sines(act):
            nc.scalar.activation(trig[:, :, 0, :], turns[:, :, 0, :], ACT.Sin, scale=W("sin_scale"))
            nc.scalar.activation(trig[:, :, 1, :], turns[:, :, 1, :], ACT.Sin, scale=TWO_PI).then_inc(trig_ready, 1)

        def take_chunk(act, c):
            x, half = CHUNKS[c]
            for swapped, source in enumerate((LO, HI)):
                for part in (LO, HI):
                    last = nc.scalar.copy(now[x][part, swapped, half * BANK:(half + 1) * BANK], side_ps[source, :])
            last.then_inc(chunk_copied, 1)


        def rotate(v, h, b):
            if b % 2 == 0:
                v.wait_ge(chunk_copied, h * 4 + b + 2)
            for x in "qk":
                src = lambda s: bc(now[x][:, s, b * S:(b + 1) * S].unsqueeze(1), both)
                table = lambda s: trig[:, b, s, :].rearrange("p (a s) -> p a s", a=2)
                dst = rotated_now[x][:, b % 2]
                nc.vector.tensor_tensor(parts[x][:], src(1), table(0), ALU.mult)
                k.vchain(v, nc.vector.tensor_tensor(dst, src(0), table(1), ALU.mult))
                done = nc.vector.tensor_tensor(dst, dst, parts[x][:], ALU.add)
            done.then_inc(rotated, 1)

        with nc.Block() as block:

            @block.gpsimd
            def _(g):
                load_rows_next(g, 0)
                load_weights_of(g, 0)
                load_rows_now(g, 0, slice(0, 4))
                load_rows_now(g, 0, slice(4, T))
                g.wait_ge(pos_ready, B)
                load_rows_next(g, 1)
                for b in range(B):
                    g.wait_ge(turns_copied, b + 1)
                    reduce_angles(g, b, b if b else None)
                with nc.gpsimd.Fori(0, H0) as h:
                    k.gchain.enter(h, B)
                    g.wait_ge(chunk_ready, (h + 1) * 4)
                    load_weights_of(g, h + 1)
                    for b in range(B):
                        g.wait_ge(turns_copied, (h + 1) * B + b + 1)
                        reduce_angles(g, b, (h + 1) * B + b)
                    g.wait_ge(pos_ready, (h + 2) * B)
                    load_rows_next(g, h + 2)
                    g.wait_ge(scores_ready, h * U + 4 + AHEAD)
                    load_rows_now(g, h + 1, slice(0, 4))
                    g.wait_ge(scores_ready, (h + 1) * U + AHEAD)
                    load_rows_now(g, h + 1, slice(4, T))
                    k.gchain.leave(H0)

            @block.tensor
            def _(pe):
                for ahead in (scores_ready, turned_ready):
                    pe.sem_inc(ahead, AHEAD)
                pe.wait_ge(rows_next, 1)
                for b in range(B):
                    if b >= 1:
                        pe.wait_ge(turns_copied, b)
                    positions(pe, b)
                pe.wait_ge(turns_copied, B)
                pe.wait_ge(weights_ready, 2)
                for c in range(4):
                    if c >= 1:
                        pe.wait_ge(chunk_copied, c)
                    project(pe, c)
                pe.wait_ge(rotated, 1)
                pe.wait_ge(rows_now, 1)
                score(pe, 0, 0)
                with nc.tensor.Fori(0, KV0) as kv:
                    with nc.tensor.Fori(0, G0) as j:
                        h = kv * G0 + j

                        def weigh(u):
                            b, i = divmod(u, TB)
                            pe.wait_ge(turned_copied, h * U + u + 1)
                            pe.wait_ge(out_used, h * U + u + AHEAD)
                            for n in range(NODES):
                                for c in range(i + 1):
                                    x = n * (i + 1) + c
                                    mm = nc.tensor.matmul(out_ps[:, n * (D0 + 1):(n + 1) * (D0 + 1)],
                                                          probs_t[:, x * P:(x + 1) * P],
                                                          values[:, TB * b + c].rearrange("p c d -> p (c d)")
                                                          [:, bass.ds(kv * (D0 + 1), D0 + 1)],
                                                          start=(c == 0), stop=(c == i))
                            mm.then_inc(out_ready, 1)

                        for u in range(U):
                            if u + 1 < U:
                                if (u + 1) % TB == 0:
                                    pe.wait_ge(rotated, h * B + (u + 1) // TB + 1)
                                if u + 1 == 4:
                                    pe.wait_ge(rows_now, h * 2 + 2)
                                pe.wait_ge(shifted, h * U + u + AHEAD)
                                score(pe, h, u + 1)
                            if u >= 1:
                                weigh(u - 1)
                            if u == 0:
                                pe.wait_ge(chunk_copied, (h + 1) * 4)
                                pe.wait_ge(rows_next, h + 2)
                            elif u <= B:
                                pe.wait_ge(turns_copied, (h + 1) * B + u)
                            else:
                                pe.wait_ge(chunk_copied, (h + 1) * 4 + u - B)
                            if u == B:
                                pe.wait_ge(weights_ready, (h + 2) * 2)
                            if u < B:
                                positions(pe, u)
                            else:
                                project(pe, u - B)
                            pe.wait_ge(exp_ready, h * U + u + 1)
                            b, i = divmod(u, TB)
                            for x in range(NODES * (i + 1)):
                                mm = nc.tensor.transpose(turned[:, x * P:(x + 1) * P],
                                                         probs[:, u % 2, x * P:(x + 1) * P], k.ident[:])
                            mm.then_inc(turned_ready, 1)
                        pe.wait_ge(rotated, (h + 1) * B + 1)
                        pe.wait_ge(rows_now, h * 2 + 3)
                        pe.wait_ge(shifted, h * U + U - 1 + AHEAD)
                        score(pe, h + 1, 0)
                        weigh(U - 1)

            @block.scalar
            def _(act):
                for b in range(B):
                    act.wait_ge(pos_ready, b + 1)
                    angles(act, b)
                for c in range(4):
                    act.wait_ge(chunk_ready, c + 1)
                    take_chunk(act, c)
                act.wait_ge(turns_ready, B)
                sines(act)
                with nc.scalar.Fori(0, H0) as h:
                    for u in range(U):
                        cols = NODES * (u % TB + 1) * P
                        act.wait_ge(shifted, h * U + u + 1 + AHEAD)
                        nc.scalar.activation(probs[:, u % 2, 0:cols], probs[:, u % 2, 0:cols], ACT.Exp,
                                             scale=D0 ** -0.5).then_inc(exp_ready, 1)
                        act.wait_ge(turned_ready, h * U + u + 1 + AHEAD)
                        nc.scalar.copy(probs_t[:, 0:cols], turned[:, 0:cols]).then_inc(turned_copied, 1)
                        if u < B:
                            act.wait_ge(pos_ready, (h + 1) * B + u + 1)
                            if u == 0:
                                act.wait_ge(trig_ready, h + 1)
                            angles(act, u)
                        else:
                            act.wait_ge(chunk_ready, (h + 1) * 4 + u - B + 1)
                            act.wait_ge(rotated, h * B + (2 if u < B + 2 else 4))
                            take_chunk(act, u - B)
                        if u == SINES_AFTER:
                            act.wait_ge(turns_ready, (h + 2) * B)
                            act.wait_ge(rotated, (h + 1) * B)
                            sines(act)

            @block.vector
            def _(v):
                link = k.vchain
                for ahead in (shifted, out_used):
                    v.sem_inc(ahead, AHEAD)
                v.wait_ge(trig_ready, 1)
                rotate(v, 0, 0)
                with nc.vector.Fori(0, H0) as h:
                    link.enter(h, 2 * B + U * 4)

                    def finish(u):
                        v.wait_ge(out_ready, h * U + u + 1)
                        out = out_ps[:, 0:NODES * (D0 + 1)].rearrange("p (n d) -> p n d", n=NODES)
                        link(v, nc.vector.reciprocal(share[:], out[:, :, D0]))
                        link(v, nc.vector.tensor_tensor(share[:], share[:], mix[:, u].rearrange("p h n -> p (h n)")
                                                        [:, bass.ds(h * NODES, NODES)], ALU.mult))
                        link(v, nc.vector.tensor_tensor(weighted[:], out[:, :, 0:D0],
                                                        bc(share[:].unsqueeze(2), [P, NODES, D0]), ALU.mult))
                        nc.vector.tensor_reduce(heads_out[:, u, bass.ds(h * D0, D0)],
                                                weighted[:].rearrange("p n d -> p d n"), AX.X, ALU.add)\
                            .then_inc(out_used, 1)

                    for u in range(U):
                        b, i = divmod(u, TB)
                        cols = NODES * (i + 1) * P
                        banks = scores[:, u % 2].rearrange("p (odd c) -> p odd c", odd=2)[:, :, 0:cols // 2]\
                            .rearrange("p odd (pair w) -> p odd pair w", pair=2)
                        packed = probs[:, u % 2, 0:cols].rearrange("p (odd pair w) -> p odd pair w", odd=2, pair=2)
                        tops = top[:, u % 2].rearrange("p (odd pair) -> p odd pair", odd=2)
                        v.wait_ge(scores_ready, h * U + u + 1 + AHEAD)
                        link(v, nc.vector.tensor_reduce(tops, banks, AX.X, ALU.max))
                        v.wait_ge(turned_ready, h * U + max(u - 1, 0) + AHEAD)
                        nc.vector.tensor_tensor(packed, banks, bc(tops.unsqueeze(3), [P, 2, 2, (i + 1) * P]),
                                                ALU.subtract).then_inc(shifted, 1)
                        if i == 0 and b + 1 < B:
                            v.wait_ge(scores_ready, h * U + TB * b + AHEAD)
                            rotate(v, h, b + 1)
                        if u >= 1:
                            finish(u - 1)
                    v.wait_ge(trig_ready, h + 2)
                    v.wait_ge(scores_ready, h * U + U - TB + AHEAD)
                    rotate(v, h + 1, 0)
                    finish(U - 1)
                    link.leave(H0)



HX, DX = 16, P // 16


def cross_pack(name):
    pack = Pack(name)
    for key, width in (("wq", P), ("wk", P), ("wv", P), ("wo", P), ("bq", 1), ("bk", 1), ("bv", P), ("bo", P)):
        pack.put(key, width)
    return pack


L0X, L1X = cross_pack("l0_xattn"), cross_pack("l1_xattn")


def l0_xattn_layout(i):
    zero, row = np.zeros((P, 1), np.float32), np.zeros((P, P), np.float32)
    return L0X.build({"wq": i["L0_xattn_w_q"], "wk": i["L0_xattn_w_k"], "wv": i["L0_xattn_w_v"],
                      "wo": i["L0_xattn_w_o"], "bq": zero, "bk": zero, "bv": row, "bo": on_all(i["L0_xattn_b_o"])})


def l1_xattn_layout(i):
    g = lambda key: np.asarray(i["L1_xattn_" + key])
    return L1X.build({"wq": g("Wq").T, "wk": g("Wk").T, "wv": g("Wv").T, "wo": g("Wp").T, "bq": column(g("bq")),
                      "bk": column(g("bk")), "bv": on_all(g("bv")), "bo": on_all(g("bp"))})


def narrow_cross_attention(k, tag, pack, w, mask):
    nc = k.nc
    W = lambda key: pack.view(w, key)
    with ExitStack() as ctx:
        sb = lambda name, shape: k.sb(f"{tag}_{name}", shape, F32, ctx)
        q_t, k_t, v_both = sb("q_t", [P, N]), sb("k_t", [P, B * SC]), sb("v_both", [P, B, P])
        keys = sb("keys", [P, B, HX, SC])
        values = sb("values", [P, B, HX, DX + 1])
        heads_out = sb("heads_out", [P, T, P])

        def all_values(pe, out):
            for b in range(B):
                mm = nc.tensor.matmul(out[:, b * P:(b + 1) * P], k.ctx_twice[:, b].rearrange("p a s -> p (a s)"), W("wv"), start=True, stop=True)
            return mm

        products(k, tag + "_proj", [
            (SCALAR, narrow(k, W("wk"), k.ctx_t[:], B * SC), activated(k, k_t[:], bias=W("bk"), cols=B * SC)),
            (VECTOR, all_values, lambda v, out: nc.vector.tensor_tensor(
                v_both[:], out[:, 0:BANK].rearrange("p (b n) -> p b n", b=B), bc(W("bv").unsqueeze(1), [P, B, P]),
                ALU.add)),
            (SCALAR, wide(k, W("wq"), k.XT), activated(k, q_t[:], bias=W("bq"))),
        ])
        with nc.Block() as block:

            @block.vector
            def _(v):
                for b in range(B):
                    nc.vector.tensor_tensor(keys[:, b], bc(k_t[:, b * SC:(b + 1) * SC].unsqueeze(1), [P, HX, SC]),
                                            bc(k.own_head.unsqueeze(2), [P, HX, SC]), ALU.mult)

            @block.gpsimd
            def _(g):
                parity = bc(k.own_parity.unsqueeze(2), [P, HX, DX])
                for b in range(B):
                    nc.gpsimd.tensor_tensor(values[:, b, :, 0:DX], v_both[:, b].rearrange("p (h d) -> p h d", h=HX),
                                            parity, ALU.mult)
                    nc.gpsimd.tensor_copy(values[:, b, :, DX], k.own_parity)

        def unit(t):
            b = t // TB

            def score(out):
                for c in range(2):
                    mm = nc.tensor.matmul(out[:, c, :], q_t[:, t * P:(t + 1) * P], keys[:, b, c * 8:(c + 1) * 8, :],
                                          start=True, stop=True)
                return mm

            def product(out, probs_t):
                for x in range(8):
                    mm = nc.tensor.matmul(out[:, 2 * x * (DX + 1):2 * (x + 1) * (DX + 1)],
                                          probs_t[:, x * P:(x + 1) * P], values[:, b, 2 * x:2 * x + 2, :],
                                          start=True, stop=True)
                return mm
            return (2 * BANK, HX, score, product, heads_out[:, t].rearrange("p (h d) -> p h d", h=HX),
                    mask(t) if mask else None)

        attention(k, tag + "_att", [unit(t) for t in range(T)], DX ** -0.5)
        close_sublayer(k, tag + "_close", heads_out[:], [W("wo")], 1, bias=W("bo"))


def l0_xattn(k):
    nc = k.nc
    with ExitStack() as ctx:
        keep = k.sb("l0x_keep", [P, TB, SC], F32, ctx)
        add = k.sb("l0x_add", [P, TB, SC], F32, ctx)
        with nc.Block() as block:

            @block.vector
            def _(v):
                k.vchain(v, nc.vector.tensor_scalar(keep[:], k.mask0[:], 0.0, None, ALU.not_equal))
                nc.vector.tensor_scalar(add[:], keep[:], 1.0, 1e9 * DX ** 0.5, ALU.subtract, ALU.mult)
        narrow_cross_attention(k, "l0x", L0X, k.weights["l0_xattn"],
                               lambda t: (keep[:, t % TB, :], add[:, t % TB, :]))


def l1_xattn(k):
    narrow_cross_attention(k, "l1x", L1X, k.weights["l1_xattn"], None)



E0, F0 = 8, 4 * P
L0F = Pack("l0_ffn")
for _key, _width in (("wqkv", 3 * P), ("wo", P), ("gate", E0 + 2), ("bq", 1), ("bk", 1), ("bv", P), ("bo", P),
                     ("g1", P), ("s1", P), ("g2", P), ("s2", P), ("coef_b", 2), ("prio", E0)):
    L0F.put(_key, _width)


def l0_ffn_layout(i):
    g = lambda key: np.asarray(i["L0_ffn_" + key])
    b = g("bqkv")
    return L0F.build({"wqkv": g("Wqkv"), "wo": g("Wo"), "gate": np.concatenate([g("gate_w"), g("coef_w")], axis=1),
                      "bq": column(b[:P]), "bk": column(b[P:2 * P]), "bv": on_all(b[2 * P:]), "bo": on_all(g("bo")),
                      "g1": on_all(g("ln1_g")), "s1": on_all(g("ln1_b")), "g2": on_all(g("ln2_g")),
                      "s2": on_all(g("ln2_b")), "coef_b": on_all(g("coef_b")),
                      "prio": on_all(np.arange(E0, 0, -1, dtype=np.float32))})


def l0_experts_layout(i):
    g = lambda key: np.asarray(i["L0_ffn_" + key])
    out = np.zeros((E0 + 1, P, 2 * F0 + F0 // P + P), np.float32)
    for e in range(E0 + 1):
        w1, b1, w2, b2 = (g(x)[e] for x in ("W1", "b1", "W2", "b2")) if e < E0 else \
            (g(x) for x in ("rW1", "rb1", "rW2", "rb2"))
        out[e, :, 0:F0] = w1
        out[e, :, F0:2 * F0] = tile_rows(w2)
        out[e, :, 2 * F0:2 * F0 + F0 // P] = b1.reshape(F0 // P, P).T
        out[e, :, 2 * F0 + F0 // P:] = on_all(b2)
    return out


def l0_ffn(k):
    nc = k.nc
    w = k.weights["l0_ffn"]
    W = lambda key: L0F.view(w, key)
    with ExitStack() as ctx:
        sb = lambda name, shape, dt=F32: k.sb("l0f_" + name, shape, dt, ctx)
        x_in, xn, xn_t = sb("x_in", [P, T, P]), sb("xn", [P, T, P]), sb("xn_t", [P, N])
        norm_and_turn(k, "l0f_ln1", k.X[:], xn[:], xn_t[:], W("g1"), W("s1"), copy_to=x_in[:])
        with ExitStack() as att:
            q_t, k_t = k.sb("l0f_q_t", [P, N], F32, att), k.sb("l0f_k_t", [P, N], F32, att)
            keys = k.sb("l0f_keys", [P, 4, N], F32, att)
            values = k.sb("l0f_values", [P, T, HX, DX + 1], F32, att)
            heads_out = k.sb("l0f_heads_out", [P, T, P], F32, att)

            def take_values(v, out):
                for t in range(T):
                    ins = nc.vector.tensor_tensor(values[:, t, :, 0:DX], out[:, t * P:(t + 1) * P]
                                                  .rearrange("p (h d) -> p h d", h=HX),
                                                  W("bv").rearrange("p (h d) -> p h d", h=HX), ALU.add)
                return ins

            products(k, "l0f_proj", [
                (SCALAR, wide(k, W("wqkv")[:, P:2 * P], xn_t), activated(k, k_t[:], bias=W("bk"))),
                (VECTOR, by_tile(k, xn_t, W("wqkv")[:, 2 * P:3 * P], P), take_values),
                (SCALAR, wide(k, W("wqkv")[:, 0:P], xn_t), activated(k, q_t[:], bias=W("bq"))),
            ])
            with nc.Block() as block:

                @block.vector
                def _(v):
                    for j in range(4):
                        nc.vector.tensor_scalar(keys[:, j, :], k_t[:], k.own_of_four[:, j:j + 1], None, ALU.mult)

                @block.gpsimd
                def _(g):
                    nc.gpsimd.memset(values[:, :, :, DX:DX + 1], 1.0)

            def unit(t, g):
                rows, b = slice(32 * g, 32 * g + 32), t // TB

                def score(out):
                    for c in range(2):
                        mm = nc.tensor.matmul(out[:, c, :], q_t[rows, t * P:(t + 1) * P],
                                              keys[rows, 2 * c:2 * c + 2, b * S:(b + 1) * S], start=True, stop=True)
                    return mm

                def product(out, probs_t):
                    for j in range(4):
                        for c in range(TB):
                            mm = nc.tensor.matmul(out[:, j * (DX + 1):(j + 1) * (DX + 1)],
                                                  probs_t[:, (2 * j + c) * P:(2 * j + c + 1) * P],
                                                  values[:, TB * b + c, 4 * g + j, :], start=(c == 0), stop=(c == 1))
                    return mm
                return (2 * BANK, 4, score, product,
                        heads_out[:, t, rows].rearrange("p (h d) -> p h d", h=4), None)

            attention(k, "l0f_att", [unit(t, g) for t in range(T) for g in range(4)], DX ** -0.5)
            close_sublayer(k, "l0f_mid", heads_out[:], [W("wo")], 1, bias=W("bo"), to=(xn[:], xn_t[:]),
                           gain=W("g2"), shift=W("s2"))
        weight = sb("weight", [P, T, E0 + 1])
        total = sb("total", [P, T, P])
        l0_ffn_route(k, W, xn_t, weight)
        l0_ffn_experts(k, xn_t, weight, total)
        norm_and_turn(k, "l0f_out", k.X[:], k.X[:], k.XT[:], addends=(x_in[:], total[:]))


def l0_ffn_route(k, W, xn_t, weight):
    nc = k.nc
    with ExitStack() as ctx:
        sb = lambda name, shape: k.sb("l0g_" + name, shape, F32, ctx)
        logits_ps = k.ps("l0g_logits_ps", [P, T, E0 + 2], ctx)
        logits, top, top2, total = sb("logits", [P, T, E0 + 2]), sb("top", [P, T]), sb("top2", [P, T]), sb("total", [P, T])
        exps, chosen, total2, share = (sb("exps", [P, T, E0 + 2]), sb("chosen", [P, T, E0]), sb("total2", [P, T]),
                                       sb("share", [P, T]))
        ready, shifted, exps_ready = k.sems("l0g", "ready shifted exps_ready")
        with nc.Block() as block:

            @block.tensor
            def _(pe):
                for t in range(T):
                    mm = nc.tensor.matmul(logits_ps[:, t, :], xn_t[:, t * P:(t + 1) * P], W("gate"), start=True,
                                          stop=True)
                mm.then_inc(ready, 1)

            @block.scalar
            def _(act):
                act.wait_ge(shifted, 1)
                nc.scalar.activation(exps[:], exps[:], ACT.Exp).then_inc(exps_ready, 1)

            @block.vector
            def _(v):
                link = k.vchain
                experts, coefs = slice(0, E0), slice(E0, E0 + 2)
                e_shape, c_shape = [P, T, E0], [P, T, 2]
                v.wait_ge(ready, 1)
                link(v, nc.vector.tensor_copy(logits[:], logits_ps[:]))
                link(v, nc.vector.tensor_tensor(logits[:, :, coefs], logits[:, :, coefs],
                                                bc(W("coef_b").unsqueeze(1), c_shape), ALU.add))
                link(v, nc.vector.tensor_reduce(top[:], logits[:, :, experts], AX.X, ALU.max))
                link(v, nc.vector.tensor_reduce(top2[:], logits[:, :, coefs], AX.X, ALU.max))
                link(v, nc.vector.tensor_tensor(exps[:, :, coefs], logits[:, :, coefs],
                                                bc(top2[:].unsqueeze(2), c_shape), ALU.subtract))
                nc.vector.tensor_tensor(exps[:, :, experts], logits[:, :, experts], bc(top[:].unsqueeze(2), e_shape),
                                        ALU.subtract).then_inc(shifted, 1)
                link(v, nc.vector.tensor_tensor(chosen[:], logits[:, :, experts], bc(top[:].unsqueeze(2), e_shape),
                                                ALU.is_equal))
                link(v, nc.vector.tensor_tensor(chosen[:], chosen[:], bc(W("prio").unsqueeze(1), e_shape), ALU.mult))
                link(v, nc.vector.tensor_reduce(top[:], chosen[:], AX.X, ALU.max))
                link(v, nc.vector.tensor_tensor(chosen[:], chosen[:], bc(top[:].unsqueeze(2), e_shape), ALU.is_equal))
                v.wait_ge(exps_ready, 1)
                link(v, nc.vector.tensor_reduce(total[:], exps[:, :, experts], AX.X, ALU.add))
                link(v, nc.vector.tensor_reduce(total2[:], exps[:, :, coefs], AX.X, ALU.add))
                link(v, nc.vector.reciprocal(total[:], total[:]))
                link(v, nc.vector.reciprocal(total2[:], total2[:]))
                link(v, nc.vector.tensor_tensor(exps[:, :, coefs], exps[:, :, coefs],
                                                bc(total2[:].unsqueeze(2), c_shape), ALU.mult))
                link(v, nc.vector.tensor_tensor(share[:], total[:], exps[:, :, E0], ALU.mult))
                link(v, nc.vector.tensor_tensor(weight[:, :, experts], chosen[:], bc(share[:].unsqueeze(2), e_shape),
                                                ALU.mult))
                link(v, nc.vector.tensor_copy(weight[:, :, E0], exps[:, :, E0 + 1]))


def l0_ffn_experts(k, xn_t, weight, total):
    nc = k.nc
    CH = F0 // P
    PER, TURNS = 3, (E0 + 1) // 3
    with ExitStack() as ctx:
        sb = lambda name, shape: k.sb("l0e_" + name, shape, F32, ctx)
        hidden_ps = k.ps("l0e_hidden_ps", [P, 4, BANK], ctx)
        out_ps = k.ps("l0e_out_ps", [P, 4, BANK], ctx)
        experts = sb("experts", [P, PER, 2 * F0 + CH + P])
        hidden = sb("hidden", [P, 2, CH, BANK])
        weighted = sb("weighted", [P, 4, P])
        (loaded0, loaded1, loaded2, hidden_ready, gelu_ready, out_ready, out_used) = k.sems(
            "l0e", "loaded0 loaded1 loaded2 hidden_ready gelu_ready out_ready out_used")
        loaded = (loaded0, loaded1, loaded2)
        with nc.Block() as block:

            @block.sync
            def _(sp):
                for j in range(PER):
                    sp.dma_start(experts[:, j, :], k.dram["l0_experts"][j]).then_inc(loaded[j], 16)
                with nc.sync.Fori(1, TURNS) as turn:
                    for j in range(PER):
                        sp.wait_ge(out_ready, (turn * PER + j - PER + 1) * 2)
                        sp.dma_start(experts[:, j, :], k.dram["l0_experts"].rearrange("e p n -> (e p) n")
                                     [bass.ds((turn * PER + j) * P, P), :]).then_inc(loaded[j], 16)

            @block.tensor
            def _(pe):
                with nc.tensor.Fori(0, TURNS) as turn:
                    for j in range(PER):
                        e = turn * PER + j
                        w = experts[:, j, :]
                        pe.wait_ge(loaded[j], (turn + 1) * 16)

                        def up(half):
                            for c in range(CH):
                                if j or half:
                                    pe.wait_ge(gelu_ready, e * 2 * CH + half * CH + c - 2)
                                else:
                                    pe.wait_ge(gelu_ready, turn * (PER * 2 * CH) + 1)
                                nc.tensor.matmul(hidden_ps[:, c, :], w[:, c * P:(c + 1) * P],
                                                 xn_t[:, half * BANK:(half + 1) * BANK], start=True, stop=True)\
                                    .then_inc(hidden_ready, 1)

                        def down(half):
                            pe.wait_ge(gelu_ready, e * 2 * CH + (half + 1) * CH + 1)
                            at = (2 * j + half) % 4
                            pe.wait_ge(out_used, e * 2 + half + (0 if j or half else 1))
                            for t in range(4):
                                for c in range(CH):
                                    nc.tensor.matmul(out_ps[:, at, t * P:(t + 1) * P],
                                                     hidden[:, half, c, t * P:(t + 1) * P],
                                                     w[:, F0 + c * P:F0 + (c + 1) * P], start=(c == 0), stop=False)
                                mm = nc.tensor.matmul(out_ps[:, at, t * P:(t + 1) * P], k.ones[0:1, :],
                                                      w[0:1, 2 * F0 + CH:], start=False, stop=True)
                            mm.then_inc(out_ready, 1)
                        up(0)
                        up(1)
                        down(0)
                        down(1)

            @block.scalar
            def _(act):
                act.sem_inc(gelu_ready, 1)
                with nc.scalar.Fori(0, TURNS) as turn:
                    for j in range(PER):
                        e = turn * PER + j
                        act.wait_ge(loaded[j], (turn + 1) * 16)
                        for half in range(2):
                            for c in range(CH):
                                act.wait_ge(hidden_ready, e * 2 * CH + half * CH + c + 1)
                                nc.scalar.activation(hidden[:, half, c, :], hidden_ps[:, c, :], ACT.Gelu,
                                                     bias=experts[:, j, 2 * F0 + c:2 * F0 + c + 1])\
                                    .then_inc(gelu_ready, 1)

            @block.vector
            def _(v):
                link = k.vchain
                link(v, nc.vector.memset(total[:], 0.0))
                v.sem_inc(out_used, 1)
                with nc.vector.Fori(0, TURNS) as turn:
                    link.enter(turn, PER * 2)
                    for j in range(PER):
                        for half in range(2):
                            n = turn * (PER * 2) + 2 * j + half
                            tiles = slice(4 * half, 4 * half + 4)
                            v.wait_ge(out_ready, n + 1)
                            share = weight[:, tiles, :].rearrange("p t e -> p e t")[:, bass.ds(turn * PER + j, 1), :]
                            nc.vector.tensor_tensor(weighted[:], out_ps[:, (2 * j + half) % 4, :]
                                                    .rearrange("p (t n) -> p t n", n=P),
                                                    bc(share.rearrange("p e t -> p (e t)").unsqueeze(2), [P, 4, P]),
                                                    ALU.mult).then_inc(out_used, 1)
                            v.wait_ge(out_used, n + 2)
                            link(v, nc.vector.tensor_tensor(total[:, tiles, :], total[:, tiles, :], weighted[:],
                                                            ALU.add))
                    link.leave(TURNS)



R1 = 32
L1A = Pack("l1_attn")
for _key, _width in (("wi", P), ("wsin", R1), ("wd", R1), ("wsel", R1), ("wso", P), ("wg", P), ("wout", P),
                     ("ln_g", 1), ("ln_b", 1), ("mix_w", 3), ("mix_b", 1), ("bi", 1), ("bsin", 1), ("bd", 1),
                     ("bsel", 1), ("bso", 1), ("bg", 1), ("bout", P)):
    L1A.put(_key, _width)


def l1_attn_layout(i):
    g = lambda key: np.asarray(i["L1_attn_" + key])
    parts = {x: column(g(x)) for x in ("ln_g", "ln_b", "mix_b", "bi", "bsin", "bd", "bsel", "bso", "bg")}
    parts.update({x.lower(): g(x) for x in ("Wi", "Wsin", "Wd", "Wsel", "Wso", "Wg", "Wout")})
    return L1A.build({**parts, "mix_w": g("mix_w").reshape(P, 3), "bout": on_all(g("bout"))})


def l1_attn(k):
    nc = k.nc
    w = k.weights["l1_attn"]
    W = lambda key: L1A.view(w, key)
    with ExitStack() as ctx:
        sb = lambda name, shape, dt=F32: k.sb("l1a_" + name, shape, dt, ctx)
        xn, h_t, mixed = sb("xn", [P, T, P]), sb("h_t", [P, B, S + 2]), sb("mixed", [P, B, S])
        u, gate, out_t = sb("u", [P, N]), sb("gate", [P, N]), sb("out_t", [P, N])
        x_state, decay, select, states = (sb(x, [R1, N]) for x in ("x_state", "decay", "select", "states"))

        norm_and_turn(k, "l1a_ln", k.X[:], xn[:], None, on_turned=lambda act, out: nc.scalar.activation(
            h_t[:, :, 1:S + 1], out.rearrange("p (b s) -> p b s", b=B), ACT.Identity, bias=W("ln_b"),
            scale=W("ln_g")))
        with nc.Block() as block:

            @block.vector
            def _(v):
                link = k.vchain
                nc.vector.memset(h_t[:, :, 0:1], 0.0)
                link(v, nc.vector.memset(h_t[:, :, S + 1:S + 2], 0.0))
                link(v, nc.vector.tensor_scalar(mixed[:], h_t[:, :, 0:S], W("mix_w")[:, 0:1], W("mix_b"), ALU.mult,
                                                ALU.add))
                for tap in (1, 2):
                    link(v, nc.vector.scalar_tensor_tensor(mixed[:], h_t[:, :, tap:tap + S],
                                                           W("mix_w")[:, tap:tap + 1], mixed[:], ALU.mult, ALU.add))
        mixed_t = mixed[:].rearrange("p b s -> p (b s)")
        small = lambda key: W(key)[0:R1, :]
        products(k, "l1a_proj", [
            (SCALAR, wide(k, W("wsin"), mixed_t, R1), activated(k, x_state[:], ACT.Tanh, small("bsin"), R1)),
            (SCALAR, wide(k, W("wd"), mixed_t, R1), activated(k, decay[:], ACT.Sigmoid, small("bd"), R1)),
            (SCALAR, wide(k, W("wsel"), mixed_t, R1), activated(k, select[:], ACT.Sigmoid, small("bsel"), R1)),
            (SCALAR, wide(k, W("wi"), mixed_t), activated(k, u[:], ACT.Tanh, W("bi"))),
            (SCALAR, wide(k, W("wg"), mixed_t), activated(k, gate[:], ACT.Sigmoid, W("bg"))),
        ])
        with nc.Block() as block:

            @block.vector
            def _(v):
                link = k.vchain
                link(v, nc.vector.tensor_scalar(states[:], decay[:], -1.0, 1.0, ALU.mult, ALU.add))
                link(v, nc.vector.tensor_tensor(x_state[:], states[:], x_state[:], ALU.mult))
                for b in range(B):
                    one = slice(b * S, (b + 1) * S)
                    link(v, nc.vector.tensor_tensor_scan(states[:, one], decay[:, one], x_state[:, one], 0.0,
                                                         ALU.mult, ALU.add))
                link(v, nc.vector.tensor_tensor(states[:], states[:], select[:], ALU.mult))

        def blend(v, out):
            k.vchain(v, nc.vector.scalar_tensor_tensor(out_t[:], out, W("bso"), u[:], ALU.add, ALU.subtract))
            k.vchain(v, nc.vector.tensor_tensor(out_t[:], out_t[:], gate[:], ALU.mult))
            return nc.vector.tensor_tensor(out_t[:], out_t[:], u[:], ALU.add)
        products(k, "l1a_y", [(VECTOR, wide(k, small("wso"), states), blend)])
        close_sublayer(k, "l1a_close", None, [W("wout")], 1, bias=W("bout"), doubled=True, features_t=[out_t])



E1, F1, FS = 16, 4 * P, 2 * P
CAP = N * 2 // E1
assert CAP == P
L1F = Pack("l1_ffn")
for _key, _width in (("gate", E1), ("sg", FS), ("su", FS), ("sd", FS), ("slot_number", P)):
    L1F.put(_key, _width)


def l1_ffn_layout(i):
    g = lambda key: np.asarray(i["L1_ffn_" + key])
    return L1F.build({"gate": g("gate_w").T, "sg": g("Sg").T, "su": g("Su").T, "sd": tile_rows(g("Sd").T),
                      "slot_number": on_all(np.arange(P, dtype=np.float32))})


def l1_experts_layout(i):
    g = lambda key: np.asarray(i["L1_ffn_" + key])
    wd = g("Wd").transpose(0, 2, 1).reshape(E1, F1 // P, P, P).transpose(0, 2, 1, 3).reshape(E1, P, F1)
    return np.ascontiguousarray(np.concatenate([g("Wg").transpose(0, 2, 1), g("Wu").transpose(0, 2, 1), wd], axis=2))


def l1_ffn(k):
    nc = k.nc
    w = k.weights["l1_ffn"]
    W = lambda key: L1F.view(w, key)
    with ExitStack() as ctx:
        sb = lambda name, shape, dt=F32: k.sb("l1f_" + name, shape, dt, ctx)
        probs = sb("probs", [P, T, E1 + 2])
        slot = sb("slot", [P, T, E1 + 2])
        total = sb("total", [P, T, P])
        l1_ffn_route(k, W, probs, slot)
        l1_ffn_experts(k, W, probs, slot, total)
        act_part, shared = sb("act_part", [P, 2, N]), sb("shared", [P, 2, N])
        products(k, "l1f_sg", [(SCALAR, wide(k, W("sg")[:, c * P:(c + 1) * P], k.XT),
                                activated(k, act_part[:, c, :], ACT.Gelu)) for c in range(2)])

        def gated(c):
            return lambda v, out: nc.vector.tensor_tensor(shared[:, c, :], out, act_part[:, c, :], ALU.mult)
        products(k, "l1f_su", [(VECTOR, wide(k, W("su")[:, c * P:(c + 1) * P], k.XT), gated(c)) for c in range(2)])
        close_sublayer(k, "l1f_close", None, [W("sd")[:, c * P:(c + 1) * P] for c in range(2)], 2,
                       features_t=[shared[:, 0, :], shared[:, 1, :]], addend=total[:])


def l1_ffn_route(k, W, probs, slot):
    nc = k.nc
    with ExitStack() as ctx:
        sb = lambda name, shape: k.sb("l1r_" + name, shape, F32, ctx)
        logits_ps = k.ps("l1r_logits_ps", [P, T, E1], ctx)
        by_expert_ps = k.ps("l1r_by_expert_ps", [E1, N], ctx)
        slot_ps = k.ps("l1r_slot_ps", [P, T, E1], ctx)
        top, exps = sb("top", [P, T]), sb("exps", [P, T, E1])
        left, best, chosen, place = sb("left", [E1, N]), sb("best", [E1, 8]), sb("chosen", [E1, N]), sb("place", [E1, N])
        ready, shifted, exps_ready, probs_ready, turned_ready, places_ready, slots_ready = k.sems(
            "l1r", "ready shifted exps_ready probs_ready turned_ready places_ready slots_ready")
        full = [P, T, E1]
        with nc.Block() as block:

            @block.tensor
            def _(pe):
                for t in range(T):
                    mm = nc.tensor.matmul(logits_ps[:, t, :], k.XT[:, t * P:(t + 1) * P], W("gate"), start=True,
                                          stop=True)
                mm.then_inc(ready, 1)
                pe.wait_ge(probs_ready, 1)
                for t in range(T):
                    mm = nc.tensor.transpose(by_expert_ps[:, t * P:(t + 1) * P], exps[:, t, :], k.ident[:])
                mm.then_inc(turned_ready, 1)
                pe.wait_ge(places_ready, 1)
                for t in range(T):
                    mm = nc.tensor.transpose(slot_ps[:, t, :], place[:, t * P:(t + 1) * P], k.ident[0:E1, 0:E1])
                mm.then_inc(slots_ready, 1)

            @block.scalar
            def _(act):
                act.wait_ge(shifted, 1)
                nc.scalar.activation(exps[:], exps[:], ACT.Exp).then_inc(exps_ready, 1)

            @block.vector
            def _(v):
                link = k.vchain
                nc.vector.memset(probs[:, :, E1:], 0.0)
                nc.vector.memset(slot[:, :, E1:], -1.0)
                v.wait_ge(ready, 1)
                link(v, nc.vector.tensor_reduce(top[:], logits_ps[:], AX.X, ALU.max))
                nc.vector.tensor_tensor(exps[:], logits_ps[:], bc(top[:].unsqueeze(2), full), ALU.subtract)\
                    .then_inc(shifted, 1)
                v.wait_ge(exps_ready, 1)
                link(v, nc.vector.tensor_reduce(top[:], exps[:], AX.X, ALU.add))
                link(v, nc.vector.reciprocal(top[:], top[:]))
                nc.vector.tensor_tensor(exps[:], exps[:], bc(top[:].unsqueeze(2), full), ALU.mult)\
                    .then_inc(probs_ready, 1)
                v.wait_ge(probs_ready, 1)
                nc.vector.tensor_copy(probs[:, :, 0:E1], exps[:])
                v.wait_ge(turned_ready, 1)
                link(v, nc.vector.tensor_copy(left[:], by_expert_ps[:]))
                for _ in range(CAP // 8):
                    link(v, nc.vector.max(best[:], left[:]))
                    link(v, nc.vector.match_replace(left[:], best[:], left[:], -1.0))
                link(v, nc.vector.tensor_scalar(chosen[:], left[:], 0.0, None, ALU.is_lt))
                link(v, nc.vector.tensor_tensor_scan(place[:], chosen[:], chosen[:], 0.0, ALU.add, ALU.max))
                link(v, nc.vector.tensor_tensor(place[:], place[:], chosen[:], ALU.mult))
                nc.vector.tensor_scalar(place[:], place[:], 1.0, None, ALU.subtract).then_inc(places_ready, 1)
                v.wait_ge(slots_ready, 1)
                link(v, nc.vector.tensor_copy(slot[:, :, 0:E1], slot_ps[:]))


def l1_ffn_experts(k, W, probs, slot, total):
    nc = k.nc
    CH, PER = F1 // P, 2
    TURNS = E1 // PER
    with ExitStack() as ctx:
        sb = lambda name, shape: k.sb("l1e_" + name, shape, F32, ctx)
        ps = lambda name, shape: k.ps("l1e_" + name, shape, ctx)
        turned_ps, gathered_ps, gate_ps = ps("turned_ps", [P, N]), ps("gathered_ps", [P, BANK]), ps("gate_ps", [P, BANK])
        up_ps, out_ps, scattered_ps = ps("up_ps", [P, BANK]), ps("out_ps", [P, BANK]), ps("scattered_ps", [P, T, P])
        experts = sb("experts", [P, PER, 3 * F1])
        onehot = sb("onehot", [P, 2, T, P])
        onehot_t = sb("onehot_t", [P, 2, N])
        gathered, act_part, hidden = sb("gathered", [P, P]), sb("act_part", [P, F1]), sb("hidden", [P, F1])
        out, weighted = sb("out", [P, P]), sb("weighted", [P, T, P])
        (loaded0, loaded1, onehot_ready, turned_ready, turned_copied, gathered_ready, gathered_copied, up_ready,
         gelu_ready, hidden_ready, out_ready, out_copied, scattered_ready, scattered_used) = k.sems(
            "l1e", "loaded0 loaded1 onehot_ready turned_ready turned_copied gathered_ready gathered_copied up_ready "
            "gelu_ready hidden_ready out_ready out_copied scattered_ready scattered_used")
        loaded = (loaded0, loaded1)

        def gather(pe, e, buffer):
            pe.wait_ge(onehot_ready, e + 1)
            pe.wait_ge(gathered_copied, e + 1)
            for t in range(T):
                mm = nc.tensor.matmul(gathered_ps[:, 0:P], k.X[:, t, :], onehot[:, buffer, t, :], start=(t == 0),
                                      stop=(t == T - 1))
            mm.then_inc(gathered_ready, 1)
            pe.wait_ge(turned_copied, e + 1)
            for t in range(T):
                mm = nc.tensor.transpose(turned_ps[:, t * P:(t + 1) * P], onehot[:, buffer, t, :], k.ident[:])
            mm.then_inc(turned_ready, 1)

        def take_gathered(act, e, buffer, first=False):
            act.wait_ge(gathered_ready, e + 1)
            act.wait_ge(up_ready, e + 1)
            nc.scalar.copy(gathered[:], gathered_ps[:, 0:P]).then_inc(gathered_copied, 1)
            act.wait_ge(turned_ready, e + 1)
            if not first:
                act.wait_ge(scattered_ready, e)
            nc.scalar.copy(onehot_t[:, buffer, :], turned_ps[:]).then_inc(turned_copied, 1)

        def make_onehot(v, e, buffer):
            nc.vector.tensor_tensor(onehot[:, buffer], bc(W("slot_number").unsqueeze(1), [P, T, P]),
                                    bc(slot[:, :, bass.ds(e, 1)], [P, T, P]), ALU.is_equal).then_inc(onehot_ready, 1)

        with nc.Block() as block:

            @block.sync
            def _(sp):
                for j in range(PER):
                    sp.dma_start(experts[:, j, :], k.dram["l1_experts"][j]).then_inc(loaded[j], 16)
                with nc.sync.Fori(1, TURNS) as turn:
                    for j in range(PER):
                        sp.wait_ge(out_ready, turn * PER + j - PER + 1)
                        sp.dma_start(experts[:, j, :], k.dram["l1_experts"].rearrange("e p n -> (e p) n")
                                     [bass.ds((turn * PER + j) * P, P), :]).then_inc(loaded[j], 16)

            @block.tensor
            def _(pe):
                pe.sem_inc(up_ready, 1)
                pe.sem_inc(scattered_ready, 1)
                gather(pe, 0, 0)
                with nc.tensor.Fori(0, TURNS) as turn:
                    for j in range(PER):
                        e = turn * PER + j
                        pe.wait_ge(loaded[j], (turn + 1) * 16)
                        pe.wait_ge(gathered_copied, e + 2)
                        pe.wait_ge(hidden_ready, e + 1)
                        for at, first in ((gate_ps, 0), (up_ps, F1)):
                            for c in range(CH):
                                mm = nc.tensor.matmul(at[:, c * P:(c + 1) * P],
                                                      experts[:, j, first + c * P:first + (c + 1) * P], gathered[:],
                                                      start=True, stop=True)
                        mm.then_inc(up_ready, 1)
                        gather(pe, e + 1, 1 - j)
                        pe.wait_ge(hidden_ready, e + 2)
                        pe.wait_ge(out_copied, e + 1)
                        for c in range(CH):
                            mm = nc.tensor.matmul(out_ps[:, 0:P], hidden[:, c * P:(c + 1) * P],
                                                  experts[:, j, 2 * F1 + c * P:2 * F1 + (c + 1) * P],
                                                  start=(c == 0), stop=(c == CH - 1))
                        mm.then_inc(out_ready, 1)
                        pe.wait_ge(out_copied, e + 2)
                        pe.wait_ge(scattered_used, e + 1)
                        for t in range(T):
                            mm = nc.tensor.matmul(scattered_ps[:, t, :], onehot_t[:, j, t * P:(t + 1) * P], out[:],
                                                  start=True, stop=True)
                        mm.then_inc(scattered_ready, 1)

            @block.scalar
            def _(act):
                act.sem_inc(gathered_copied, 1)
                act.sem_inc(turned_copied, 1)
                act.sem_inc(out_copied, 1)
                take_gathered(act, 0, 0, first=True)
                with nc.scalar.Fori(0, TURNS) as turn:
                    for j in range(PER):
                        e = turn * PER + j
                        act.wait_ge(up_ready, e + 2)
                        act.wait_ge(hidden_ready, e + 1)
                        nc.scalar.activation(act_part[:], gate_ps[:], ACT.Gelu).then_inc(gelu_ready, 1)
                        take_gathered(act, e + 1, 1 - j)
                        act.wait_ge(out_ready, e + 1)
                        act.wait_ge(scattered_ready, e + 1)
                        nc.scalar.copy(out[:], out_ps[:, 0:P]).then_inc(out_copied, 1)

            @block.vector
            def _(v):
                link = k.vchain
                v.sem_inc(hidden_ready, 1)
                v.sem_inc(scattered_used, 1)
                link(v, nc.vector.memset(total[:], 0.0))
                make_onehot(v, 0, 0)
                make_onehot(v, 1, 1)
                with nc.vector.Fori(0, TURNS) as turn:
                    link.enter(turn, PER)
                    for j in range(PER):
                        e = turn * PER + j
                        v.wait_ge(gelu_ready, e + 1)
                        nc.vector.tensor_tensor(hidden[:], act_part[:], up_ps[:], ALU.mult).then_inc(hidden_ready, 1)
                        v.wait_ge(turned_ready, e + 1)
                        make_onehot(v, e + 2, j)
                        v.wait_ge(scattered_ready, e + 2)
                        nc.vector.tensor_tensor(weighted[:], scattered_ps[:], bc(probs[:, :, bass.ds(e, 1)], [P, T, P]),
                                                ALU.mult).then_inc(scattered_used, 1)
                        v.wait_ge(scattered_used, e + 2)
                        link(v, nc.vector.tensor_tensor(total[:], total[:], weighted[:], ALU.add))
                    link.leave(TURNS)



L2A = Pack("l2_attn")
for _key, _width in (("wqkv", 3 * P), ("wout", P)):
    L2A.put(_key, _width)


def l2_attn_layout(i):
    return L2A.build({"wqkv": np.asarray(i["L2_attn_W_qkv"]).T, "wout": np.asarray(i["L2_attn_W_out"]).T})


def l2_attn(k):
    nc = k.nc
    w = k.weights["l2_attn"]
    W = lambda key: L2A.view(w, key)
    with ExitStack() as ctx:
        sb = lambda name, shape, dt=F32: k.sb("l2a_" + name, shape, dt, ctx)
        q, q_t, k_t, values = sb("q", [P, T, P]), sb("q_t", [P, N]), sb("k_t", [P, N]), sb("values", [P, T, P])
        running, queries, heads_out = sb("running", [P, N]), sb("queries", [P, 4, N]), sb("heads_out", [P, T, P])
        top, ktop = sb("top", [P, T * HX]), sb("ktop", [P, B])
        seen = sb("seen", [P, S])
        products(k, "l2a_proj", [
            (VECTOR, wide(k, W("wqkv")[:, P:2 * P], k.XT), lambda v, out: nc.vector.tensor_copy(k_t[:], out)),
            (SCALAR, by_tile(k, k.XT, W("wqkv")[:, 0:P], P),
             lambda act, out: nc.scalar.copy(q[:].rearrange("p t n -> p (t n)"), out)),
            (SCALAR, by_tile(k, k.XT, W("wqkv")[:, 2 * P:3 * P], P),
             lambda act, out: nc.scalar.copy(values[:].rearrange("p t n -> p (t n)"), out)),
        ])
        with ExitStack() as inner:
            q_ps = k.ps("l2a_q_ps", [P, N], inner)
            q_shifted, q_exp, k_shifted, k_exp, q_soft, q_turned = k.sems(
                "l2a", "q_shifted q_exp k_shifted k_exp q_soft q_turned")
            heads = q[:].rearrange("p t (h d) -> p (t h) d", h=HX)
            with nc.Block() as block:

                @block.vector
                def _(v):
                    link = k.vchain
                    link(v, nc.vector.tensor_reduce(top[:], heads, AX.X, ALU.max))
                    nc.vector.tensor_tensor(heads, heads, bc(top[:].unsqueeze(2), [P, T * HX, DX]), ALU.subtract)\
                        .then_inc(q_shifted, 1)
                    batches = k_t[:].rearrange("p (b s) -> p b s", b=B)
                    link(v, nc.vector.tensor_reduce(ktop[:], batches, AX.X, ALU.max))
                    nc.vector.tensor_tensor(batches, batches, bc(ktop[:].unsqueeze(2), [P, B, S]), ALU.subtract)\
                        .then_inc(k_shifted, 1)
                    v.wait_ge(q_exp, 1)
                    link(v, nc.vector.tensor_reduce(top[:], heads, AX.X, ALU.add))
                    link(v, nc.vector.reciprocal(top[:], top[:]))
                    link(v, nc.vector.tensor_scalar(top[:], top[:], DX ** -0.5, None, ALU.mult))
                    nc.vector.tensor_tensor(heads, heads, bc(top[:].unsqueeze(2), [P, T * HX, DX]), ALU.mult)\
                        .then_inc(q_soft, 1)
                    v.wait_ge(k_exp, 1)
                    for b in range(B):
                        one = slice(b * S, (b + 1) * S)
                        link(v, nc.vector.tensor_tensor_scan(running[:, one], k_t[:, one], k_t[:, one], 0.0, ALU.add,
                                                             ALU.max))
                    link(v, nc.vector.tensor_scalar(running[:], running[:], 1e-9, None, ALU.add))
                    link(v, nc.vector.reciprocal(running[:], running[:]))
                    v.wait_ge(q_turned, 1)
                    link(v, nc.vector.tensor_tensor(q_t[:], q_ps[:], running[:], ALU.mult))
                    for j in range(4):
                        link(v, nc.vector.tensor_scalar(queries[:, j, :], q_t[:], k.own_of_four[:, j:j + 1], None,
                                                        ALU.mult))

                @block.scalar
                def _(act):
                    act.wait_ge(q_shifted, 1)
                    nc.scalar.activation(q[:], q[:], ACT.Exp).then_inc(q_exp, 1)
                    act.wait_ge(k_shifted, 1)
                    nc.scalar.activation(k_t[:], k_t[:], ACT.Exp).then_inc(k_exp, 1)

                @block.tensor
                def _(pe):
                    pe.wait_ge(q_soft, 1)
                    for t in range(T):
                        mm = nc.tensor.transpose(q_ps[:, t * P:(t + 1) * P], q[:, t, :], k.ident[:])
                    mm.then_inc(q_turned, 1)

                @block.gpsimd
                def _(g):
                    nc.gpsimd.memset(seen[:, P:S], 1.0)
                    k.gchain(g, nc.gpsimd.memset(seen[:, 0:P], 1.0))
                    nc.gpsimd.affine_select(out=seen[:, 0:P], in_=seen[:, 0:P], compare_op=ALU.is_ge, fill=0.0,
                                            base=0, pattern=[[1, P]], channel_multiplier=-1)

        with ExitStack() as inner:
            first_ps = k.ps("l2a_first_ps", [P, 2, 4, S], inner)
            second_ps = k.ps("l2a_second_ps", [P, 2, 4, P], inner)
            out_ps = k.ps("l2a_out_ps", [P, 2, BANK], inner)
            first = k.sb("l2a_first", [P, 2, 4, S], F32, inner)
            second = k.sb("l2a_second", [P, 2, 4, P], F32, inner)
            ready, masked, out_ready, out_used = k.sems("l2u", "ready masked out_ready out_used")
            units = [(b, g) for b in range(B) for g in range(4)]
            out_of = lambda n: out_ps[:, n % 2, 0:TB * 4 * DX]
            with nc.Block() as block:

                @block.tensor
                def _(pe):
                    def weights(n):
                        b, g = units[n]
                        rows = slice(32 * g, 32 * g + 32)
                        if n >= 2:
                            pe.wait_ge(masked, n - 1)
                        for c in range(2):
                            nc.tensor.matmul(first_ps[:, n % 2, 2 * c:2 * c + 2, :], k_t[rows, b * S:b * S + P],
                                             queries[rows, 2 * c:2 * c + 2, b * S:(b + 1) * S], start=True, stop=True)
                        nc.tensor.matmul(second_ps[:, n % 2], k_t[rows, b * S + P:(b + 1) * S],
                                         queries[rows, :, b * S + P:(b + 1) * S], start=True, stop=True)\
                            .then_inc(ready, 1)
                    weights(0)
                    for n, (b, g) in enumerate(units):
                        if n + 1 < len(units):
                            weights(n + 1)
                        pe.wait_ge(masked, n + 1)
                        if n >= 2:
                            pe.wait_ge(out_used, n - 1)
                        for j in range(4):
                            v_of = lambda c: values[:, TB * b + c, (4 * g + j) * DX:(4 * g + j + 1) * DX]
                            at = lambda i: out_of(n)[:, (i * 4 + j) * DX:(i * 4 + j + 1) * DX]
                            nc.tensor.matmul(at(0), first[:, n % 2, j, 0:P], v_of(0), start=True, stop=True)
                            nc.tensor.matmul(at(1), first[:, n % 2, j, P:S], v_of(0), start=True, stop=False)
                            mm = nc.tensor.matmul(at(1), second[:, n % 2, j, :], v_of(1), start=False, stop=True)
                        mm.then_inc(out_ready, 1)

                @block.vector
                def _(v):
                    for n in range(len(units)):
                        v.wait_ge(ready, n + 1)
                        if n >= 2:
                            v.wait_ge(out_ready, n - 1)
                        nc.vector.tensor_tensor(first[:, n % 2], first_ps[:, n % 2],
                                                bc(seen[:].unsqueeze(1), [P, 4, S]), ALU.mult)
                        nc.vector.tensor_tensor(second[:, n % 2], second_ps[:, n % 2],
                                                bc(seen[:, 0:P].unsqueeze(1), [P, 4, P]), ALU.mult).then_inc(masked, 1)

                @block.scalar
                def _(act):
                    for n, (b, g) in enumerate(units):
                        act.wait_ge(out_ready, n + 1)
                        nc.scalar.copy(heads_out[:, TB * b:TB * b + TB, 32 * g:32 * g + 32],
                                       out_of(n).rearrange("p (i c) -> p i c", i=TB)).then_inc(out_used, 1)
        close_sublayer(k, "l2a_close", heads_out[:], [W("wout")], 1)



L2X = Pack("l2_xattn")
for _key, _width in (("w1", 1), ("w2", 1), ("w3", 1), ("b_sim", 1), ("w_qv", 4 * P), ("b_qv", P)):
    L2X.put(_key, _width)


def l2_xattn_layout(i):
    g = lambda key: np.asarray(i["L2_xattn_" + key])
    w = g("w_sim").reshape(3, P)
    return L2X.build({"w1": column(w[0]), "w2": column(w[1]), "w3": column(w[2]), "b_sim": on_all(g("b_sim")),
                      "w_qv": tile_rows(g("W_qv")), "b_qv": on_all(g("b_qv"))})


def l2_xattn(k):
    nc = k.nc
    w = k.weights["l2_xattn"]
    W = lambda key: L2X.view(w, key)
    with ExitStack() as ctx:
        sb = lambda name, shape, dt=F32: k.sb("l2x_" + name, shape, dt, ctx)
        keys = sb("keys", [P, B * SC])
        w2_all = sb("w2_all", [P, P])
        sim, weights_t = sb("sim", [P, T, SC]), sb("weights_t", [SC, N])
        top, total = sb("top", [P, T]), sb("total", [P, T])
        tops_t, top8, tops_row, tops_pair = sb("tops_t", [T, P]), sb("top8", [T, 1]), sb("tops_row", [1, T]), sb("tops_pair", [1, B, TB])
        back, pooled, share = sb("back", [P, T]), sb("pooled", [P, B]), sb("share", [P, B])
        attended, product_t, pooled_t = sb("attended", [P, N]), sb("product_t", [P, N]), sb("pooled_t", [P, N])
        psum = ctx.enter_context(ExitStack())
        sim_ps = k.ps("l2x_sim_ps", [P, T, SC], psum)
        turned_ps = k.ps("l2x_turned_ps", [SC, N], psum)
        attended_ps = k.ps("l2x_attended_ps", [P, N], psum)
        small_ps = k.ps("l2x_small_ps", [P, 3, BANK], psum)
        (keys_ready, sim_ready, sim_taken, shifted, exp_ready, soft_ready, turned_ready, turned_copied,
         attended_ready, tops_turned, tops_reduced, row_ready, pairs_ready, spread_ready, back_shifted, back_exp,
         pooled_ready) = k.sems(
            "l2x", "keys_ready sim_ready sim_taken shifted exp_ready soft_ready turned_ready turned_copied "
            "attended_ready tops_turned tops_reduced row_ready pairs_ready spread_ready back_shifted back_exp "
            "pooled_ready")
        full = [P, T, SC]
        with nc.Block() as block:

            @block.tensor
            def _(pe):
                pe.wait_ge(keys_ready, 1)
                for t in range(T):
                    b = t // TB
                    nc.tensor.matmul(sim_ps[:, t, :], k.XT[:, t * P:(t + 1) * P], keys[:, b * SC:(b + 1) * SC],
                                     start=True, stop=False)
                    mm = nc.tensor.matmul(sim_ps[:, t, :], w2_all[:], k.ctx_t[:, b * SC:(b + 1) * SC], start=False,
                                          stop=True)
                mm.then_inc(sim_ready, 1)
                pe.wait_ge(sim_taken, 1)
                nc.tensor.transpose(small_ps[0:T, 0, 0:P], top[:], k.ident[:]).then_inc(tops_turned, 1)
                pe.wait_ge(tops_reduced, 1)
                nc.tensor.transpose(small_ps[0:1, 1, 0:T], top8[:], k.ident[0:T, 0:T]).then_inc(row_ready, 1)
                pe.wait_ge(pairs_ready, 1)
                nc.tensor.matmul(small_ps[:, 2, 0:T], k.ones[0:1, :], tops_pair[:].rearrange("p b i -> p (b i)"),
                                 start=True, stop=True).then_inc(spread_ready, 1)
                pe.wait_ge(soft_ready, 1)
                for t in range(T):
                    mm = nc.tensor.transpose(turned_ps[:, t * P:(t + 1) * P], sim[:, t, :], k.ident[:])
                mm.then_inc(turned_ready, 1)
                pe.wait_ge(turned_copied, 1)
                for b in range(B):
                    mm = nc.tensor.matmul(attended_ps[:, b * S:(b + 1) * S], k.ctx_rows[:, b, :],
                                          weights_t[:, b * S:(b + 1) * S], start=True, stop=True)
                mm.then_inc(attended_ready, 1)
                pe.wait_ge(back_exp, 1)
                for b in range(B):
                    for i in range(TB):
                        nc.tensor.matmul(small_ps[:, 0, b:b + 1], k.X[:, TB * b + i, :],
                                         back[:, TB * b + i:TB * b + i + 1], start=(i == 0), stop=(i == 1))
                    for i in range(TB):
                        mm = nc.tensor.matmul(small_ps[:, 1, b:b + 1], k.ones[:],
                                              back[:, TB * b + i:TB * b + i + 1], start=(i == 0), stop=(i == 1))
                mm.then_inc(pooled_ready, 1)

            @block.scalar
            def _(act):
                act.wait_ge(shifted, 1)
                nc.scalar.activation(sim[:], sim[:], ACT.Exp).then_inc(exp_ready, 1)
                act.wait_ge(back_shifted, 1)
                nc.scalar.activation(back[:], back[:], ACT.Exp).then_inc(back_exp, 1)
                act.wait_ge(turned_ready, 1)
                nc.scalar.copy(weights_t[:], turned_ps[:]).then_inc(turned_copied, 1)

            @block.vector
            def _(v):
                link = k.vchain
                link(v, nc.vector.tensor_copy(w2_all[:], bc(W("w2"), [P, P])))
                nc.vector.tensor_scalar(keys[:], k.ctx_t[:], W("w3"), W("w1"), ALU.mult, ALU.add)\
                    .then_inc(keys_ready, 1)
                v.wait_ge(sim_ready, 1)
                link(v, nc.vector.tensor_scalar(sim[:], sim_ps[:], W("b_sim"), None, ALU.add))
                nc.vector.tensor_reduce(top[:], sim[:], AX.X, ALU.max).then_inc(sim_taken, 1)
                v.wait_ge(sim_taken, 1)
                nc.vector.tensor_tensor(sim[:], sim[:], bc(top[:].unsqueeze(2), full), ALU.subtract)\
                    .then_inc(shifted, 1)
                v.wait_ge(tops_turned, 1)
                nc.vector.tensor_reduce(top8[:], small_ps[0:T, 0, 0:P], AX.X, ALU.max).then_inc(tops_reduced, 1)
                v.wait_ge(row_ready, 1)
                row = small_ps[0:1, 1, 0:T].rearrange("p (b i) -> p b i", b=B)
                link(v, nc.vector.tensor_copy(tops_row[:], small_ps[0:1, 1, 0:T]))
                pairs = tops_row[:].rearrange("p (b i) -> p b i", b=B)
                nc.vector.tensor_tensor(tops_pair[:], bc(pairs[:, :, 0:1], [1, B, TB]), bc(pairs[:, :, 1:2], [1, B, TB]),
                                        ALU.max).then_inc(pairs_ready, 1)
                v.wait_ge(spread_ready, 1)
                nc.vector.tensor_tensor(back[:], top[:], small_ps[:, 2, 0:T], ALU.subtract).then_inc(back_shifted, 1)
                v.wait_ge(exp_ready, 1)
                link(v, nc.vector.tensor_reduce(total[:], sim[:], AX.X, ALU.add))
                link(v, nc.vector.reciprocal(total[:], total[:]))
                nc.vector.tensor_tensor(sim[:], sim[:], bc(total[:].unsqueeze(2), full), ALU.mult)\
                    .then_inc(soft_ready, 1)
                v.wait_ge(pooled_ready, 1)
                link(v, nc.vector.reciprocal(share[:], small_ps[:, 1, 0:B]))
                link(v, nc.vector.tensor_tensor(pooled[:], small_ps[:, 0, 0:B], share[:], ALU.mult))
                link(v, nc.vector.tensor_tensor(pooled_t[:].rearrange("p (b s) -> p b s", b=B),
                                                k.XT[:].rearrange("p (b s) -> p b s", b=B),
                                                bc(pooled[:].unsqueeze(2), [P, B, S]), ALU.mult))
                v.wait_ge(attended_ready, 1)
                link(v, nc.vector.tensor_copy(attended[:], attended_ps[:]))
                link(v, nc.vector.tensor_tensor(product_t[:], k.XT[:], attended[:], ALU.mult))
        features = [k.XT, attended, product_t, pooled_t]
        psum.close()
        close_sublayer(k, "l2x_close", None, [W("w_qv")[:, c * P:(c + 1) * P] for c in range(4)], 4, bias=W("b_qv"),
                       features_t=features)



SLOTS, F2 = 8 * 64, 4 * P
TS = SLOTS // P
L2F = Pack("l2_ffn")
for _key, _width in (("w1", F2), ("w2", F2), ("slots", TS * P), ("gain_x", P), ("gain_slot", P)):
    L2F.put(_key, _width)


def l2_ffn_layout(i):
    g = lambda key: np.asarray(i["L2_ffn_" + key])
    return L2F.build({"w1": g("w1"), "w2": tile_rows(g("w2")), "slots": tile_rows(g("slot_embeds").reshape(SLOTS, P)),
                      "gain_x": on_all(g("gamma_x")), "gain_slot": on_all(g("gamma_slot"))})


def l2_ffn(k):
    nc = k.nc
    w = k.weights["l2_ffn"]
    W = lambda key: L2F.view(w, key)
    TA = T + TS
    with ExitStack() as ctx:
        sb = lambda name, shape, dt=F32: k.sb("l2f_" + name, shape, dt, ctx)
        rows = sb("rows", [P, TA, P + 1])
        xn_t, slots_t = sb("xn_t", [P, N]), sb("slots_t", [P, SLOTS])
        hidden_in, processed = sb("hidden_in", [P, B * TS, P]), sb("processed", [P, B * TS, P + 1])
        hidden_in_t, hidden = sb("hidden_in_t", [P, B * SLOTS]), sb("hidden", [P, F2 // P, B * SLOTS])
        combined = sb("combined", [P, T, P])
        with ExitStack() as inner:
            squares = k.sb("l2f_squares", [P, TA, P], F32, inner)
            norms, half = k.sb("l2f_norms", [P, TA], F32, inner), k.sb("l2f_half", [P, TA], F32, inner)
            summed, rooted = k.sems("l2f", "summed rooted")
            with nc.Block() as block:

                @block.gpsimd
                def _(g):
                    nc.gpsimd.memset(rows[:, :, P:P + 1], 1.0)
                    nc.gpsimd.memset(processed[:, :, P:P + 1], 1.0)
                    k.gchain(g, nc.gpsimd.memset(half[:], 0.5))
                    g.wait_ge(summed, 1)
                    nc.gpsimd.tensor_tensor(norms[:], norms[:], half[:], ALU.pow).then_inc(rooted, 1)

                @block.vector
                def _(v):
                    link = k.vchain
                    slots = W("slots").rearrange("p (t n) -> p t n", t=TS)
                    nc.vector.tensor_tensor(squares[:, 0:T, :], k.X[:], k.X[:], ALU.mult)
                    link(v, nc.vector.tensor_tensor(squares[:, T:TA, :], slots, slots, ALU.mult))
                    nc.vector.tensor_reduce(norms[:], squares[:], AX.X, ALU.add).then_inc(summed, 1)
                    v.wait_ge(rooted, 1)
                    link(v, nc.vector.tensor_scalar(norms[:], norms[:], 1e-12, None, ALU.max))
                    link(v, nc.vector.reciprocal(norms[:], norms[:]))
                    link(v, nc.vector.tensor_scalar(norms[:], norms[:], float(P) ** 0.5, None, ALU.mult))
                    for at, src, gain in ((slice(0, T), k.X[:], "gain_x"), (slice(T, TA), slots, "gain_slot")):
                        shape = [P, at.stop - at.start, P]
                        link(v, nc.vector.tensor_tensor(squares[:, at, :], src, bc(norms[:, at].unsqueeze(2), shape),
                                                        ALU.mult))
                        link(v, nc.vector.tensor_tensor(rows[:, at, 0:P], squares[:, at, :],
                                                        bc(W(gain).unsqueeze(1), shape), ALU.mult))

        def turn(source, first, count, width=P):
            def issue(pe, out):
                for t in range(count):
                    mm = nc.tensor.transpose(out[:, t * P:(t + 1) * P], source[:, first + t, 0:width], k.ident[:])
                return mm
            return issue
        copy = lambda dst, cols=N: lambda act, out: nc.scalar.copy(dst, out[:, 0:cols])
        products(k, "l2f_turn", [(SCALAR, turn(rows, 0, T), copy(xn_t[:])),
                                 (SCALAR, turn(rows, T, TS), copy(slots_t[:], SLOTS))])

        def dispatch(b, pair):
            def score(out):
                for o in range(2):
                    mm = nc.tensor.matmul(out[:, o, 0:S], slots_t[:, (2 * pair + o) * P:(2 * pair + o + 1) * P],
                                          xn_t[:, b * S:(b + 1) * S], start=True, stop=True)
                return mm

            def product(out, probs_t):
                for o in range(2):
                    for c in range(TB):
                        x = o * TB + c
                        mm = nc.tensor.matmul(out[:, o * (P + 1):(o + 1) * (P + 1)], probs_t[:, x * P:(x + 1) * P],
                                              rows[:, TB * b + c, :], start=(c == 0), stop=(c == TB - 1))
                return mm
            first = b * TS + 2 * pair
            return 2 * S, 2, score, product, hidden_in[:, first:first + 2, :], None

        attention(k, "l2f_dispatch", [dispatch(b, pair) for b in range(B) for pair in range(TS // 2)], 1.0)
        products(k, "l2f_turn2", [(SCALAR, turn(hidden_in, 8 * c, 8), copy(hidden_in_t[:, c * N:(c + 1) * N]))
                                  for c in range(2)])
        products(k, "l2f_up", [(SCALAR, wide(k, W("w1")[:, f * P:(f + 1) * P], hidden_in_t[:, c * N:(c + 1) * N]),
                                activated(k, hidden[:, f, c * N:(c + 1) * N], ACT.Gelu))
                               for c in range(2) for f in range(F2 // P)])

        def down(c):
            def issue(pe, out):
                for t in range(8):
                    at = (8 * c + t) * P
                    for f in range(F2 // P):
                        mm = nc.tensor.matmul(out[:, t * P:(t + 1) * P], hidden[:, f, at:at + P],
                                              W("w2")[:, f * P:(f + 1) * P], start=(f == 0), stop=(f == F2 // P - 1))
                return mm
            return issue
        products(k, "l2f_down", [(VECTOR, down(c), lambda v, out, c=c: nc.vector.tensor_copy(
            processed[:, 8 * c:8 * c + 8, 0:P], out.rearrange("p (t n) -> p t n", n=P))) for c in range(2)])

        def combine(b):
            def score(out):
                for o in range(TB):
                    t = TB * b + o
                    mm = nc.tensor.matmul(out[:, o, :], xn_t[:, t * P:(t + 1) * P], slots_t[:], start=True, stop=True)
                return mm

            def product(out, probs_t):
                for o in range(TB):
                    for c in range(TS):
                        x = o * TS + c
                        mm = nc.tensor.matmul(out[:, o * (P + 1):(o + 1) * (P + 1)], probs_t[:, x * P:(x + 1) * P],
                                              processed[:, b * TS + c, :], start=(c == 0), stop=(c == TS - 1))
                return mm
            return 2 * BANK, 2, score, product, combined[:, TB * b:TB * b + TB, :], None

        attention(k, "l2f_combine", [combine(b) for b in range(B)], 1.0)
        norm_and_turn(k, "l2f_out", k.X[:], k.X[:], k.XT[:], addends=(combined[:],))



L3A = Pack("l3_attn")
for _key, _width in (("wq", P), ("wk", P), ("wv", P), ("wo", P), ("bo", P), ("alpha", 1), ("temperature", 1),
                     ("gamma", P), ("beta", P), ("other_rows", DX * DX)):
    L3A.put(_key, _width)


def l3_attn_layout(i):
    g = lambda key: np.asarray(i["L3_attn_" + key])
    return L3A.build({"wq": g("Wq").T, "wk": g("Wk").T, "wv": g("Wv").T, "wo": g("Wo").T, "bo": on_all(g("bo")),
                      "alpha": on_all(g("alpha")), "temperature": on_all(g("temperature")), "gamma": on_all(g("gamma")),
                      "beta": on_all(g("beta")),
                      "other_rows": np.broadcast_to(1.0 - np.eye(DX).reshape(1, -1), (P, DX * DX))})


def l3_attn(k):
    nc = k.nc
    w = k.weights["l3_attn"]
    W = lambda key: L3A.view(w, key)
    M = B * HX
    with ExitStack() as ctx:
        sb = lambda name, shape, dt=F32: k.sb("l3a_" + name, shape, dt, ctx)
        x_in, inner, inner_t = sb("x_in", [P, T, P]), sb("inner", [P, T, P]), sb("inner_t", [P, N])
        q_t, kv, out_t = sb("q_t", [P, N]), sb("kv", [P, T, 2 * P]), sb("out_t", [P, N])
        products(k, "l3a_proj", [
            (SCALAR, by_tile(k, k.XT, W("wk"), P), lambda act, out: nc.scalar.copy(
                kv[:, :, 0:P], out.rearrange("p (t n) -> p t n", n=P))),
            (VECTOR, by_tile(k, k.XT, W("wv"), P), lambda v, out: nc.vector.tensor_copy(
                kv[:, :, P:2 * P], out.rearrange("p (t n) -> p t n", n=P))),
            (SCALAR, wide(k, W("wq"), k.XT), activated(k, q_t[:])),
            ])
        with ExitStack() as att:
            psum = k.ps("l3a_gram_ps", [P, B, 2 * P], att)
            out_ps = k.ps("l3a_out_ps", [P, N], att)
            tmp = k.sb("l3a_tmp", [P, 2 * B, HX, DX], F32, att)
            own = k.sb("l3a_own", [P, B, 2, DX], F32, att)
            system = k.sb("l3a_system", [M, DX, 2 * DX], F32, att)
            row = k.sb("l3a_row", [M, 2 * DX], F32, att)
            factor, pivot = k.sb("l3a_factor", [M, DX], F32, att), k.sb("l3a_pivot", [M, 1], F32, att)
            outer = k.sb("l3a_outer", [M, DX, 2 * DX], F32, att)
            solved, top = k.sb("l3a_solved", [M, DX, DX], F32, att), k.sb("l3a_top", [M, DX], F32, att)
            maps = k.sb("l3a_maps", [P, B, DX], F32, att)
            maps_wide = k.sb("l3a_maps_wide", [P, B, HX, DX], F32, att)
            gram_dram = nc.dram_tensor("l3a_gram", (P, B * 2 * DX), F32, kind="Internal").ap()
            maps_dram = nc.dram_tensor("l3a_maps_dram", (M, DX * DX), F32, kind="Internal").ap()
            (gram_ready, own_ready, gram_stored, gram_loaded, shifted, exp_ready, solved_ready, maps_stored,
             maps_loaded, maps_ready, out_ready) = k.sems(
                "l3a", "gram_ready own_ready gram_stored gram_loaded shifted exp_ready solved_ready maps_stored "
                "maps_loaded maps_ready out_ready")
            with nc.Block() as block:

                @block.tensor
                def _(pe):
                    for b in range(B):
                        for i in range(TB):
                            mm = nc.tensor.matmul(psum[:, b, :], kv[:, TB * b + i, 0:P], kv[:, TB * b + i, :],
                                                  start=(i == 0), stop=(i == TB - 1))
                    mm.then_inc(gram_ready, 1)
                    pe.wait_ge(maps_ready, 1)
                    for b in range(B):
                        mm = nc.tensor.matmul(out_ps[:, b * S:(b + 1) * S], maps_wide[:, b].rearrange("p h e -> p (h e)"),
                                              q_t[:, b * S:(b + 1) * S], start=True, stop=True)
                    mm.then_inc(out_ready, 1)

                @block.scalar
                def _(act):
                    act.wait_ge(shifted, 1)
                    nc.scalar.activation(solved[:], solved[:], ACT.Exp).then_inc(exp_ready, 1)
                    act.wait_ge(out_ready, 1)
                    nc.scalar.copy(out_t[:], out_ps[:])

                @block.sync
                def _(sp):
                    sp.wait_ge(own_ready, 1)
                    sp.dma_start(gram_dram, own[:].rearrange("p b s e -> p (b s e)")).then_inc(gram_stored, 16)
                    sp.wait_ge(gram_stored, 16)
                    for b in range(B):
                        sp.dma_start(system[b * HX:(b + 1) * HX],
                                     gram_dram.rearrange("(h d) (b e) -> b h d e", d=DX, b=B)[b]).then_inc(gram_loaded, 16)
                    sp.wait_ge(solved_ready, 1)
                    sp.dma_start(maps_dram, solved[:].rearrange("m d e -> m (d e)")).then_inc(maps_stored, 16)
                    sp.wait_ge(maps_stored, 16)
                    for b in range(B):
                        sp.dma_start(maps[:, b, :], maps_dram[b * HX:(b + 1) * HX, :]
                                     .rearrange("h (d e) -> (h d) e", d=DX)).then_inc(maps_loaded, 16)

                @block.vector
                def _(v):
                    link = k.vchain
                    nc.vector.tensor_copy(x_in[:], k.X[:])
                    v.wait_ge(gram_ready, 1)
                    link(v, nc.vector.tensor_tensor(
                        tmp[:], psum[:].rearrange("p b (s h e) -> p (b s) h e", s=2, h=HX),
                        bc(k.own_head.unsqueeze(1).unsqueeze(3), [P, 2 * B, HX, DX]), ALU.mult))
                    nc.vector.tensor_reduce(own[:].rearrange("p b s e -> p (b s) e"),
                                            tmp[:].rearrange("p x h e -> p x e h"), AX.X, ALU.add)\
                        .then_inc(own_ready, 1)
                    v.wait_ge(gram_loaded, 16 * B)
                    flat = system[:].rearrange("m d e -> m (d e)")
                    diagonal = flat[:, 0:DX * 2 * DX:2 * DX + 1]
                    link(v, nc.vector.tensor_scalar(diagonal, diagonal, W("alpha")[0:M], None, ALU.add))
                    others = W("other_rows").rearrange("p (a b) -> p a b", a=DX)[0:M]
                    for p in range(DX):
                        link(v, nc.vector.reciprocal(pivot[:], system[:, p, p:p + 1]))
                        link(v, nc.vector.tensor_scalar(row[:], system[:, p, :], pivot[:], None, ALU.mult))
                        link(v, nc.vector.tensor_tensor(factor[:], system[:, :, p], others[:, p, :], ALU.mult))
                        link(v, nc.vector.tensor_tensor(outer[:], bc(factor[:].unsqueeze(2), [M, DX, 2 * DX]),
                                                        bc(row[:].unsqueeze(1), [M, DX, 2 * DX]), ALU.mult))
                        link(v, nc.vector.tensor_tensor(system[:], system[:], outer[:], ALU.subtract))
                        link(v, nc.vector.tensor_copy(system[:, p, :], row[:]))
                    link(v, nc.vector.reciprocal(pivot[:], W("temperature")[0:M]))
                    link(v, nc.vector.tensor_scalar(solved[:], system[:, :, DX:2 * DX], pivot[:], None, ALU.mult))
                    by_e = solved[:].rearrange("m d e -> m e d")
                    spread = lambda: bc(top[:].unsqueeze(1), [M, DX, DX])
                    link(v, nc.vector.tensor_reduce(top[:], by_e, AX.X, ALU.max))
                    nc.vector.tensor_tensor(solved[:], solved[:], spread(), ALU.subtract).then_inc(shifted, 1)
                    v.wait_ge(exp_ready, 1)
                    link(v, nc.vector.tensor_reduce(top[:], by_e, AX.X, ALU.add))
                    link(v, nc.vector.reciprocal(top[:], top[:]))
                    nc.vector.tensor_tensor(solved[:], solved[:], spread(), ALU.mult).then_inc(solved_ready, 1)
                    v.wait_ge(maps_loaded, 16 * B)
                    for b in range(B):
                        ins = nc.vector.tensor_tensor(maps_wide[:, b], bc(maps[:, b, :].unsqueeze(1), [P, HX, DX]),
                                                      bc(k.own_head.unsqueeze(2), [P, HX, DX]), ALU.mult)
                    ins.then_inc(maps_ready, 1)
        close_sublayer(k, "l3a_close", None, [W("wo")], 1, bias=W("bo"), features_t=[out_t],
                       to=(inner[:], inner_t[:]), gain=W("gamma"), shift=W("beta"))
        norm_and_turn(k, "l3a_out", inner[:], k.X[:], k.XT[:], addends=(x_in[:],))



H3, D3 = 16, 64
PAIRS = H3 * D3 // P
L3X = Pack("l3_xattn")
for _key, _width in (("wq", H3 * D3), ("wk", H3 * D3), ("wv", H3 * D3), ("wo", PAIRS * P), ("bq", PAIRS),
                     ("bk", PAIRS), ("bv", H3 * D3), ("bo", P)):
    L3X.put(_key, _width)


def l3_xattn_layout(i):
    g = lambda key: np.asarray(i["L3_xattn_" + key])
    wide_of = lambda x: g(x).transpose(1, 0, 2).reshape(P, H3 * D3)
    return L3X.build({"wq": wide_of("Wq"), "wk": wide_of("Wk"), "wv": wide_of("Wv"), "wo": tile_rows(g("Wo")),
                      "bq": g("bq").reshape(PAIRS, P).T, "bk": g("bk").reshape(PAIRS, P).T,
                      "bv": on_all(g("bv").reshape(-1)), "bo": on_all(g("bo"))})


def l3_xattn(k):
    nc = k.nc
    w = k.weights["l3_xattn"]
    W = lambda key: L3X.view(w, key)
    with ExitStack() as ctx:
        sb = lambda name, shape, dt=F32: k.sb("l3x_" + name, shape, dt, ctx)
        heads_out = sb("heads_out", [P, T, H3 * D3])
        with ExitStack() as att:
            sb = lambda name, shape, dt=F32: k.sb("l3x_" + name, shape, dt, att)
            q_t = sb("q_t", [P, PAIRS, N])
            keys = sb("keys", [P, PAIRS, B, 2, SC])
            values = sb("values", [P, B, H3, D3])
            v_tmp = sb("v_tmp", [P, H3, D3])
            keep, add = sb("keep", [P, T, SC]), sb("add", [P, T, SC])
            with nc.Block() as block:

                @block.gpsimd
                def _(g):
                    nc.gpsimd.memset(keys[:], 0.0)

                @block.vector
                def _(v):
                    k.vchain(v, nc.vector.tensor_scalar(keep[:], k.mask3[:], 0.0, None, ALU.is_equal))
                    nc.vector.tensor_scalar(add[:], keep[:], 1.0, 1e9 * D3 ** 0.5, ALU.subtract, ALU.mult)

            def four_keys(c):
                def issue(pe, out):
                    for j in range(4):
                        x = 4 * c + j
                        mm = nc.tensor.matmul(out[:, j * B * SC:(j + 1) * B * SC], W("wk")[:, x * P:(x + 1) * P],
                                              k.ctx_t[:], start=True, stop=True)
                    return mm
                return issue

            def take_keys(c):
                def take(act, out):
                    for j in range(4):
                        x = 4 * c + j
                        for half in range(2):
                            part = slice(half * D3, (half + 1) * D3)
                            ins = nc.scalar.activation(
                                keys[part, x, :, half, :],
                                out[part, j * B * SC:(j + 1) * B * SC].rearrange("p (b s) -> p b s", b=B),
                                ACT.Identity, bias=W("bk")[part, x:x + 1])
                    return ins
                return take

            def take_values(b):
                def take(v, out):
                    k.vchain(v, nc.vector.tensor_tensor(v_tmp[:].rearrange("p h d -> p (h d)"), out, W("bv"), ALU.add))
                    return nc.vector.tensor_tensor(values[:, b], v_tmp[:],
                                                   bc(k.own_parity.unsqueeze(2), [P, H3, D3]), ALU.mult)
                return take

            products(k, "l3x_proj", [(SCALAR, four_keys(c), take_keys(c)) for c in range(2)] + [
                (VECTOR, wide(k, k.ctx_twice[:, b].rearrange("p a s -> p (a s)"), W("wv")), take_values(b))
                for b in range(B)] + [
                (SCALAR, wide(k, W("wq")[:, x * P:(x + 1) * P], k.XT),
                 activated(k, q_t[:, x, :], bias=W("bq")[:, x:x + 1])) for x in range(PAIRS)])

            def unit(t):
                b = t // TB

                def score(out):
                    for x in range(PAIRS):
                        mm = nc.tensor.matmul(out[:, x // 4, (x % 4) * P:(x % 4 + 1) * P],
                                              q_t[:, x, t * P:(t + 1) * P], keys[:, x, b], start=True, stop=True)
                    return mm

                def product(out, probs_t):
                    for x in range(PAIRS):
                        mm = nc.tensor.matmul(out[:, x * P:(x + 1) * P], probs_t[:, x * P:(x + 1) * P],
                                              values[:, b, 2 * x:2 * x + 2, :], start=True, stop=True)
                    return mm
                return (2 * BANK, H3, score, product, heads_out[:, t].rearrange("p (h d) -> p h d", h=H3),
                        (keep[:, t, :], add[:, t, :]))

            attention(k, "l3x_att", [unit(t) for t in range(T)], D3 ** -0.5, wide_out=True)
        close_sublayer(k, "l3x_close", heads_out[:], [W("wo")[:, c * P:(c + 1) * P] for c in range(PAIRS)], PAIRS,
                       bias=W("bo"))



DEPTH, HL, DL, WINDOW = 2, 8, 64, 64
INNER = HL * DL
HID = int(P * 4 * 2 / 3)
CHUNKS = [(0, P), (P, P), (2 * P, HID - 2 * P)]
L3F = Pack("l3_ffn")
for _l in range(DEPTH):
    for _key, _width in (("wqkv", 3 * INNER), ("wo", INNER), ("w1", 2 * HID), ("w2", 3 * P), ("b1", 6), ("b2", P),
                         ("ln_g", P), ("ln_b", P), ("q_scale", DL), ("q_swapped", DL), ("k_scale", DL),
                         ("k_swapped", DL)):
        L3F.put(_key + str(_l), _width)
for _key in ("cos_q", "sin_q", "cos_k", "sin_k"):
    L3F.put(_key, TB * DL)


def l3_ffn_layout(i):
    g = lambda key, l: np.asarray(i["L3_ffn_" + key])[l]
    swap = np.r_[DL // 2:DL, 0:DL // 2]
    parts = {}

    def padded(a, n):
        out = np.zeros((n,) + a.shape[1:], a.dtype)
        out[:a.shape[0]] = a
        return out
    for l in range(DEPTH):
        b1 = g("b1", l)
        columns = [padded(b1[half * HID + first:half * HID + first + n], P) for half in range(2) for first, n in CHUNKS]
        parts.update({f"wqkv{l}": g("wqkv", l), f"wo{l}": tile_rows(g("wo", l)), f"w1{l}": g("w1", l),
                      f"w2{l}": tile_rows(padded(g("w2", l), 3 * P)), f"b1{l}": np.stack(columns, axis=1),
                      f"b2{l}": on_all(g("b2", l)), f"ln_g{l}": on_all(g("ln_g", l)), f"ln_b{l}": on_all(g("ln_b", l)),
                      f"q_scale{l}": on_all(g("q_scale", l)), f"q_swapped{l}": on_all(g("q_scale", l)[swap]),
                      f"k_scale{l}": on_all(g("k_scale", l)), f"k_swapped{l}": on_all(g("k_scale", l)[swap])})
    f = np.float32
    half = np.arange(0, DL, 2, dtype=f)
    t = np.arange(S, dtype=f)
    freqs = t[:, None] * (f(1.0) / f(10000.0) ** (half / f(DL)))[None, :]
    freqs = np.concatenate([freqs, freqs], axis=1).astype(np.float64)
    base = (half + 0.4 * DL) / (1.4 * DL)
    scale = base[None, :].astype(np.float64) ** ((t - S // 2) / (WINDOW // 2))[:, None]
    scale = np.concatenate([scale, scale], axis=1)
    sign = np.r_[-np.ones(DL // 2), np.ones(DL // 2)]
    for key, table in (("cos_q", np.cos(freqs) * scale), ("sin_q", np.sin(freqs) * scale * sign),
                       ("cos_k", np.cos(freqs) / scale), ("sin_k", np.sin(freqs) / scale * sign)):
        parts[key] = tile_rows(table.astype(f))
    return L3F.build(parts)


def shift_tokens(k, dst, extra=None):
    nc = k.nc
    H = P // 2
    with nc.Block() as block:

        @block.vector
        def _(v):
            nc.vector.tensor_copy(dst[0:H, :], k.XT[0:H, :])
            nc.vector.memset(dst[H:P].rearrange("p (b s) -> p b s", b=B)[:, :, 0:1], 0.0)

        @block.scalar
        def _(act):
            nc.scalar.copy(dst[H:P].rearrange("p (b s) -> p b s", b=B)[:, :, 1:S],
                           k.XT[H:P].rearrange("p (b s) -> p b s", b=B)[:, :, 0:S - 1])


def l3_ffn(k):
    nc = k.nc
    with ExitStack() as ctx:
        x_in = k.sb("l3f_x_in", [P, T, P], F32, ctx)
        shifted = k.sb("l3f_shifted", [P, N], F32, ctx)
        far_own, far_before = (k.sb("l3f_" + x, [P, P], BF16, ctx) for x in ("far_own", "far_before"))
        with nc.Block() as block:

            @block.vector
            def _(v):
                nc.vector.tensor_copy(x_in[:], k.X[:])

            @block.gpsimd
            def _(g):
                nc.gpsimd.memset(far_own[:], 0.0)
                k.gchain(g, nc.gpsimd.memset(far_before[:], 0.0))
                k.gchain(g, nc.gpsimd.affine_select(out=far_own[:], in_=far_own[:], compare_op=ALU.is_ge, fill=1.0,
                                                    base=0, pattern=[[1, P]], channel_multiplier=-1))
                nc.gpsimd.affine_select(out=far_own[:], in_=far_own[:], compare_op=ALU.is_ge, fill=1.0,
                                        base=WINDOW, pattern=[[-1, P]], channel_multiplier=1)
                nc.gpsimd.affine_select(out=far_before[:], in_=far_before[:], compare_op=ALU.is_ge, fill=1.0,
                                        base=WINDOW - P, pattern=[[-1, P]], channel_multiplier=1)
        for l in range(DEPTH):
            l3_ffn_attention(k, l, shifted, far_own, far_before)
            l3_ffn_net(k, l, shifted, x_in)


def l3_ffn_attention(k, l, shifted, far_own, far_before):
    nc = k.nc
    w = k.weights["l3_ffn"]
    W = lambda key: L3F.view(w, f"{key}{l}")
    table = lambda key: L3F.view(w, key).rearrange("p (i d) -> p i d", i=TB)
    tag = f"l3f{l}"
    with ExitStack() as ctx:
        sb = lambda name, shape, dt=F32: k.sb(f"{tag}_{name}", shape, dt, ctx)
        heads_out = sb("heads_out", [P, T, INNER])
        with ExitStack() as att:
            sb = lambda name, shape, dt=F32: k.sb(f"{tag}_{name}", shape, dt, att)
            values = sb("values", [P, T, HL, DL + 1])
            q_t, k_t = sb("q_t", [P, HL // 2, N]), sb("k_t", [P, HL // 2, N])
            with ExitStack() as unturned:
                rows = {"q": k.sb(f"{tag}_q", [P, T, INNER], F32, unturned), "k": k.sb(f"{tag}_k", [P, T, INNER], F32, unturned)}
                shift_tokens(k, shifted)

                def two_tiles(part, c):
                    def issue(pe, out):
                        for j in range(2):
                            t = 2 * c + j
                            mm = nc.tensor.matmul(out[:, j * INNER:(j + 1) * INNER], shifted[:, t * P:(t + 1) * P],
                                                  W("wqkv")[:, part * INNER:(part + 1) * INNER], start=True, stop=True)
                        return mm
                    return issue
                both = lambda out: out.rearrange("p (t n) -> p t n", t=2)
                products(k, tag + "_qkv", [e for c in range(T // 2) for e in (
                    (SCALAR, two_tiles(0, c), lambda act, out, c=c: nc.scalar.copy(rows["q"][:, 2 * c:2 * c + 2], both(out))),
                    (VECTOR, two_tiles(1, c), lambda v, out, c=c: nc.vector.tensor_copy(rows["k"][:, 2 * c:2 * c + 2],
                                                                                      both(out))),
                    (SCALAR, two_tiles(2, c), lambda act, out, c=c: nc.scalar.copy(
                        values[:, 2 * c:2 * c + 2, :, 0:DL].rearrange("p t h d -> p (t h) d"),
                        out.rearrange("p (x d) -> p x d", d=DL))))])
                l3_ffn_rotate(k, tag, W, table, rows, values, heads_out)

                def turn(src, x):
                    def issue(pe, out):
                        for t in range(T):
                            mm = nc.tensor.transpose(out[:, t * P:(t + 1) * P], src[:, t, x * P:(x + 1) * P], k.ident[:])
                        return mm
                    return issue
                products(k, tag + "_turn", [e for x in range(HL // 2) for e in (
                    (SCALAR, turn(rows["q"], x), lambda act, out, x=x: nc.scalar.copy(q_t[:, x, :], out)),
                    (VECTOR, turn(rows["k"], x), lambda v, out, x=x: nc.vector.tensor_copy(k_t[:, x, :], out)))])

            def unit(t, g):
                b, i = divmod(t, TB)
                width = (i + 1) * P

                def score(out):
                    for o in range(2):
                        for y in range(2):
                            at = out[:, o, y * width:(y + 1) * width]
                            if i:
                                nc.tensor.matmul(at[:, 0:P], far_before[:], k.masker[:], start=True, stop=False,
                                                 skip_group_check=True)
                            nc.tensor.matmul(at[:, i * P:(i + 1) * P], far_own[:], k.masker[:], start=(i == 0),
                                             stop=False, skip_group_check=True)
                            part = slice(o * DL, (o + 1) * DL)
                            mm = nc.tensor.matmul(at, q_t[part, 2 * g + y, t * P:(t + 1) * P],
                                                  k_t[part, 2 * g + y, b * S:b * S + width], start=False, stop=True,
                                                  skip_group_check=True)
                    return mm

                def product(out, probs_t):
                    for o in range(2):
                        for y in range(2):
                            for c in range(i + 1):
                                x = (o * 2 + y) * (i + 1) + c
                                mm = nc.tensor.matmul(out[:, (o * 2 + y) * (DL + 1):(o * 2 + y + 1) * (DL + 1)],
                                                      probs_t[:, x * P:(x + 1) * P],
                                                      values[:, TB * b + c, 4 * g + 2 * y + o, :], start=(c == 0),
                                                      stop=(c == i))
                    return mm
                dest = heads_out[:, t, 4 * g * DL:4 * (g + 1) * DL].rearrange("p (y o d) -> p o y d", y=2, o=2)
                return 4 * width, 4, score, product, dest, None

            attention(k, tag + "_att", [unit(t, g) for t in range(T) for g in range(2)], 8.0)
        close_sublayer(k, tag + "_mid", heads_out[:], [W("wo")[:, c * P:(c + 1) * P] for c in range(INNER // P)],
                       INNER // P, norm=False)


def l3_ffn_rotate(k, tag, W, table, rows, values, scratch):
    nc = k.nc
    with ExitStack() as ctx:
        sb = lambda name, shape: k.sb(f"{tag}r_{name}", shape, F32, ctx)
        squares = scratch[:].rearrange("p t (h d) -> p (t h) d", d=DL)
        part = sb("part", [P, HL, DL])
        length, half = sb("length", [P, 2, T * HL]), sb("half", [P, 2, T * HL])
        tables = {x: sb("table_" + x, [P, TB, DL]) for x in ("cos_q", "sin_q", "cos_k", "sin_k")}
        summed, rooted = k.sems(tag + "r", "summed rooted")
        with nc.Block() as block:

            @block.gpsimd
            def _(g):
                nc.gpsimd.memset(values[:, :, :, DL:DL + 1], 1.0)
                k.gchain(g, nc.gpsimd.memset(half[:], 0.5))
                g.wait_ge(summed, 1)
                nc.gpsimd.tensor_tensor(length[:], length[:], half[:], ALU.pow).then_inc(rooted, 1)

            @block.vector
            def _(v):
                link = k.vchain
                for x in "qk":
                    for trig, by in (("cos_", "_scale"), ("sin_", "_swapped")):
                        nc.vector.tensor_tensor(tables[trig + x][:], table(trig + x), bc(W(x + by).unsqueeze(1),
                                                                                        [P, TB, DL]), ALU.mult)
                for n, x in enumerate("qk"):
                    heads = rows[x][:].rearrange("p t (h d) -> p (t h) d", d=DL)
                    link(v, nc.vector.tensor_tensor(squares, heads, heads, ALU.mult))
                    last = nc.vector.tensor_reduce(length[:, n, :], squares, AX.X, ALU.add)
                    if n == 0:
                        link(v, last)
                last.then_inc(summed, 1)
                v.wait_ge(rooted, 1)
                link(v, nc.vector.tensor_scalar(length[:], length[:], 1e-12, None, ALU.max))
                link(v, nc.vector.reciprocal(length[:], length[:]))
                for n, x in enumerate("qk"):
                    heads = rows[x][:].rearrange("p t (h d) -> p (t h) d", d=DL)
                    link(v, nc.vector.tensor_tensor(heads, heads, bc(length[:, n, :].unsqueeze(2), [P, T * HL, DL]),
                                                    ALU.mult))
                    for t in range(T):
                        i = t % TB
                        one = rows[x][:, t].rearrange("p (h d) -> p h d", h=HL)
                        for to, of in ((slice(0, DL // 2), slice(DL // 2, DL)), (slice(DL // 2, DL), slice(0, DL // 2))):
                            last = nc.vector.tensor_tensor(part[:, :, to], one[:, :, of], bc(
                                tables["sin_" + x][:, i, to].unsqueeze(1), [P, HL, DL // 2]), ALU.mult)
                        link(v, last)
                        link(v, nc.vector.tensor_tensor(one, one, bc(tables["cos_" + x][:, i].unsqueeze(1),
                                                                     [P, HL, DL]), ALU.mult))
                        link(v, nc.vector.tensor_tensor(one, one, part[:], ALU.add))


def l3_ffn_net(k, l, shifted, x_in):
    nc = k.nc
    w = k.weights["l3_ffn"]
    W = lambda key: L3F.view(w, f"{key}{l}")
    tag = f"l3n{l}"
    with ExitStack() as ctx:
        sb = lambda name, shape, dt=F32: k.sb(f"{tag}_{name}", shape, dt, ctx)
        rows, normed = sb("rows", [P, T, P]), sb("normed", [P, N])
        act_part, hidden = sb("act_part", [P, 3, N]), sb("hidden", [P, 3, N])
        shift_tokens(k, shifted)

        def token_major(pe, out):
            for t in range(T):
                mm = nc.tensor.transpose(out[:, t * P:(t + 1) * P], shifted[:, t * P:(t + 1) * P], k.ident[:])
            return mm
        products(k, tag + "_rows", [(SCALAR, token_major, activated(k, rows[:].rearrange("p t n -> p (t n)")))])
        norm_and_turn(k, tag + "_norm", rows[:], rows[:], normed[:], W("ln_g"), W("ln_b"))
        products(k, tag + "_g", [(SCALAR, wide(k, W("w1")[:, HID + first:HID + first + n], normed, n),
                                  activated(k, act_part[0:n, c, :], ACT.Gelu, W("b1")[0:n, 3 + c:4 + c], n))
                                 for c, (first, n) in enumerate(CHUNKS)])
        products(k, tag + "_a", [(VECTOR, wide(k, W("w1")[:, first:first + n], normed, n),
                                  lambda v, out, c=c, n=n: nc.vector.scalar_tensor_tensor(
                                      hidden[0:n, c, :], out[0:n, :], W("b1")[0:n, c:c + 1], act_part[0:n, c, :],
                                      ALU.add, ALU.mult))
                                 for c, (first, n) in enumerate(CHUNKS)])
        end = l == DEPTH - 1
        close_sublayer(k, tag + "_close", None, [W("w2")[0:n, c * P:(c + 1) * P] for c, (_, n) in enumerate(CHUNKS)], 3,
                       bias=W("b2"), features_t=[hidden[0:n, c, :] for c, (_, n) in enumerate(CHUNKS)],
                       addend=x_in[:] if end else None, norm=end)


MARKS = Pack("marks")
for _key, _width in (("own_head", HX), ("own_of_four", 4), ("own_parity", HX)):
    MARKS.put(_key, _width)


def marks_layout(i):
    head = np.arange(P)[:, None] // DX
    return MARKS.build({"own_head": head == np.arange(HX), "own_of_four": head % 4 == np.arange(4),
                        "own_parity": np.arange(P)[:, None] // SC == np.arange(HX) % 2})


def other_layouts(i):
    ctx_t = np.asarray(i["ctx_1024"]).transpose(2, 0, 1)
    return {
        "ctx_t": np.ascontiguousarray(ctx_t.reshape(P, B * SC)),
        "ctx_twice": np.ascontiguousarray(np.stack([ctx_t, ctx_t], axis=2)),
        "ctx_rows": np.ascontiguousarray(np.asarray(i["ctx_1024"]).transpose(1, 0, 2)),
        "l1_experts": l1_experts_layout(i),
        "marks": marks_layout(i),
        "mask3": np.ascontiguousarray(np.asarray(i["mask_BxSxS2_bk1"]).reshape(T, P, SC)
                                      .transpose(1, 0, 2).astype(np.int32)),
        "mask0": np.ascontiguousarray(np.asarray(i["mask_1x1xSxS2_ik1"]).reshape(TB, P, SC).transpose(1, 0, 2)),
        "l0_experts": l0_experts_layout(i),
    }

STAGES = [0,1,2,3,4,5,6,7,8,9,10,11]



GROUPS = [
    ("layers_0_1", {"l0_attn": (L0A, l0_attn_layout), "l0_xattn": (L0X, l0_xattn_layout),
                    "l0_ffn": (L0F, l0_ffn_layout), "l1_attn": (L1A, l1_attn_layout),
                    "l1_xattn": (L1X, l1_xattn_layout), "l1_ffn": (L1F, l1_ffn_layout)},
     [l0_attn, l0_xattn, l0_ffn, l1_attn, l1_xattn, l1_ffn]),
    ("layer_2", {"l2_attn": (L2A, l2_attn_layout), "l2_xattn": (L2X, l2_xattn_layout),
                 "l2_ffn": (L2F, l2_ffn_layout)}, [l2_attn, l2_xattn, l2_ffn]),
    ("layer_3", {"l3_attn": (L3A, l3_attn_layout), "l3_xattn": (L3X, l3_xattn_layout),
                 "l3_ffn": (L3F, l3_ffn_layout)}, [l3_attn, l3_xattn, l3_ffn])]


def load_weights(k, tag, packs, ctx, others=()):
    nc = k.nc
    k.weights = {name: k.sb("w_" + name, [P, pack.width], F32, ctx) for name, (pack, _) in packs.items()}
    loaded = k.sem(tag)
    pairs = list(others) + [(k.weights[name][:], k.dram["w_" + name]) for name in packs]
    with nc.Block() as block:

        @block.sync
        def _(sp):
            for dst, src in pairs:
                sp.dma_start(dst, src).then_inc(loaded, 16)
            sp.wait_ge(loaded, 16 * len(pairs))


def decoder(nc, dram, stages):
    with ExitStack() as ctx:
        k = Core(nc, ctx, dram)
        k.quarter = k.sb("quarter", [P, 1])
        k.ctx_t = k.sb("ctx_t", [P, B * SC])
        k.ctx_twice = k.sb("ctx_twice", [P, B, 2, SC])
        k.ctx_rows = k.sb("ctx_rows", [SC, B, P])
        k.mask0 = k.sb("mask0", [P, TB, SC], I32)
        k.mask3 = k.sb("mask3", [P, T, SC], I32)
        k.marks = k.sb("marks", [P, MARKS.width])
        k.own_head, k.own_of_four, k.own_parity = (MARKS.view(k.marks, x)
                                                   for x in ("own_head", "own_of_four", "own_parity"))
        constants(k)
        others = [(k.X[:], dram["x"].rearrange("b (i p) d -> p (b i) d", p=P)), (k.XT[:], dram["xt"]),
                  (k.ctx_t[:], dram["ctx_t"]), (k.ctx_twice[:], dram["ctx_twice"]), (k.ctx_rows[:], dram["ctx_rows"]),
                  (k.mask0[:], dram["mask0"]), (k.mask3[:], dram["mask3"]), (k.marks[:], dram["marks"])]
        n = 0
        for name, packs, sublayers in GROUPS:
            with ExitStack() as weights:
                load_weights(k, "loaded_" + name, packs, weights, others)
                for sublayer in sublayers:
                    if n in stages:
                        sublayer(k)
                    n += 1
            others = []
        stored = k.sem("stored")
        with nc.Block() as block:

            @block.sync
            def _(sp):
                sp.dma_start(dram["out"].rearrange("b (i p) d -> p (b i) d", p=P), k.X[:]).then_inc(stored, 16)
                sp.wait_ge(stored, 16)


def kernel(**inputs):
    from concourse import bacc
    from concourse.bass_utils import run_bass_kernel_spmd

    x = np.asarray(inputs["x"])
    arrays = {"x": x, "xt": np.ascontiguousarray(x.reshape(N, P).T)}
    for _, packs, _ in GROUPS:
        arrays.update({"w_" + name: layout(inputs) for name, (_, layout) in packs.items()})
    arrays.update(other_layouts(inputs))
    nc = bacc.Bacc("TRN2", target_bir_lowering=False, num_devices=1)
    dram = {name: nc.dram_tensor("in_" + name, a.shape, mybir.dt.from_np(a.dtype), kind="ExternalInput").ap()
            for name, a in arrays.items()}
    dram["out"] = nc.dram_tensor("out", (B, S, P), F32, kind="ExternalOutput").ap()
    decoder(nc, dram, STAGES)
    result = run_bass_kernel_spmd(nc, [{"in_" + name: a for name, a in arrays.items()}], core_ids=[0])
    return result.results[0]["out"]
```

```python
from contextlib import ExitStack

import numpy as np

import concourse.bass as bass
from concourse import mybir
from concourse.alu_op_type import AluOpType as ALU

ACT = mybir.ActivationFunctionType
F32 = mybir.dt.float32
BF16 = mybir.dt.bfloat16
I32 = mybir.dt.int32
AX = mybir.AxisListType

P = 128
B = 4
S = 256
SC = 64
T = B * S // P
TB = S // P
N = B * S
BANK = 512
MASKED = -2.0 ** 30
EPS = 1e-5


class Chain:

    def __init__(self, sem):
        self.sem, self.base, self.n = sem, 0, 0

    def __call__(self, eng, ins):
        self.n += 1
        ins.then_inc(self.sem, 1)
        eng.wait_ge(self.sem, self.base + self.n)

    def enter(self, turn, per_turn):
        self.kept, self.per_turn = self.n, per_turn
        self.base, self.n = self.n + turn * per_turn, 0

    def leave(self, turns):
        assert self.n == self.per_turn, (self.n, self.per_turn)
        self.base, self.n = 0, self.kept + turns * self.per_turn


class Counted:

    def __init__(self, sem):
        self.sem, self.base = sem, 0


class Core:

    def __init__(self, nc, ctx, dram):
        self.nc, self.ctx, self.dram, self.shared = nc, ctx, dram, {}
        self.X = self.sb("X", [P, T, P])
        self.XT = self.sb("XT", [P, N])
        self.centred = self.sb("centred", [P, T, P])
        self.squared = self.sb("squared", [P, T, P])
        self.stat = self.sb("stat", [P, 4, T])
        self.vchain = Chain(self.sem("vector_chain"))
        self.gchain = Chain(self.sem("gpsimd_chain"))

    def sb(self, name, shape, dt=F32, ctx=None):
        return (ctx or self.ctx).enter_context(self.nc.sbuf_tensor(name, shape, dt))

    def ps(self, name, shape, ctx, dt=F32):
        return ctx.enter_context(self.nc.psum_tensor(name, shape, dt))

    def sem(self, name):
        return self.ctx.enter_context(self.nc.semaphore(name))

    def counted(self, tag, names):
        for n in names.split():
            if (tag, n) not in self.shared:
                self.shared[tag, n] = Counted(self.sem(f"{tag}_{n}"))
        return [self.shared[tag, n] for n in names.split()]

    def sems(self, tag, names):
        return [self.sem(f"{tag}_{n}") for n in names.split()]


def bc(ap, shape):
    return ap.broadcast_to(shape)



class Pack:

    def __init__(self, name):
        self.name, self.at, self.width = name, {}, 0

    def put(self, key, width):
        self.at[key] = (self.width, width)
        self.width += width

    def build(self, parts):
        out = np.zeros((P, self.width), np.float32)
        for key, a in parts.items():
            start, width = self.at[key]
            a = np.asarray(a)
            assert a.ndim == 2 and a.shape[1] == width and a.shape[0] <= P, (key, a.shape, width)
            out[:a.shape[0], start:start + width] = a
        return out

    def view(self, tile, key):
        start, width = self.at[key]
        return tile[:, start:start + width]


def tile_rows(a, rows=P):
    n = a.shape[0] // rows
    return a.reshape(n, rows, a.shape[1]).transpose(1, 0, 2).reshape(rows, -1)


def on_all(v):
    return np.broadcast_to(np.asarray(v).reshape(1, -1), (P, np.asarray(v).size))


def column(v):
    return np.asarray(v).reshape(-1, 1)



HALVES = (slice(0, T // 2), slice(T // 2, T))
NORM_SIGNALS = "centred_ready squared_ready var_ready rstd_ready normed"


def norm_vector(k, v, src, dst, signals, n, gain=None, shift=None):
    centred_ready, squared_ready, var_ready, rstd_ready, normed = signals
    nc, link, full = k.nc, k.vchain, [P, T // 2, P]
    stat = lambda row, half: k.stat[:, row, half]
    for half in HALVES:
        last = nc.vector.tensor_reduce(stat(0, half), src[:, half], AX.X, ALU.add)
    link(v, last)
    for half in HALVES:
        last = nc.vector.tensor_scalar(stat(1, half), stat(0, half), 1.0 / P, None, ALU.mult)
    link(v, last)
    for half in HALVES:
        nc.vector.tensor_tensor(k.centred[:, half], src[:, half], bc(stat(1, half).unsqueeze(2), full),
                                ALU.subtract).then_inc(centred_ready.sem, 1)
    for i, half in enumerate(HALVES):
        v.wait_ge(squared_ready.sem, squared_ready.base + 2 * n + i + 1)
        link(v, nc.vector.tensor_reduce(stat(2, half), k.squared[:, half], AX.X, ALU.add))
        nc.vector.tensor_scalar(stat(3, half), stat(2, half), 1.0 / P, EPS, ALU.mult, ALU.add)\
            .then_inc(var_ready.sem, 1)
    for i, half in enumerate(HALVES):
        v.wait_ge(rstd_ready.sem, rstd_ready.base + 2 * n + i + 1)
        last = nc.vector.tensor_tensor(dst[:, half], k.centred[:, half], bc(k.rstd[:, half].unsqueeze(2), full),
                                       ALU.mult)
        if gain is not None:
            link(v, last)
            link(v, nc.vector.tensor_tensor(dst[:, half], dst[:, half], bc(gain.unsqueeze(1), full), ALU.mult))
            last = nc.vector.tensor_tensor(dst[:, half], dst[:, half], bc(shift.unsqueeze(1), full), ALU.add)
        last.then_inc(normed.sem, 1)


def norm_scalar(k, act, signals, n):
    centred_ready, squared_ready, *_ = signals
    for i, half in enumerate(HALVES):
        act.wait_ge(centred_ready.sem, centred_ready.base + 2 * n + i + 1)
        k.nc.scalar.activation(k.squared[:, half], k.centred[:, half], ACT.Square).then_inc(squared_ready.sem, 1)


def norm_gpsimd(k, g, signals, n):
    _, _, var_ready, rstd_ready, _ = signals
    for i, half in enumerate(HALVES):
        g.wait_ge(var_ready.sem, var_ready.base + 2 * n + i + 1)
        k.nc.gpsimd.tensor_tensor(k.rstd[:, half], k.stat[:, 3, half], k.minus_half[:, half], ALU.pow)\
            .then_inc(rstd_ready.sem, 1)


def turn_normed(k, pe, signals, n, source, xt, xt_ready):
    normed = signals[-1]
    for i, half in enumerate(HALVES):
        pe.wait_ge(normed.sem, normed.base + 2 * n + i + 1)
        for t in range(T)[half]:
            mm = k.nc.tensor.transpose(xt[:, t * P:(t + 1) * P], source[:, t, :], k.ident[:])
        mm.then_inc(xt_ready.sem, 1)


def count_norms(signals, norms):
    for counted in signals:
        counted.base += 2 * norms


def constants(k):
    k.ident = k.sb("ident", [P, P])
    k.masker = k.sb("masker", [P, P], BF16)
    k.above = k.sb("above", [P, P], BF16)
    k.ones = k.sb("ones", [P, P])
    k.rstd = k.sb("rstd", [P, T])
    k.minus_half = k.sb("minus_half", [P, T])
    filled, = k.sems("const", "filled")
    with k.nc.Block() as block:

        @block.gpsimd
        def _(g):
            nc = k.nc
            nc.gpsimd.memset(k.ident[:], 0.0).then_inc(filled, 1)
            nc.gpsimd.memset(k.masker[:], 0.0).then_inc(filled, 1)
            nc.gpsimd.memset(k.above[:], 0.0).then_inc(filled, 1)
            nc.gpsimd.memset(k.ones[:], 1.0)
            nc.gpsimd.memset(k.quarter[:], 0.25)
            nc.gpsimd.memset(k.minus_half[:], -0.5)
            g.wait_ge(filled, 3)
            for m, value in ((k.ident, 1.0), (k.masker, MASKED)):
                nc.gpsimd.affine_select(out=m[:], in_=m[:], compare_op=ALU.not_equal, fill=value, base=0,
                                        pattern=[[-1, P]], channel_multiplier=1)
            nc.gpsimd.affine_select(out=k.above[:], in_=k.above[:], compare_op=ALU.is_ge, fill=1.0, base=0,
                                    pattern=[[1, P]], channel_multiplier=-1)


SCALAR, VECTOR = "scalar", "vector"


def products(k, tag, table):
    nc = k.nc
    ring = 4
    with ExitStack() as ctx:
        areas = k.ps(f"{tag}_areas", [P, ring, 2 * BANK], ctx)
        ready, by_scalar, by_vector = k.counted("products", "ready taken_by_scalar taken_by_vector")
        taken = {SCALAR: by_scalar, VECTOR: by_vector}
        upto = lambda n: sum(1 for who, _, _ in table[:n] if who == table[n - 1][0])
        with nc.Block() as block:

            @block.tensor
            def _(pe):
                for n, (who, issue, _) in enumerate(table):
                    if n >= ring:
                        last = taken[table[n - ring][0]]
                        pe.wait_ge(last.sem, last.base + upto(n - ring + 1))
                    issue(pe, areas[:, n % ring, :]).then_inc(ready.sem, 1)

            def take_out(eng, me):
                for n, (who, _, take) in enumerate(table):
                    if who == me:
                        eng.wait_ge(ready.sem, ready.base + n + 1)
                        take(eng, areas[:, n % ring, :]).then_inc(taken[me].sem, 1)
                        eng.wait_ge(taken[me].sem, taken[me].base + upto(n + 1))

            @block.scalar
            def _(act):
                take_out(act, SCALAR)

            @block.vector
            def _(v):
                take_out(v, VECTOR)
        ready.base += len(table)
        for who in taken:
            taken[who].base += sum(1 for entry in table if entry[0] == who)


def wide(k, lhsT, rhs, rows=P):
    def issue(pe, out):
        for c in range(2):
            mm = k.nc.tensor.matmul(out[0:rows, c * BANK:(c + 1) * BANK], lhsT, rhs[:, c * BANK:(c + 1) * BANK],
                                    start=True, stop=True)
        return mm
    return issue


def narrow(k, lhsT, rhs, cols, rows=P):
    return lambda pe, out: k.nc.tensor.matmul(out[0:rows, 0:cols], lhsT, rhs, start=True, stop=True)


def by_tile(k, source_t, rhs, width):
    def issue(pe, out):
        for t in range(T):
            mm = k.nc.tensor.matmul(out[:, t * width:(t + 1) * width], source_t[:, t * P:(t + 1) * P], rhs,
                                    start=True, stop=True)
        return mm
    return issue


def activated(k, dst, func=ACT.Identity, bias=0.0, rows=P, cols=N, scale=1.0):
    return lambda act, out: k.nc.scalar.activation(dst, out[0:rows, 0:cols], func, bias=bias, scale=scale)


def attention(k, tag, units, scale, wide_out=False):
    nc = k.nc
    with ExitStack() as ctx:
        scores = k.ps(f"{tag}_scores", [P, 2, 2, BANK], ctx)
        turned = k.ps(f"{tag}_turned", [P, 2 * BANK], ctx)
        outs = k.ps(f"{tag}_outs", [P, 2, BANK], ctx)
        probs = k.sb(f"{tag}_probs", [P, 2, 2 * BANK], ctx=ctx)
        probs_t = k.sb(f"{tag}_probs_t", [P, 2 * BANK], ctx=ctx)
        top = k.sb(f"{tag}_top", [P, 2, 16], ctx=ctx)
        total = k.sb(f"{tag}_total", [P, 2, 16], ctx=ctx)
        (scores_ready, shifted, exp_ready, turned_ready, turned_copied, out_ready, out_used) = k.counted(
            "attention", "scores_ready shifted exp_ready turned_ready turned_copied out_ready out_used")
        area = lambda u: outs[:].rearrange("p a b -> p (a b)") if wide_out else outs[:, u % 2]
        outs_in_turn = 1 if wide_out else 2
        with nc.Block() as block:

            @block.tensor
            def _(pe):
                def score(u):
                    if u >= 2:
                        pe.wait_ge(shifted.sem, shifted.base + u - 1)
                    units[u][2](scores[:, u % 2]).then_inc(scores_ready.sem, 1)

                def weigh(u):
                    pe.wait_ge(turned_copied.sem, turned_copied.base + u + 1)
                    if u >= outs_in_turn:
                        pe.wait_ge(out_used.sem, out_used.base + u + 1 - outs_in_turn)
                    units[u][3](area(u), probs_t).then_inc(out_ready.sem, 1)

                score(0)
                for u, (columns, *_) in enumerate(units):
                    if u + 1 < len(units):
                        score(u + 1)
                    if u >= 1:
                        weigh(u - 1)
                    pe.wait_ge(exp_ready.sem, exp_ready.base + u + 1)
                    for x in range(columns // P):
                        mm = nc.tensor.transpose(turned[:, x * P:(x + 1) * P], probs[:, u % 2, x * P:(x + 1) * P],
                                                 k.ident[:])
                    mm.then_inc(turned_ready.sem, 1)
                weigh(len(units) - 1)

            @block.scalar
            def _(act):
                for u, (columns, *_) in enumerate(units):
                    act.wait_ge(shifted.sem, shifted.base + u + 1)
                    nc.scalar.activation(probs[:, u % 2, 0:columns], probs[:, u % 2, 0:columns], ACT.Exp,
                                         scale=scale).then_inc(exp_ready.sem, 1)
                    act.wait_ge(turned_ready.sem, turned_ready.base + u + 1)
                    nc.scalar.copy(probs_t[:, 0:columns], turned[:, 0:columns]).then_inc(turned_copied.sem, 1)

            @block.vector
            def _(v):
                link = k.vchain
                lag = 1 if wide_out else min(2, len(units))

                def finish(u):
                    columns, groups, _, _, dest, _ = units[u]
                    sums = total[:, u % 2, 0:groups]
                    if wide_out:
                        out = area(u)[:, 0:columns].rearrange("p (g d) -> p g d", g=groups)
                        v.wait_ge(exp_ready.sem, exp_ready.base + u + 1)
                        link(v, nc.vector.tensor_reduce(sums, probs[:, u % 2, 0:columns].rearrange(
                            "p (g w) -> p g w", g=groups), AX.X, ALU.add))
                        v.wait_ge(out_ready.sem, out_ready.base + u + 1)
                        link(v, nc.vector.reciprocal(sums, sums))
                    else:
                        width = dest.shape[-1]
                        out = area(u)[:, 0:groups * (width + 1)].rearrange("p (g d) -> p g d", g=groups)
                        v.wait_ge(out_ready.sem, out_ready.base + u + 1)
                        link(v, nc.vector.reciprocal(sums, out[:, :, width]))
                        out = out[:, :, 0:width]
                    sums = sums.unsqueeze(2)
                    if len(dest.shape) == 4:
                        out, sums = (x.rearrange("p (o g) d -> p o g d", o=2) for x in (out, sums))
                    nc.vector.tensor_tensor(dest, out, bc(sums, list(dest.shape)), ALU.mult)\
                        .then_inc(out_used.sem, 1)

                for u, (columns, groups, _, _, dest, mask) in enumerate(units):
                    split = lambda x: x.rearrange("p o (g w) -> p o g w", g=groups // 2)
                    banks = split(scores[:, u % 2, :, 0:columns // 2])
                    packed = split(probs[:, u % 2, 0:columns].rearrange("p (o c) -> p o c", o=2))
                    tops = top[:, u % 2, 0:groups].rearrange("p (o g) -> p o g", o=2)
                    full = [P, 2, groups // 2, columns // groups]
                    v.wait_ge(scores_ready.sem, scores_ready.base + u + 1)
                    if u >= 2:
                        v.wait_ge(turned_ready.sem, turned_ready.base + u - 1)
                    if mask:
                        packed_groups = probs[:, u % 2, 0:columns].rearrange("p (g w) -> p g w", g=groups)
                        flat = [P, groups, columns // groups]
                        for o in range(2):
                            link(v, nc.vector.tensor_tensor(packed[:, o], banks[:, o],
                                                            bc(mask[0].unsqueeze(1), full[:1] + full[2:]), ALU.mult))
                        link(v, nc.vector.tensor_tensor(packed_groups, packed_groups, bc(mask[1].unsqueeze(1), flat),
                                                        ALU.add))
                        source = packed
                    else:
                        source = banks
                    link(v, nc.vector.tensor_reduce(tops, source, AX.X, ALU.max))
                    nc.vector.tensor_tensor(packed, source, bc(tops.unsqueeze(3), full), ALU.subtract)\
                        .then_inc(shifted.sem, 1)
                    v.wait_ge(shifted.sem, shifted.base + u + 1)
                    if u >= lag:
                        finish(u - lag)
                for u in range(len(units) - lag, len(units)):
                    finish(u)
        for counted in (scores_ready, shifted, exp_ready, turned_ready, turned_copied, out_ready, out_used):
            counted.base += len(units)


def close_sublayer(k, tag, features, weights, chunks, bias=None, doubled=False, extra_norm=None,
                   features_t=None, addend=None, to=None, gain=None, shift=None, norm=True):
    normed_to, turned_to = to or (k.X[:], k.XT[:])
    nc = k.nc
    with ExitStack() as ctx:
        width = chunks * P
        turned = k.ps(f"{tag}_turned", [P, 2, 2, BANK], ctx)
        product = k.ps(f"{tag}_product", [P, T, P], ctx)
        xt = k.ps(f"{tag}_xt", [P, N], ctx)
        turned_sb = k.sb(f"{tag}_turned_sb", [P, 2, width], ctx=ctx)
        turned_ready, turned_copied, product_ready, xt_ready, added = k.counted(
            "close", "turned_ready turned_copied product_ready xt_ready added")
        signals = k.counted("norm", NORM_SIGNALS)
        norms = 2 if extra_norm else 1 if norm else 0
        flat = lambda t: turned[:, t % 2].rearrange("p a b -> p (a b)")[:, 0:width]
        with nc.Block() as block:

            @block.tensor
            def _(pe):
                def turn(t):
                    if t >= 2:
                        pe.wait_ge(turned_copied.sem, turned_copied.base + t - 1)
                    for c in range(chunks):
                        last_one = nc.tensor.transpose(flat(t)[:, c * P:(c + 1) * P],
                                                       features[:, t, c * P:(c + 1) * P], k.ident[:])
                    last_one.then_inc(turned_ready.sem, 1)

                if not features_t:
                    turn(0)
                for t in range(T):
                    if not features_t:
                        if t + 1 < T:
                            turn(t + 1)
                        pe.wait_ge(turned_copied.sem, turned_copied.base + t + 1)
                    for c in range(chunks):
                        rows = features_t[c][:, t * P:(t + 1) * P] if features_t else \
                            turned_sb[:, t % 2, c * P:(c + 1) * P]
                        last_one = nc.tensor.matmul(product[:, t, :], rows, weights[c], start=(c == 0),
                                                    stop=(c == chunks - 1))
                    last_one.then_inc(product_ready.sem, 1)
                if norms:
                    turn_normed(k, pe, signals, norms - 1, normed_to, xt, xt_ready)
                else:
                    for i, half in enumerate(HALVES):
                        pe.wait_ge(added.sem, added.base + i + 1)
                        for t in range(T)[half]:
                            last_one = nc.tensor.transpose(xt[:, t * P:(t + 1) * P], k.X[:, t, :], k.ident[:])
                        last_one.then_inc(xt_ready.sem, 1)

            @block.scalar
            def _(act):
                for t in range(0 if features_t else T):
                    act.wait_ge(turned_ready.sem, turned_ready.base + t + 1)
                    if t >= 2:
                        act.wait_ge(product_ready.sem, product_ready.base + t - 1)
                    nc.scalar.copy(turned_sb[:, t % 2, :], flat(t)).then_inc(turned_copied.sem, 1)
                for n in range(norms):
                    norm_scalar(k, act, signals, n)
                for i in range(2):
                    act.wait_ge(xt_ready.sem, xt_ready.base + i + 1)
                    nc.scalar.copy(turned_to[:, i * BANK:(i + 1) * BANK], xt[:, i * BANK:(i + 1) * BANK])

            @block.vector
            def _(v):
                link = k.vchain
                if doubled:
                    link(v, nc.vector.tensor_scalar(k.X[:], k.X[:], 2.0, None, ALU.mult))
                if bias is not None:
                    link(v, nc.vector.tensor_tensor(k.X[:], k.X[:], bc(bias.unsqueeze(1), [P, T, P]), ALU.add))
                if addend is not None:
                    link(v, nc.vector.tensor_tensor(k.X[:], k.X[:], addend, ALU.add))
                for i, half in enumerate(HALVES):
                    v.wait_ge(product_ready.sem, product_ready.base + half.stop)
                    nc.vector.tensor_tensor(k.X[:, half], k.X[:, half], product[:, half], ALU.add)\
                        .then_inc(added.sem, 1)
                v.wait_ge(added.sem, added.base + 2)
                if extra_norm:
                    norm_vector(k, v, k.X[:], k.X[:], signals, 0, *extra_norm)
                    v.wait_ge(signals[-1].sem, signals[-1].base + 2)
                if norm:
                    norm_vector(k, v, k.X[:], normed_to, signals, norms - 1, gain, shift)

            @block.gpsimd
            def _(g):
                for n in range(norms):
                    norm_gpsimd(k, g, signals, n)
        for counted, count in ((turned_ready, 0 if features_t else T), (turned_copied, 0 if features_t else T),
                               (product_ready, T), (xt_ready, 2), (added, 2)):
            counted.base += count
        count_norms(signals, norms)


def norm_and_turn(k, tag, src, dst, dst_t, gain=None, shift=None, addends=(), copy_to=None, on_turned=None):
    nc = k.nc
    with ExitStack() as ctx:
        xt = k.ps(f"{tag}_xt", [P, N], ctx)
        signals = k.counted("norm", NORM_SIGNALS)
        xt_ready, = k.counted("norm_and_turn", "xt_ready")
        with nc.Block() as block:

            @block.tensor
            def _(pe):
                turn_normed(k, pe, signals, 0, dst, xt, xt_ready)

            @block.scalar
            def _(act):
                norm_scalar(k, act, signals, 0)
                for i in range(2):
                    act.wait_ge(xt_ready.sem, xt_ready.base + i + 1)
                    half = slice(i * BANK, (i + 1) * BANK)
                    if on_turned:
                        on_turned(act, i, xt[:, half])
                    else:
                        nc.scalar.copy(dst_t[:, half], xt[:, half])

            @block.vector
            def _(v):
                if copy_to is not None:
                    k.vchain(v, nc.vector.tensor_copy(copy_to, src))
                for a in addends:
                    k.vchain(v, nc.vector.tensor_tensor(src, src, a, ALU.add))
                norm_vector(k, v, src, dst, signals, 0, gain, shift)

            @block.gpsimd
            def _(g):
                norm_gpsimd(k, g, signals, 0)
        count_norms(signals, 1)
        xt_ready.base += 2



H0, KV0, D0, NODES = 16, 4, 64, 4
G0 = H0 // KV0
SINES_AFTER = 5
ROUND = 1.5 * 2.0 ** 23
TWO_PI = 6.283185

L0A = Pack("l0_attn")
for _key, _width in (("wv", KV0 * D0), ("wr", H0 * NODES), ("freq", 1), ("sin_scale", 1), ("earlier", NODES * NODES),
                     ("wq", (H0 + 1) * 2 * D0), ("wk", (H0 + 1) * 2 * D0), ("wo", 8 * P)):
    L0A.put(_key, _width)


def l0_attn_layout(i):
    swap = np.r_[D0 // 2:D0, 0:D0 // 2]

    def heads(w, n):
        w = np.asarray(w).reshape(P, n, D0)
        return np.stack([w, w[:, :, swap]], axis=2).reshape(P, n * 2 * D0)
    none = np.zeros((P, 2 * D0), np.float32)
    wq = np.concatenate([heads(i["L0_attn_wq"], H0), none], axis=1)
    wk = heads(i["L0_attn_wk"], KV0).reshape(P, KV0, 1, 2 * D0).repeat(G0, axis=2).reshape(P, H0 * 2 * D0)
    inv_freq = (1.0 / 10000.0 ** (np.arange(0, D0, 2, dtype=np.float32) / D0)).astype(np.float64)
    freq = np.tile(inv_freq / (2 * np.pi), 4).astype(np.float32).reshape(P, 1)
    sign = np.tile(np.r_[-np.ones(D0 // 2), np.ones(D0 // 2)], 2).reshape(P, 1)
    earlier = np.tril(np.ones((NODES, NODES)), -1).reshape(1, -1)
    return L0A.build({"wq": wq, "wk": np.concatenate([wk, none], axis=1), "wv": i["L0_attn_wv"], "wr": i["L0_attn_wr"],
                      "wo": tile_rows(np.asarray(i["L0_attn_wo"])), "freq": freq, "sin_scale": sign * TWO_PI,
                      "earlier": np.broadcast_to(earlier, (P, NODES * NODES))})


def l0_attn(k):
    nc = k.nc
    with ExitStack() as ctx:
        sb = lambda name, shape, dt=F32: k.sb("l0a_" + name, shape, dt, ctx)
        w = k.weights["l0_attn"]
        W = lambda key: L0A.view(w, key)
        values = sb("values", [P, T, KV0, D0 + 1])
        member = sb("member", [P, T, H0 + 2, NODES], BF16)
        absent = sb("absent", [P, T, H0 + 1, NODES], BF16)
        mix = sb("mix", [P, T, H0, NODES])
        before = sb("before", [P, 2, P], BF16)
        heads_out = sb("heads_out", [P, T, H0 * D0])
        l0_attn_route(k, W, values, member, absent, mix, before)
        l0_attn_heads(k, W, values, member, absent, mix, before, heads_out)
        close_sublayer(k, "l0a_close", heads_out[:], [W("wo")[:, c * P:(c + 1) * P] for c in range(8)], 8)


def l0_attn_route(k, W, values, member, absent, mix, before):
    nc = k.nc
    pairs = [P, T * H0, NODES, NODES]
    with ExitStack() as ctx:
        sb = lambda name, shape, dt=F32: k.sb("l0r_" + name, shape, dt, ctx)
        logits_ps = k.ps("l0r_logits_ps", [P, T * H0, NODES], ctx)
        values_ps = k.ps("l0r_values_ps", [P, T, KV0, D0], ctx)
        logits = sb("logits", [P, T * H0, NODES])
        greater = sb("greater", [P, T * H0, NODES, NODES])
        tied = sb("tied", [P, T * H0, NODES, NODES])
        rank = sb("rank", [P, T * H0, NODES])
        top = sb("top", [P, T * H0])
        exps = sb("exps", [P, T * H0, NODES])
        logits_ready, values_ready, shifted, exps_ready = k.sems("l0r", "logits_ready values_ready shifted exps_ready")
        with nc.Block() as block:

            @block.tensor
            def _(pe):
                for t in range(T):
                    mm = nc.tensor.matmul(logits_ps[:, t * H0:(t + 1) * H0, :], k.XT[:, t * P:(t + 1) * P], W("wr"),
                                          start=True, stop=True)
                mm.then_inc(logits_ready, 1)
                for t in range(T):
                    mm = nc.tensor.matmul(values_ps[:, t], k.XT[:, t * P:(t + 1) * P], W("wv"), start=True, stop=True)
                mm.then_inc(values_ready, 1)

            @block.gpsimd
            def _(g):
                nc.gpsimd.memset(values[:, :, :, D0:D0 + 1], 1.0)
                nc.gpsimd.memset(member[:, :, H0:, :], 0.0)
                nc.gpsimd.memset(absent[:, :, H0, :], 0.0)
                nc.gpsimd.memset(before[:, 1, :], 1.0)
                k.gchain(g, nc.gpsimd.memset(before[:, 0, :], 1.0))
                nc.gpsimd.affine_select(out=before[:, 0, :], in_=before[:, 0, :], compare_op=ALU.is_gt, fill=0.0,
                                        base=0, pattern=[[1, P]], channel_multiplier=-1)

            @block.scalar
            def _(act):
                act.wait_ge(shifted, 1)
                nc.scalar.activation(exps[:], exps[:], ACT.Exp).then_inc(exps_ready, 1)
                act.wait_ge(values_ready, 1)
                for t in range(0, T, 2):
                    nc.scalar.copy(values[:, t:t + 2, :, 0:D0].rearrange("p t c d -> p (t c) d"),
                                   values_ps[:, t:t + 2].rearrange("p t c d -> p (t c) d"))

            @block.vector
            def _(v):
                link = k.vchain
                v.wait_ge(logits_ready, 1)
                link(v, nc.vector.tensor_copy(logits[:], logits_ps[:]))
                link(v, nc.vector.tensor_reduce(top[:], logits[:], AX.X, ALU.max))
                nc.vector.tensor_tensor(exps[:], logits[:], bc(top[:].unsqueeze(2), [P, T * H0, NODES]),
                                        ALU.subtract).then_inc(shifted, 1)
                one = bc(logits[:].unsqueeze(3), pairs)
                other = bc(logits[:].unsqueeze(2), pairs)
                link(v, nc.vector.tensor_tensor(greater[:], other, one, ALU.is_gt))
                link(v, nc.vector.tensor_tensor(tied[:], other, one, ALU.is_equal))
                flat = "p a n m -> p a (n m)"
                link(v, nc.vector.tensor_tensor(tied[:].rearrange(flat), tied[:].rearrange(flat),
                                                bc(W("earlier").unsqueeze(1), [P, T * H0, NODES * NODES]), ALU.mult))
                link(v, nc.vector.tensor_tensor(greater[:], greater[:], tied[:], ALU.add))
                link(v, nc.vector.tensor_reduce(rank[:], greater[:], AX.X, ALU.add))
                ranks = rank[:].rearrange("p (t h) n -> p t h n", t=T)
                link(v, nc.vector.tensor_scalar(absent[:, :, 0:H0, :], ranks, 1.5, None, ALU.is_gt))
                link(v, nc.vector.tensor_scalar(member[:, :, 0:H0, :], ranks, 1.5, None, ALU.is_lt))
                link(v, nc.vector.tensor_scalar(rank[:], rank[:], 1.5, None, ALU.is_lt))
                v.wait_ge(exps_ready, 1)
                link(v, nc.vector.tensor_tensor(exps[:], exps[:], rank[:], ALU.mult))
                link(v, nc.vector.tensor_reduce(top[:], exps[:], AX.X, ALU.add))
                link(v, nc.vector.reciprocal(top[:], top[:]))
                link(v, nc.vector.tensor_tensor(
                    mix[:].rearrange("p t h (odd pair) -> p (t h) pair odd", odd=2),
                    exps[:].rearrange("p a (pair odd) -> p a pair odd", odd=2),
                    bc(top[:].unsqueeze(2).unsqueeze(3), [P, T * H0, 2, 2]), ALU.mult))


def l0_attn_heads(k, W, values, member, absent, mix, before, heads_out):
    nc = k.nc
    U = T
    AHEAD = 1
    ROTATIONS = {0: (1, "qk"), 1: (2, "q"), 2: (2, "k"), 3: (3, "q"), 4: (3, "k")}
    NEXT_ROTATIONS = {SINES_AFTER + 1: "q", SINES_AFTER + 2: "k"}
    CHUNKS = [("q", 0), ("k", 0), ("q", 1), ("k", 1)]
    assert U == B + len(CHUNKS)
    LO, HI = slice(0, D0), slice(D0, P)
    with ExitStack() as ctx:
        sb = lambda name, shape, dt=F32: k.sb("l0h_" + name, shape, dt, ctx)
        scores = k.ps("l0h_scores", [P, 2, 2 * BANK], ctx)
        turned = k.ps("l0h_turned", [P, 2 * BANK], ctx)
        out_ps = k.ps("l0h_out_ps", [P, BANK], ctx)
        side_ps = k.ps("l0h_side_ps", [P, BANK], ctx)
        weights = {x: sb("w" + x, [P, P]) for x in "qk"}
        member_next = sb("member_next", [P, T, NODES, D0], BF16)
        absent_now = sb("absent_now", [P, T, NODES], BF16)
        now = {x: sb(x + "_now", [P, 2, N]) for x in "qk"}
        turns = sb("turns", [P, B, 2, BANK])
        nearest = k.centred[:].rearrange("p t n -> p (t n)").rearrange("p (a n) -> p a n", a=2)
        probs_t = k.squared[:].rearrange("p t n -> p (t n)")
        touched = sb("touched", [1, 1])
        trig = sb("trig", [P, B, 2, BANK])
        rotated_now = {x: sb(x + "_rot", [P, 2, 2, S]) for x in "qk"}
        parts = {x: sb(x + "_part", [P, 2, S]) for x in "qk"}
        q_rot, k_rot = rotated_now["q"], rotated_now["k"]
        probs = sb("probs", [P, 2, NODES * S])
        blocked = sb("blocked", [P, 2, NODES, P], BF16)
        top = sb("top", [P, 2, NODES])
        share = sb("share", [P, NODES])
        weighted = sb("weighted", [P, NODES, D0])
        (weights_ready, rows_next, rows_now, pos_ready, turns_copied, turns_ready, trig_ready, chunk_ready,
         chunk_copied, rotated, scores_ready, shifted, exp_ready, turned_ready, turned_copied, out_ready,
         out_used, blocked_ready) = k.sems(
            "l0h", "weights_ready rows_next rows_now pos_ready turns_copied turns_ready trig_ready chunk_ready "
            "chunk_copied rotated scores_ready shifted exp_ready turned_ready turned_copied out_ready out_used "
            "blocked_ready")
        both = [P, 2, S]


        def load_weights_of(g, head):
            for x in "qk":
                nc.gpsimd.tensor_copy(weights[x][:], W("w" + x)[:, bass.ds(head * P, P)]).then_inc(weights_ready, 1)

        def load_rows_next(engine, head):
            engine.tensor_copy(member_next[:], bc(member[:].rearrange("p t h n -> p t (h n)")
                                                     [:, :, bass.ds(head * NODES, NODES)].unsqueeze(3),
                                                     [P, T, NODES, D0])).then_inc(rows_next, 1)

        def load_rows_now(g, head, tiles):
            nc.gpsimd.tensor_copy(absent_now[:, tiles], absent[:].rearrange("p t h n -> p t (h n)")
                                  [:, tiles, bass.ds(head * NODES, NODES)]).then_inc(rows_now, 1)

        def reduce_angles(g, b, before_it):
            if before_it is not None:
                g.wait_ge(turns_ready, before_it)
            nc.gpsimd.tensor_tensor(touched[:], k.ones[0:1, 0:1], k.ones[0:1, 0:1], ALU.mult)
            k.gchain(g, nc.gpsimd.tensor_scalar(nearest, turns[:, b], ROUND, ROUND, ALU.add, ALU.subtract))
            nc.gpsimd.tensor_tensor(turns[:, b], turns[:, b], nearest, ALU.subtract).then_inc(turns_ready, 1)


        def positions(pe, b):
            for pair in range(2):
                at = side_ps[:, pair * S:(pair + 1) * S]
                rows = lambda t: member_next[:, t, 2 * pair:2 * pair + 2, :].rearrange("p n d -> p (n d)")
                nc.tensor.matmul(at, rows(TB * b), before[:].rearrange("p a b -> p (a b)"), start=True, stop=False,
                                 skip_group_check=True)
                mm = nc.tensor.matmul(at[:, P:S], rows(TB * b + 1), before[:, 0, :], start=False, stop=True,
                                      skip_group_check=True)
            mm.then_inc(pos_ready, 1)

        def project(pe, c):
            x, half = CHUNKS[c]
            nc.tensor.matmul(side_ps[:], weights[x][:], k.XT[:, half * BANK:(half + 1) * BANK], start=True, stop=True)\
                .then_inc(chunk_ready, 1)

        def score(pe, h, u):
            b, i = divmod(u, TB)
            width = (i + 1) * P
            for n in range(NODES):
                first = (n % 2) * BANK + (n // 2) * width
                at = scores[:, u % 2, first:first + width]
                for c in range(i):
                    nc.tensor.matmul(at[:, c * P:(c + 1) * P], bc(absent_now[:, TB * b + c, n:n + 1], [P, P]),
                                     k.masker[:], start=(c == 0), stop=False, skip_group_check=True)
                nc.tensor.matmul(at[:, i * P:(i + 1) * P], blocked[:, u % 2, n, :], k.masker[:], start=(i == 0),
                                 stop=False, skip_group_check=True)
                part = (LO, HI)[n % 2]
                mm = nc.tensor.matmul(at, q_rot[part, b % 2, n // 2, i * P:(i + 1) * P],
                                      k_rot[part, b % 2, n // 2, 0:width], start=False, stop=True,
                                      skip_group_check=True)
            mm.then_inc(scores_ready, 1)


        def angles(act, b):
            nc.scalar.activation(turns[:, b, 0, :], side_ps[:], ACT.Identity, scale=W("freq"))
            nc.scalar.activation(turns[:, b, 1, :], side_ps[:], ACT.Identity, scale=W("freq"),
                                 bias=k.quarter[:]).then_inc(turns_copied, 1)

        def sines(act):
            nc.scalar.activation(trig[:, :, 0, :], turns[:, :, 0, :], ACT.Sin, scale=W("sin_scale"))
            nc.scalar.activation(trig[:, :, 1, :], turns[:, :, 1, :], ACT.Sin, scale=TWO_PI).then_inc(trig_ready, 1)

        def take_chunk(act, c):
            x, half = CHUNKS[c]
            for swapped, source in enumerate((LO, HI)):
                for part in (LO, HI):
                    last = nc.scalar.copy(now[x][part, swapped, half * BANK:(half + 1) * BANK], side_ps[source, :])
            last.then_inc(chunk_copied, 1)


        def block_keys(v, h, u):
            nc.vector.tensor_tensor(blocked[:, u % 2], bc(k.above[:].unsqueeze(1), [P, NODES, P]),
                                    bc(absent[:, u].rearrange("p h n -> p (h n)")[:, bass.ds(h * NODES, NODES)]
                                       .unsqueeze(2), [P, NODES, P]), ALU.max).then_inc(blocked_ready, 1)

        def rotate(v, h, b, which):
            if b % 2 == 0:
                v.wait_ge(chunk_copied, h * 4 + b + 2)
            for x in which:
                src = lambda s: bc(now[x][:, s, b * S:(b + 1) * S].unsqueeze(1), both)
                table = lambda s: trig[:, b, s, :].rearrange("p (a s) -> p a s", a=2)
                dst = rotated_now[x][:, b % 2]
                nc.vector.tensor_tensor(parts[x][:], src(1), table(0), ALU.mult)
                k.vchain(v, nc.vector.tensor_tensor(dst, src(0), table(1), ALU.mult))
                nc.vector.tensor_tensor(dst, dst, parts[x][:], ALU.add).then_inc(rotated, 1)

        with nc.Block() as block:

            @block.sync
            def _(sp):
                sp.wait_ge(k.loaded_rest, k.rest_signals)

            @block.gpsimd
            def _(g):
                load_rows_next(nc.gpsimd, 0)
                g.wait_ge(k.loaded_projections, 16)
                load_weights_of(g, 0)
                load_rows_now(g, 0, slice(0, 4))
                load_rows_now(g, 0, slice(4, T))
                g.wait_ge(pos_ready, B)
                load_rows_next(nc.gpsimd, 1)
                for b in range(B):
                    g.wait_ge(turns_copied, b + 1)
                    reduce_angles(g, b, b if b else None)
                with nc.gpsimd.Fori(0, H0) as h:
                    k.gchain.enter(h, B)
                    g.wait_ge(chunk_ready, (h + 1) * 4)
                    load_weights_of(g, h + 1)
                    for b in range(B):
                        g.wait_ge(turns_copied, (h + 1) * B + b + 1)
                        reduce_angles(g, b, (h + 1) * B + b)
                    g.wait_ge(scores_ready, h * U + 4 + AHEAD)
                    load_rows_now(g, h + 1, slice(0, 4))
                    g.wait_ge(scores_ready, (h + 1) * U + AHEAD)
                    load_rows_now(g, h + 1, slice(4, T))
                    k.gchain.leave(H0)

            @block.tensor
            def _(pe):
                for ahead in (scores_ready, turned_ready):
                    pe.sem_inc(ahead, AHEAD)
                pe.wait_ge(rows_next, 1)
                for b in range(B):
                    if b >= 1:
                        pe.wait_ge(turns_copied, b)
                    positions(pe, b)
                pe.wait_ge(turns_copied, B)
                pe.wait_ge(weights_ready, 2)
                for c in range(4):
                    if c >= 1:
                        pe.wait_ge(chunk_copied, c)
                    project(pe, c)
                pe.wait_ge(rotated, 2)
                pe.wait_ge(rows_now, 1)
                pe.wait_ge(blocked_ready, 1)
                score(pe, 0, 0)
                with nc.tensor.Fori(0, KV0) as kv:
                    with nc.tensor.Fori(0, G0) as j:
                        h = kv * G0 + j

                        def weigh(u):
                            b, i = divmod(u, TB)
                            pe.wait_ge(turned_copied, h * U + u + 1)
                            pe.wait_ge(out_used, h * U + u + AHEAD)
                            for n in range(NODES):
                                for c in range(i + 1):
                                    x = n * (i + 1) + c
                                    mm = nc.tensor.matmul(out_ps[:, n * (D0 + 1):(n + 1) * (D0 + 1)],
                                                          probs_t[:, x * P:(x + 1) * P],
                                                          values[:, TB * b + c].rearrange("p c d -> p (c d)")
                                                          [:, bass.ds(kv * (D0 + 1), D0 + 1)],
                                                          start=(c == 0), stop=(c == i))
                            mm.then_inc(out_ready, 1)

                        for u in range(U):
                            if u + 1 < U:
                                if (u + 1) % TB == 0:
                                    pe.wait_ge(rotated, h * (2 * B) + 2 * ((u + 1) // TB + 1))
                                if u + 1 == 4:
                                    pe.wait_ge(rows_now, h * 2 + 2)
                                pe.wait_ge(shifted, h * U + u + AHEAD)
                                pe.wait_ge(blocked_ready, h * U + u + 2)
                                score(pe, h, u + 1)
                            if u >= 1:
                                weigh(u - 1)
                            if u == 0:
                                pe.wait_ge(chunk_copied, (h + 1) * 4)
                                pe.wait_ge(rows_next, h + 2)
                            elif u <= B:
                                pe.wait_ge(turns_copied, (h + 1) * B + u)
                            else:
                                pe.wait_ge(chunk_copied, (h + 1) * 4 + u - B)
                            if u == B:
                                pe.wait_ge(weights_ready, (h + 2) * 2)
                            if u < B:
                                positions(pe, u)
                            else:
                                project(pe, u - B)
                            pe.wait_ge(exp_ready, h * U + u + 1)
                            b, i = divmod(u, TB)
                            for x in range(NODES * (i + 1)):
                                mm = nc.tensor.transpose(turned[:, x * P:(x + 1) * P],
                                                         probs[:, u % 2, x * P:(x + 1) * P], k.ident[:])
                            mm.then_inc(turned_ready, 1)
                        pe.wait_ge(rotated, (h + 1) * (2 * B) + 2)
                        pe.wait_ge(rows_now, h * 2 + 3)
                        pe.wait_ge(shifted, h * U + U - 1 + AHEAD)
                        pe.wait_ge(blocked_ready, (h + 1) * U + 1)
                        score(pe, h + 1, 0)
                        weigh(U - 1)

            @block.scalar
            def _(act):
                for b in range(B):
                    act.wait_ge(pos_ready, b + 1)
                    angles(act, b)
                for c in range(4):
                    act.wait_ge(chunk_ready, c + 1)
                    take_chunk(act, c)
                act.wait_ge(turns_ready, B)
                sines(act)
                with nc.scalar.Fori(0, H0) as h:
                    for u in range(U):
                        cols = NODES * (u % TB + 1) * P
                        act.wait_ge(shifted, h * U + u + 1 + AHEAD)
                        nc.scalar.activation(probs[:, u % 2, 0:cols], probs[:, u % 2, 0:cols], ACT.Exp,
                                             scale=D0 ** -0.5).then_inc(exp_ready, 1)
                        act.wait_ge(turned_ready, h * U + u + 1 + AHEAD)
                        nc.scalar.copy(probs_t[:, 0:cols], turned[:, 0:cols]).then_inc(turned_copied, 1)
                        if u < B:
                            act.wait_ge(pos_ready, (h + 1) * B + u + 1)
                            if u == 0:
                                act.wait_ge(trig_ready, h + 1)
                            angles(act, u)
                        else:
                            act.wait_ge(chunk_ready, (h + 1) * 4 + u - B + 1)
                            act.wait_ge(rotated, h * (2 * B) + (4 if u < B + 2 else 8))
                            take_chunk(act, u - B)
                        if u == SINES_AFTER:
                            act.wait_ge(turns_ready, (h + 2) * B)
                            act.wait_ge(rotated, (h + 1) * (2 * B))
                            sines(act)

            @block.vector
            def _(v):
                link = k.vchain
                for ahead in (shifted, out_used):
                    v.sem_inc(ahead, AHEAD)
                block_keys(v, 0, 0)
                block_keys(v, 0, 1)
                v.wait_ge(trig_ready, 1)
                rotate(v, 0, 0, "qk")
                with nc.vector.Fori(0, H0) as h:
                    link.enter(h, 2 * B + U * 4)

                    def finish(u):
                        v.wait_ge(out_ready, h * U + u + 1)
                        out = out_ps[:, 0:NODES * (D0 + 1)].rearrange("p (n d) -> p n d", n=NODES)
                        link(v, nc.vector.reciprocal(share[:], out[:, :, D0]))
                        link(v, nc.vector.tensor_tensor(share[:], share[:], mix[:, u].rearrange("p h n -> p (h n)")
                                                        [:, bass.ds(h * NODES, NODES)], ALU.mult))
                        link(v, nc.vector.tensor_tensor(weighted[:], out[:, :, 0:D0],
                                                        bc(share[:].unsqueeze(2), [P, NODES, D0]), ALU.mult))
                        nc.vector.tensor_reduce(heads_out[:, u, bass.ds(h * D0, D0)],
                                                weighted[:].rearrange("p n d -> p d n"), AX.X, ALU.add)\
                            .then_inc(out_used, 1)

                    for u in range(U):
                        b, i = divmod(u, TB)
                        cols = NODES * (i + 1) * P
                        banks = scores[:, u % 2].rearrange("p (odd c) -> p odd c", odd=2)[:, :, 0:cols // 2]\
                            .rearrange("p odd (pair w) -> p odd pair w", pair=2)
                        packed = probs[:, u % 2, 0:cols].rearrange("p (odd pair w) -> p odd pair w", odd=2, pair=2)
                        tops = top[:, u % 2].rearrange("p (odd pair) -> p odd pair", odd=2)
                        v.wait_ge(scores_ready, h * U + u + 1 + AHEAD)
                        link(v, nc.vector.tensor_reduce(tops, banks, AX.X, ALU.max))
                        v.wait_ge(turned_ready, h * U + max(u - 1, 0) + AHEAD)
                        nc.vector.tensor_tensor(packed, banks, bc(tops.unsqueeze(3), [P, 2, 2, (i + 1) * P]),
                                                ALU.subtract).then_inc(shifted, 1)
                        block_keys(v, h + (u + 2) // U, (u + 2) % U)
                        if u in ROTATIONS:
                            batch, which = ROTATIONS[u]
                            v.wait_ge(scores_ready, h * U + TB * (batch - 1) + AHEAD)
                            rotate(v, h, batch, which)
                        if u in NEXT_ROTATIONS:
                            v.wait_ge(trig_ready, h + 2)
                            v.wait_ge(scores_ready, h * U + U - TB + AHEAD)
                            rotate(v, h + 1, 0, NEXT_ROTATIONS[u])
                        if u >= 1:
                            finish(u - 1)
                        if u == B + 1:
                            v.wait_ge(pos_ready, (h + 2) * B)
                            load_rows_next(nc.vector, h + 2)
                    finish(U - 1)
                    link.leave(H0)



HX, DX = 16, P // 16


def cross_pack(name):
    pack = Pack(name)
    for key, width in (("wq", P), ("wk", P), ("wv", P), ("wo", P), ("bq", 1), ("bk", 1), ("bv", P), ("bo", P)):
        pack.put(key, width)
    return pack


L0X, L1X = cross_pack("l0_xattn"), cross_pack("l1_xattn")


def l0_xattn_layout(i):
    zero, row = np.zeros((P, 1), np.float32), np.zeros((P, P), np.float32)
    return L0X.build({"wq": i["L0_xattn_w_q"], "wk": i["L0_xattn_w_k"], "wv": i["L0_xattn_w_v"],
                      "wo": i["L0_xattn_w_o"], "bq": zero, "bk": zero, "bv": row, "bo": on_all(i["L0_xattn_b_o"])})


def l1_xattn_layout(i):
    g = lambda key: np.asarray(i["L1_xattn_" + key])
    return L1X.build({"wq": g("Wq").T, "wk": g("Wk").T, "wv": g("Wv").T, "wo": g("Wp").T, "bq": column(g("bq")),
                      "bk": column(g("bk")), "bv": on_all(g("bv")), "bo": on_all(g("bp"))})


def narrow_cross_attention(k, tag, pack, w, mask):
    nc = k.nc
    W = lambda key: pack.view(w, key)
    with ExitStack() as ctx:
        sb = lambda name, shape: k.sb(f"{tag}_{name}", shape, F32, ctx)
        q_t, k_t, v_both = sb("q_t", [P, N]), sb("k_t", [P, B * SC]), sb("v_both", [P, B, P])
        keys = sb("keys", [P, B, HX, SC])
        values = sb("values", [P, B, HX, DX + 1])
        heads_out = sb("heads_out", [P, T, P])

        def all_values(pe, out):
            for b in range(B):
                mm = nc.tensor.matmul(out[:, b * P:(b + 1) * P], k.ctx_twice[:, b].rearrange("p a s -> p (a s)"), W("wv"), start=True, stop=True)
            return mm

        products(k, tag + "_proj", [
            (SCALAR, narrow(k, W("wk"), k.ctx_t[:], B * SC), activated(k, k_t[:], bias=W("bk"), cols=B * SC)),
            (VECTOR, all_values, lambda v, out: nc.vector.tensor_tensor(
                v_both[:], out[:, 0:BANK].rearrange("p (b n) -> p b n", b=B), bc(W("bv").unsqueeze(1), [P, B, P]),
                ALU.add)),
            (SCALAR, wide(k, W("wq"), k.XT), activated(k, q_t[:], bias=W("bq"))),
        ])
        with nc.Block() as block:

            @block.vector
            def _(v):
                for b in range(B):
                    nc.vector.tensor_tensor(keys[:, b], bc(k_t[:, b * SC:(b + 1) * SC].unsqueeze(1), [P, HX, SC]),
                                            bc(k.own_head.unsqueeze(2), [P, HX, SC]), ALU.mult)

            @block.gpsimd
            def _(g):
                parity = bc(k.own_parity.unsqueeze(2), [P, HX, DX])
                for b in range(B):
                    nc.gpsimd.tensor_tensor(values[:, b, :, 0:DX], v_both[:, b].rearrange("p (h d) -> p h d", h=HX),
                                            parity, ALU.mult)
                    nc.gpsimd.tensor_copy(values[:, b, :, DX], k.own_parity)

        def unit(t):
            b = t // TB

            def score(out):
                for c in range(2):
                    mm = nc.tensor.matmul(out[:, c, :], q_t[:, t * P:(t + 1) * P], keys[:, b, c * 8:(c + 1) * 8, :],
                                          start=True, stop=True)
                return mm

            def product(out, probs_t):
                for x in range(8):
                    mm = nc.tensor.matmul(out[:, 2 * x * (DX + 1):2 * (x + 1) * (DX + 1)],
                                          probs_t[:, x * P:(x + 1) * P], values[:, b, 2 * x:2 * x + 2, :],
                                          start=True, stop=True)
                return mm
            return (2 * BANK, HX, score, product, heads_out[:, t].rearrange("p (h d) -> p h d", h=HX),
                    mask(t) if mask else None)

        attention(k, tag + "_att", [unit(t) for t in range(T)], DX ** -0.5)
        close_sublayer(k, tag + "_close", heads_out[:], [W("wo")], 1, bias=W("bo"))


def l0_xattn(k):
    nc = k.nc
    with ExitStack() as ctx:
        keep = k.sb("l0x_keep", [P, TB, SC], F32, ctx)
        add = k.sb("l0x_add", [P, TB, SC], F32, ctx)
        with nc.Block() as block:

            @block.vector
            def _(v):
                k.vchain(v, nc.vector.tensor_scalar(keep[:], k.mask0[:], 0.0, None, ALU.not_equal))
                nc.vector.tensor_scalar(add[:], keep[:], 1.0, 1e9 * DX ** 0.5, ALU.subtract, ALU.mult)
        narrow_cross_attention(k, "l0x", L0X, k.weights["l0_xattn"],
                               lambda t: (keep[:, t % TB, :], add[:, t % TB, :]))


def l1_xattn(k):
    narrow_cross_attention(k, "l1x", L1X, k.weights["l1_xattn"], None)



E0, F0 = 8, 4 * P
L0F = Pack("l0_ffn")
for _key, _width in (("wqkv", 3 * P), ("wo", P), ("gate", E0 + 2), ("bq", 1), ("bk", 1), ("bv", P), ("bo", P),
                     ("g1", P), ("s1", P), ("g2", P), ("s2", P), ("coef_b", 2), ("prio", E0)):
    L0F.put(_key, _width)


def l0_ffn_layout(i):
    g = lambda key: np.asarray(i["L0_ffn_" + key])
    b = g("bqkv")
    return L0F.build({"wqkv": g("Wqkv"), "wo": g("Wo"), "gate": np.concatenate([g("gate_w"), g("coef_w")], axis=1),
                      "bq": column(b[:P]), "bk": column(b[P:2 * P]), "bv": on_all(b[2 * P:]), "bo": on_all(g("bo")),
                      "g1": on_all(g("ln1_g")), "s1": on_all(g("ln1_b")), "g2": on_all(g("ln2_g")),
                      "s2": on_all(g("ln2_b")), "coef_b": on_all(g("coef_b")),
                      "prio": on_all(np.arange(E0, 0, -1, dtype=np.float32))})


def l0_experts_layout(i):
    g = lambda key: np.asarray(i["L0_ffn_" + key])
    out = np.zeros((E0 + 1, P, 2 * F0 + F0 // P + P), np.float32)
    for e in range(E0 + 1):
        w1, b1, w2, b2 = (g(x)[e] for x in ("W1", "b1", "W2", "b2")) if e < E0 else \
            (g(x) for x in ("rW1", "rb1", "rW2", "rb2"))
        out[e, :, 0:F0] = w1
        out[e, :, F0:2 * F0] = tile_rows(w2)
        out[e, :, 2 * F0:2 * F0 + F0 // P] = b1.reshape(F0 // P, P).T
        out[e, :, 2 * F0 + F0 // P:] = on_all(b2)
    return out


def l0_ffn(k):
    nc = k.nc
    w = k.weights["l0_ffn"]
    W = lambda key: L0F.view(w, key)
    with ExitStack() as ctx:
        sb = lambda name, shape, dt=F32: k.sb("l0f_" + name, shape, dt, ctx)
        x_in, xn, xn_t = sb("x_in", [P, T, P]), sb("xn", [P, T, P]), sb("xn_t", [P, N])
        norm_and_turn(k, "l0f_ln1", k.X[:], xn[:], xn_t[:], W("g1"), W("s1"), copy_to=x_in[:])
        with ExitStack() as att:
            q_t, k_t = k.sb("l0f_q_t", [P, N], F32, att), k.sb("l0f_k_t", [P, N], F32, att)
            keys = k.sb("l0f_keys", [P, 4, N], F32, att)
            values = k.sb("l0f_values", [P, T, HX, DX + 1], F32, att)
            heads_out = k.sb("l0f_heads_out", [P, T, P], F32, att)

            def take_values(v, out):
                for t in range(T):
                    ins = nc.vector.tensor_tensor(values[:, t, :, 0:DX], out[:, t * P:(t + 1) * P]
                                                  .rearrange("p (h d) -> p h d", h=HX),
                                                  W("bv").rearrange("p (h d) -> p h d", h=HX), ALU.add)
                return ins

            products(k, "l0f_proj", [
                (SCALAR, wide(k, W("wqkv")[:, P:2 * P], xn_t), activated(k, k_t[:], bias=W("bk"))),
                (VECTOR, by_tile(k, xn_t, W("wqkv")[:, 2 * P:3 * P], P), take_values),
                (SCALAR, wide(k, W("wqkv")[:, 0:P], xn_t), activated(k, q_t[:], bias=W("bq"))),
            ])
            with nc.Block() as block:

                @block.vector
                def _(v):
                    for j in range(4):
                        nc.vector.tensor_scalar(keys[:, j, :], k_t[:], k.own_of_four[:, j:j + 1], None, ALU.mult)

                @block.gpsimd
                def _(g):
                    nc.gpsimd.memset(values[:, :, :, DX:DX + 1], 1.0)

            def unit(t, g):
                rows, b = slice(32 * g, 32 * g + 32), t // TB

                def score(out):
                    for c in range(2):
                        mm = nc.tensor.matmul(out[:, c, :], q_t[rows, t * P:(t + 1) * P],
                                              keys[rows, 2 * c:2 * c + 2, b * S:(b + 1) * S], start=True, stop=True)
                    return mm

                def product(out, probs_t):
                    for j in range(4):
                        for c in range(TB):
                            mm = nc.tensor.matmul(out[:, j * (DX + 1):(j + 1) * (DX + 1)],
                                                  probs_t[:, (2 * j + c) * P:(2 * j + c + 1) * P],
                                                  values[:, TB * b + c, 4 * g + j, :], start=(c == 0), stop=(c == 1))
                    return mm
                return (2 * BANK, 4, score, product,
                        heads_out[:, t, rows].rearrange("p (h d) -> p h d", h=4), None)

            attention(k, "l0f_att", [unit(t, g) for t in range(T) for g in range(4)], DX ** -0.5)
            close_sublayer(k, "l0f_mid", heads_out[:], [W("wo")], 1, bias=W("bo"), to=(xn[:], xn_t[:]),
                           gain=W("g2"), shift=W("s2"))
        weight = sb("weight", [P, T, E0 + 1])
        total = sb("total", [P, T, P])
        l0_ffn_route(k, W, xn_t, weight)
        l0_ffn_experts(k, xn_t, weight, total)
        norm_and_turn(k, "l0f_out", k.X[:], k.X[:], k.XT[:], addends=(x_in[:], total[:]))


def l0_ffn_route(k, W, xn_t, weight):
    nc = k.nc
    with ExitStack() as ctx:
        sb = lambda name, shape: k.sb("l0g_" + name, shape, F32, ctx)
        logits_ps = k.ps("l0g_logits_ps", [P, T, E0 + 2], ctx)
        logits, top, top2, total = sb("logits", [P, T, E0 + 2]), sb("top", [P, T]), sb("top2", [P, T]), sb("total", [P, T])
        exps, chosen, total2, share = (sb("exps", [P, T, E0 + 2]), sb("chosen", [P, T, E0]), sb("total2", [P, T]),
                                       sb("share", [P, T]))
        ready, shifted, exps_ready = k.sems("l0g", "ready shifted exps_ready")
        with nc.Block() as block:

            @block.tensor
            def _(pe):
                for t in range(T):
                    mm = nc.tensor.matmul(logits_ps[:, t, :], xn_t[:, t * P:(t + 1) * P], W("gate"), start=True,
                                          stop=True)
                mm.then_inc(ready, 1)

            @block.scalar
            def _(act):
                act.wait_ge(shifted, 1)
                nc.scalar.activation(exps[:], exps[:], ACT.Exp).then_inc(exps_ready, 1)

            @block.vector
            def _(v):
                link = k.vchain
                experts, coefs = slice(0, E0), slice(E0, E0 + 2)
                e_shape, c_shape = [P, T, E0], [P, T, 2]
                v.wait_ge(ready, 1)
                link(v, nc.vector.tensor_copy(logits[:], logits_ps[:]))
                link(v, nc.vector.tensor_tensor(logits[:, :, coefs], logits[:, :, coefs],
                                                bc(W("coef_b").unsqueeze(1), c_shape), ALU.add))
                link(v, nc.vector.tensor_reduce(top[:], logits[:, :, experts], AX.X, ALU.max))
                link(v, nc.vector.tensor_reduce(top2[:], logits[:, :, coefs], AX.X, ALU.max))
                link(v, nc.vector.tensor_tensor(exps[:, :, coefs], logits[:, :, coefs],
                                                bc(top2[:].unsqueeze(2), c_shape), ALU.subtract))
                nc.vector.tensor_tensor(exps[:, :, experts], logits[:, :, experts], bc(top[:].unsqueeze(2), e_shape),
                                        ALU.subtract).then_inc(shifted, 1)
                link(v, nc.vector.tensor_tensor(chosen[:], logits[:, :, experts], bc(top[:].unsqueeze(2), e_shape),
                                                ALU.is_equal))
                link(v, nc.vector.tensor_tensor(chosen[:], chosen[:], bc(W("prio").unsqueeze(1), e_shape), ALU.mult))
                link(v, nc.vector.tensor_reduce(top[:], chosen[:], AX.X, ALU.max))
                link(v, nc.vector.tensor_tensor(chosen[:], chosen[:], bc(top[:].unsqueeze(2), e_shape), ALU.is_equal))
                v.wait_ge(exps_ready, 1)
                link(v, nc.vector.tensor_reduce(total[:], exps[:, :, experts], AX.X, ALU.add))
                link(v, nc.vector.tensor_reduce(total2[:], exps[:, :, coefs], AX.X, ALU.add))
                link(v, nc.vector.reciprocal(total[:], total[:]))
                link(v, nc.vector.reciprocal(total2[:], total2[:]))
                link(v, nc.vector.tensor_tensor(exps[:, :, coefs], exps[:, :, coefs],
                                                bc(total2[:].unsqueeze(2), c_shape), ALU.mult))
                link(v, nc.vector.tensor_tensor(share[:], total[:], exps[:, :, E0], ALU.mult))
                link(v, nc.vector.tensor_tensor(weight[:, :, experts], chosen[:], bc(share[:].unsqueeze(2), e_shape),
                                                ALU.mult))
                link(v, nc.vector.tensor_copy(weight[:, :, E0], exps[:, :, E0 + 1]))


def l0_ffn_experts(k, xn_t, weight, total):
    nc = k.nc
    CH = F0 // P
    PER, TURNS = 3, (E0 + 1) // 3
    with ExitStack() as ctx:
        sb = lambda name, shape: k.sb("l0e_" + name, shape, F32, ctx)
        hidden_ps = k.ps("l0e_hidden_ps", [P, 4, BANK], ctx)
        out_ps = k.ps("l0e_out_ps", [P, 4, BANK], ctx)
        experts = sb("experts", [P, PER, 2 * F0 + CH + P])
        hidden = sb("hidden", [P, 2, CH, BANK])
        weighted = sb("weighted", [P, 4, P])
        (loaded0, loaded1, loaded2, hidden_ready, gelu_ready, out_ready, out_used) = k.sems(
            "l0e", "loaded0 loaded1 loaded2 hidden_ready gelu_ready out_ready out_used")
        loaded = (loaded0, loaded1, loaded2)
        with nc.Block() as block:

            @block.sync
            def _(sp):
                for j in range(PER):
                    sp.dma_start(experts[:, j, :], k.dram["l0_experts"][j]).then_inc(loaded[j], 16)
                with nc.sync.Fori(1, TURNS) as turn:
                    for j in range(PER):
                        sp.wait_ge(out_ready, (turn * PER + j - PER + 1) * 2)
                        sp.dma_start(experts[:, j, :], k.dram["l0_experts"].rearrange("e p n -> (e p) n")
                                     [bass.ds((turn * PER + j) * P, P), :]).then_inc(loaded[j], 16)

            @block.tensor
            def _(pe):
                with nc.tensor.Fori(0, TURNS) as turn:
                    for j in range(PER):
                        e = turn * PER + j
                        w = experts[:, j, :]
                        pe.wait_ge(loaded[j], (turn + 1) * 16)

                        def up(half):
                            for c in range(CH):
                                if j or half:
                                    pe.wait_ge(gelu_ready, e * 2 * CH + half * CH + c - 2)
                                else:
                                    pe.wait_ge(gelu_ready, turn * (PER * 2 * CH) + 1)
                                nc.tensor.matmul(hidden_ps[:, c, :], w[:, c * P:(c + 1) * P],
                                                 xn_t[:, half * BANK:(half + 1) * BANK], start=True, stop=True)\
                                    .then_inc(hidden_ready, 1)

                        def down(half):
                            pe.wait_ge(gelu_ready, e * 2 * CH + (half + 1) * CH + 1)
                            at = (2 * j + half) % 4
                            pe.wait_ge(out_used, e * 2 + half + (0 if j or half else 1))
                            for t in range(4):
                                for c in range(CH):
                                    nc.tensor.matmul(out_ps[:, at, t * P:(t + 1) * P],
                                                     hidden[:, half, c, t * P:(t + 1) * P],
                                                     w[:, F0 + c * P:F0 + (c + 1) * P], start=(c == 0), stop=False)
                                mm = nc.tensor.matmul(out_ps[:, at, t * P:(t + 1) * P], k.ones[0:1, :],
                                                      w[0:1, 2 * F0 + CH:], start=False, stop=True)
                            mm.then_inc(out_ready, 1)
                        up(0)
                        up(1)
                        down(0)
                        down(1)

            @block.scalar
            def _(act):
                act.sem_inc(gelu_ready, 1)
                with nc.scalar.Fori(0, TURNS) as turn:
                    for j in range(PER):
                        e = turn * PER + j
                        act.wait_ge(loaded[j], (turn + 1) * 16)
                        for half in range(2):
                            for c in range(CH):
                                act.wait_ge(hidden_ready, e * 2 * CH + half * CH + c + 1)
                                nc.scalar.activation(hidden[:, half, c, :], hidden_ps[:, c, :], ACT.Gelu,
                                                     bias=experts[:, j, 2 * F0 + c:2 * F0 + c + 1])\
                                    .then_inc(gelu_ready, 1)

            @block.vector
            def _(v):
                link = k.vchain
                link(v, nc.vector.memset(total[:], 0.0))
                v.sem_inc(out_used, 1)
                with nc.vector.Fori(0, TURNS) as turn:
                    link.enter(turn, PER * 2)
                    for j in range(PER):
                        for half in range(2):
                            n = turn * (PER * 2) + 2 * j + half
                            tiles = slice(4 * half, 4 * half + 4)
                            v.wait_ge(out_ready, n + 1)
                            share = weight[:, tiles, :].rearrange("p t e -> p e t")[:, bass.ds(turn * PER + j, 1), :]
                            nc.vector.tensor_tensor(weighted[:], out_ps[:, (2 * j + half) % 4, :]
                                                    .rearrange("p (t n) -> p t n", n=P),
                                                    bc(share.rearrange("p e t -> p (e t)").unsqueeze(2), [P, 4, P]),
                                                    ALU.mult).then_inc(out_used, 1)
                            v.wait_ge(out_used, n + 2)
                            link(v, nc.vector.tensor_tensor(total[:, tiles, :], total[:, tiles, :], weighted[:],
                                                            ALU.add))
                    link.leave(TURNS)



R1 = 32
L1A = Pack("l1_attn")
for _key, _width in (("wi", P), ("wsin", R1), ("wd", R1), ("wsel", R1), ("wso", P), ("wg", P), ("wout", P),
                     ("ln_g", 1), ("ln_b", 1), ("mix_w", 3), ("mix_b", 1), ("bi", 1), ("bsin", 1), ("bd", 1),
                     ("bsel", 1), ("bso", 1), ("bg", 1), ("bout", P)):
    L1A.put(_key, _width)


def l1_attn_layout(i):
    g = lambda key: np.asarray(i["L1_attn_" + key])
    parts = {x: column(g(x)) for x in ("ln_g", "ln_b", "mix_b", "bi", "bsin", "bd", "bsel", "bso", "bg")}
    parts.update({x.lower(): g(x) for x in ("Wi", "Wsin", "Wd", "Wsel", "Wso", "Wg", "Wout")})
    return L1A.build({**parts, "mix_w": g("mix_w").reshape(P, 3), "bout": on_all(g("bout"))})


def l1_attn(k):
    nc = k.nc
    w = k.weights["l1_attn"]
    W = lambda key: L1A.view(w, key)
    with ExitStack() as ctx:
        sb = lambda name, shape, dt=F32: k.sb("l1a_" + name, shape, dt, ctx)
        xn, h_t, mixed = sb("xn", [P, T, P]), sb("h_t", [P, B, S + 2]), sb("mixed", [P, B, S])
        u, gate, out_t = sb("u", [P, N]), sb("gate", [P, N]), sb("out_t", [P, N])
        x_state, decay, select, states = (sb(x, [R1, N]) for x in ("x_state", "decay", "select", "states"))

        norm_and_turn(k, "l1a_ln", k.X[:], xn[:], None, on_turned=lambda act, i, out: nc.scalar.activation(
            h_t[:, 2 * i:2 * i + 2, 1:S + 1], out.rearrange("p (b s) -> p b s", b=2), ACT.Identity, bias=W("ln_b"),
            scale=W("ln_g")))
        with nc.Block() as block:

            @block.vector
            def _(v):
                link = k.vchain
                nc.vector.memset(h_t[:, :, 0:1], 0.0)
                link(v, nc.vector.memset(h_t[:, :, S + 1:S + 2], 0.0))
                link(v, nc.vector.tensor_scalar(mixed[:], h_t[:, :, 0:S], W("mix_w")[:, 0:1], W("mix_b"), ALU.mult,
                                                ALU.add))
                for tap in (1, 2):
                    link(v, nc.vector.scalar_tensor_tensor(mixed[:], h_t[:, :, tap:tap + S],
                                                           W("mix_w")[:, tap:tap + 1], mixed[:], ALU.mult, ALU.add))
        mixed_t = mixed[:].rearrange("p b s -> p (b s)")
        small = lambda key: W(key)[0:R1, :]
        products(k, "l1a_proj", [
            (SCALAR, wide(k, W("wsin"), mixed_t, R1), activated(k, x_state[:], ACT.Tanh, small("bsin"), R1)),
            (SCALAR, wide(k, W("wd"), mixed_t, R1), activated(k, decay[:], ACT.Sigmoid, small("bd"), R1)),
            (SCALAR, wide(k, W("wsel"), mixed_t, R1), activated(k, select[:], ACT.Sigmoid, small("bsel"), R1)),
            (SCALAR, wide(k, W("wi"), mixed_t), activated(k, u[:], ACT.Tanh, W("bi"))),
            (SCALAR, wide(k, W("wg"), mixed_t), activated(k, gate[:], ACT.Sigmoid, W("bg"))),
        ])
        with nc.Block() as block:

            @block.vector
            def _(v):
                link = k.vchain
                link(v, nc.vector.tensor_scalar(states[:], decay[:], -1.0, 1.0, ALU.mult, ALU.add))
                link(v, nc.vector.tensor_tensor(x_state[:], states[:], x_state[:], ALU.mult))
                for b in range(B):
                    one = slice(b * S, (b + 1) * S)
                    link(v, nc.vector.tensor_tensor_scan(states[:, one], decay[:, one], x_state[:, one], 0.0,
                                                         ALU.mult, ALU.add))
                link(v, nc.vector.tensor_tensor(states[:], states[:], select[:], ALU.mult))

        def blend(v, out):
            k.vchain(v, nc.vector.scalar_tensor_tensor(out_t[:], out, W("bso"), u[:], ALU.add, ALU.subtract))
            k.vchain(v, nc.vector.tensor_tensor(out_t[:], out_t[:], gate[:], ALU.mult))
            return nc.vector.tensor_tensor(out_t[:], out_t[:], u[:], ALU.add)
        products(k, "l1a_y", [(VECTOR, wide(k, small("wso"), states), blend)])
        close_sublayer(k, "l1a_close", None, [W("wout")], 1, bias=W("bout"), doubled=True, features_t=[out_t])



E1, F1, FS = 16, 4 * P, 2 * P
CAP = N * 2 // E1
assert CAP == P
L1F = Pack("l1_ffn")
for _key, _width in (("gate", E1), ("sg", FS), ("su", FS), ("sd", FS), ("slot_number", P)):
    L1F.put(_key, _width)


def l1_ffn_layout(i):
    g = lambda key: np.asarray(i["L1_ffn_" + key])
    return L1F.build({"gate": g("gate_w").T, "sg": g("Sg").T, "su": g("Su").T, "sd": tile_rows(g("Sd").T),
                      "slot_number": on_all(np.arange(P, dtype=np.float32))})


def l1_experts_layout(i):
    g = lambda key: np.asarray(i["L1_ffn_" + key])
    wd = g("Wd").transpose(0, 2, 1).reshape(E1, F1 // P, P, P).transpose(0, 2, 1, 3).reshape(E1, P, F1)
    return np.ascontiguousarray(np.concatenate([g("Wg").transpose(0, 2, 1), g("Wu").transpose(0, 2, 1), wd], axis=2))


def l1_ffn(k):
    nc = k.nc
    w = k.weights["l1_ffn"]
    W = lambda key: L1F.view(w, key)
    with ExitStack() as ctx:
        sb = lambda name, shape, dt=F32: k.sb("l1f_" + name, shape, dt, ctx)
        probs = sb("probs", [P, T, E1 + 2])
        slot = sb("slot", [P, T, E1 + 2])
        total = sb("total", [P, T, P])
        l1_ffn_route(k, W, probs, slot)
        l1_ffn_experts(k, W, probs, slot, total)
        act_part, shared = sb("act_part", [P, 2, N]), sb("shared", [P, 2, N])
        products(k, "l1f_sg", [(SCALAR, wide(k, W("sg")[:, c * P:(c + 1) * P], k.XT),
                                activated(k, act_part[:, c, :], ACT.Gelu)) for c in range(2)])

        def gated(c):
            return lambda v, out: nc.vector.tensor_tensor(shared[:, c, :], out, act_part[:, c, :], ALU.mult)
        products(k, "l1f_su", [(VECTOR, wide(k, W("su")[:, c * P:(c + 1) * P], k.XT), gated(c)) for c in range(2)])
        close_sublayer(k, "l1f_close", None, [W("sd")[:, c * P:(c + 1) * P] for c in range(2)], 2,
                       features_t=[shared[:, 0, :], shared[:, 1, :]], addend=total[:])


def l1_ffn_route(k, W, probs, slot):
    nc = k.nc
    with ExitStack() as ctx:
        sb = lambda name, shape: k.sb("l1r_" + name, shape, F32, ctx)
        logits_ps = k.ps("l1r_logits_ps", [P, T, E1], ctx)
        by_expert_ps = k.ps("l1r_by_expert_ps", [E1, N], ctx)
        slot_ps = k.ps("l1r_slot_ps", [P, T, E1], ctx)
        top, exps = sb("top", [P, T]), sb("exps", [P, T, E1])
        left, best, chosen, place = sb("left", [E1, N]), sb("best", [E1, 8]), sb("chosen", [E1, N]), sb("place", [E1, N])
        ready, shifted, exps_ready, probs_ready, turned_ready, places_ready, slots_ready = k.sems(
            "l1r", "ready shifted exps_ready probs_ready turned_ready places_ready slots_ready")
        full = [P, T, E1]
        with nc.Block() as block:

            @block.tensor
            def _(pe):
                for t in range(T):
                    mm = nc.tensor.matmul(logits_ps[:, t, :], k.XT[:, t * P:(t + 1) * P], W("gate"), start=True,
                                          stop=True)
                mm.then_inc(ready, 1)
                pe.wait_ge(probs_ready, 1)
                for t in range(T):
                    mm = nc.tensor.transpose(by_expert_ps[:, t * P:(t + 1) * P], exps[:, t, :], k.ident[:])
                mm.then_inc(turned_ready, 1)
                pe.wait_ge(places_ready, 1)
                for t in range(T):
                    mm = nc.tensor.transpose(slot_ps[:, t, :], place[:, t * P:(t + 1) * P], k.ident[0:E1, 0:E1])
                mm.then_inc(slots_ready, 1)

            @block.scalar
            def _(act):
                act.wait_ge(shifted, 1)
                nc.scalar.activation(exps[:], exps[:], ACT.Exp).then_inc(exps_ready, 1)

            @block.vector
            def _(v):
                link = k.vchain
                nc.vector.memset(probs[:, :, E1:], 0.0)
                nc.vector.memset(slot[:, :, E1:], -1.0)
                v.wait_ge(ready, 1)
                link(v, nc.vector.tensor_reduce(top[:], logits_ps[:], AX.X, ALU.max))
                nc.vector.tensor_tensor(exps[:], logits_ps[:], bc(top[:].unsqueeze(2), full), ALU.subtract)\
                    .then_inc(shifted, 1)
                v.wait_ge(exps_ready, 1)
                link(v, nc.vector.tensor_reduce(top[:], exps[:], AX.X, ALU.add))
                link(v, nc.vector.reciprocal(top[:], top[:]))
                nc.vector.tensor_tensor(exps[:], exps[:], bc(top[:].unsqueeze(2), full), ALU.mult)\
                    .then_inc(probs_ready, 1)
                v.wait_ge(probs_ready, 1)
                nc.vector.tensor_copy(probs[:, :, 0:E1], exps[:])
                v.wait_ge(turned_ready, 1)
                link(v, nc.vector.tensor_copy(left[:], by_expert_ps[:]))
                for _ in range(CAP // 8):
                    link(v, nc.vector.max(best[:], left[:]))
                    link(v, nc.vector.match_replace(left[:], best[:], left[:], -1.0))
                link(v, nc.vector.tensor_scalar(chosen[:], left[:], 0.0, None, ALU.is_lt))
                link(v, nc.vector.tensor_tensor_scan(place[:], chosen[:], chosen[:], 0.0, ALU.add, ALU.max))
                link(v, nc.vector.tensor_tensor(place[:], place[:], chosen[:], ALU.mult))
                nc.vector.tensor_scalar(place[:], place[:], 1.0, None, ALU.subtract).then_inc(places_ready, 1)
                v.wait_ge(slots_ready, 1)
                link(v, nc.vector.tensor_copy(slot[:, :, 0:E1], slot_ps[:]))


def l1_ffn_experts(k, W, probs, slot, total):
    nc = k.nc
    CH, PER = F1 // P, 2
    TURNS = E1 // PER
    with ExitStack() as ctx:
        sb = lambda name, shape: k.sb("l1e_" + name, shape, F32, ctx)
        ps = lambda name, shape: k.ps("l1e_" + name, shape, ctx)
        turned_ps, gathered_ps, gate_ps = ps("turned_ps", [P, N]), ps("gathered_ps", [P, BANK]), ps("gate_ps", [P, BANK])
        up_ps, out_ps, scattered_ps = ps("up_ps", [P, BANK]), ps("out_ps", [P, BANK]), ps("scattered_ps", [P, T, P])
        experts = sb("experts", [P, PER, 3 * F1])
        onehot = sb("onehot", [P, 2, T, P])
        onehot_t = sb("onehot_t", [P, 2, N])
        gathered, act_part, hidden = sb("gathered", [P, P]), sb("act_part", [P, F1]), sb("hidden", [P, F1])
        out, weighted = sb("out", [P, P]), sb("weighted", [P, T, P])
        (loaded0, loaded1, onehot_ready, turned_ready, turned_copied, gathered_ready, gathered_copied, up_ready,
         gelu_ready, hidden_ready, out_ready, out_copied, scattered_ready, scattered_used) = k.sems(
            "l1e", "loaded0 loaded1 onehot_ready turned_ready turned_copied gathered_ready gathered_copied up_ready "
            "gelu_ready hidden_ready out_ready out_copied scattered_ready scattered_used")
        loaded = (loaded0, loaded1)

        def gather(pe, e, buffer):
            pe.wait_ge(onehot_ready, e + 1)
            pe.wait_ge(gathered_copied, e + 1)
            for t in range(T):
                mm = nc.tensor.matmul(gathered_ps[:, 0:P], k.X[:, t, :], onehot[:, buffer, t, :], start=(t == 0),
                                      stop=(t == T - 1))
            mm.then_inc(gathered_ready, 1)
            pe.wait_ge(turned_copied, e + 1)
            for t in range(T):
                mm = nc.tensor.transpose(turned_ps[:, t * P:(t + 1) * P], onehot[:, buffer, t, :], k.ident[:])
            mm.then_inc(turned_ready, 1)

        def take_gathered(act, e, buffer, first=False):
            act.wait_ge(gathered_ready, e + 1)
            act.wait_ge(up_ready, e + 1)
            nc.scalar.copy(gathered[:], gathered_ps[:, 0:P]).then_inc(gathered_copied, 1)
            act.wait_ge(turned_ready, e + 1)
            if not first:
                act.wait_ge(scattered_ready, e)
            nc.scalar.copy(onehot_t[:, buffer, :], turned_ps[:]).then_inc(turned_copied, 1)

        def make_onehot(v, e, buffer):
            nc.vector.tensor_tensor(onehot[:, buffer], bc(W("slot_number").unsqueeze(1), [P, T, P]),
                                    bc(slot[:, :, bass.ds(e, 1)], [P, T, P]), ALU.is_equal).then_inc(onehot_ready, 1)

        with nc.Block() as block:

            @block.sync
            def _(sp):
                for j in range(PER):
                    sp.dma_start(experts[:, j, :], k.dram["l1_experts"][j]).then_inc(loaded[j], 16)
                with nc.sync.Fori(1, TURNS) as turn:
                    for j in range(PER):
                        sp.wait_ge(out_ready, turn * PER + j - PER + 1)
                        sp.dma_start(experts[:, j, :], k.dram["l1_experts"].rearrange("e p n -> (e p) n")
                                     [bass.ds((turn * PER + j) * P, P), :]).then_inc(loaded[j], 16)

            @block.tensor
            def _(pe):
                pe.sem_inc(up_ready, 1)
                pe.sem_inc(scattered_ready, 1)
                gather(pe, 0, 0)
                with nc.tensor.Fori(0, TURNS) as turn:
                    for j in range(PER):
                        e = turn * PER + j
                        pe.wait_ge(loaded[j], (turn + 1) * 16)
                        pe.wait_ge(gathered_copied, e + 2)
                        pe.wait_ge(hidden_ready, e + 1)
                        for at, first in ((gate_ps, 0), (up_ps, F1)):
                            for c in range(CH):
                                mm = nc.tensor.matmul(at[:, c * P:(c + 1) * P],
                                                      experts[:, j, first + c * P:first + (c + 1) * P], gathered[:],
                                                      start=True, stop=True)
                        mm.then_inc(up_ready, 1)
                        gather(pe, e + 1, 1 - j)
                        pe.wait_ge(hidden_ready, e + 2)
                        pe.wait_ge(out_copied, e + 1)
                        for c in range(CH):
                            mm = nc.tensor.matmul(out_ps[:, 0:P], hidden[:, c * P:(c + 1) * P],
                                                  experts[:, j, 2 * F1 + c * P:2 * F1 + (c + 1) * P],
                                                  start=(c == 0), stop=(c == CH - 1))
                        mm.then_inc(out_ready, 1)
                        pe.wait_ge(out_copied, e + 2)
                        pe.wait_ge(scattered_used, e + 1)
                        for t in range(T):
                            mm = nc.tensor.matmul(scattered_ps[:, t, :], onehot_t[:, j, t * P:(t + 1) * P], out[:],
                                                  start=True, stop=True)
                        mm.then_inc(scattered_ready, 1)

            @block.scalar
            def _(act):
                act.sem_inc(gathered_copied, 1)
                act.sem_inc(turned_copied, 1)
                act.sem_inc(out_copied, 1)
                take_gathered(act, 0, 0, first=True)
                with nc.scalar.Fori(0, TURNS) as turn:
                    for j in range(PER):
                        e = turn * PER + j
                        act.wait_ge(up_ready, e + 2)
                        act.wait_ge(hidden_ready, e + 1)
                        nc.scalar.activation(act_part[:], gate_ps[:], ACT.Gelu).then_inc(gelu_ready, 1)
                        take_gathered(act, e + 1, 1 - j)
                        act.wait_ge(out_ready, e + 1)
                        act.wait_ge(scattered_ready, e + 1)
                        nc.scalar.copy(out[:], out_ps[:, 0:P]).then_inc(out_copied, 1)

            @block.vector
            def _(v):
                link = k.vchain
                v.sem_inc(hidden_ready, 1)
                v.sem_inc(scattered_used, 1)
                link(v, nc.vector.memset(total[:], 0.0))
                make_onehot(v, 0, 0)
                make_onehot(v, 1, 1)
                with nc.vector.Fori(0, TURNS) as turn:
                    link.enter(turn, PER)
                    for j in range(PER):
                        e = turn * PER + j
                        v.wait_ge(gelu_ready, e + 1)
                        nc.vector.tensor_tensor(hidden[:], act_part[:], up_ps[:], ALU.mult).then_inc(hidden_ready, 1)
                        v.wait_ge(turned_ready, e + 1)
                        make_onehot(v, e + 2, j)
                        v.wait_ge(scattered_ready, e + 2)
                        nc.vector.tensor_tensor(weighted[:], scattered_ps[:], bc(probs[:, :, bass.ds(e, 1)], [P, T, P]),
                                                ALU.mult).then_inc(scattered_used, 1)
                        v.wait_ge(scattered_used, e + 2)
                        link(v, nc.vector.tensor_tensor(total[:], total[:], weighted[:], ALU.add))
                    link.leave(TURNS)



L2A = Pack("l2_attn")
for _key, _width in (("wqkv", 3 * P), ("wout", P)):
    L2A.put(_key, _width)


def l2_attn_layout(i):
    return L2A.build({"wqkv": np.asarray(i["L2_attn_W_qkv"]).T, "wout": np.asarray(i["L2_attn_W_out"]).T})


def l2_attn(k):
    nc = k.nc
    w = k.weights["l2_attn"]
    W = lambda key: L2A.view(w, key)
    with ExitStack() as ctx:
        sb = lambda name, shape, dt=F32: k.sb("l2a_" + name, shape, dt, ctx)
        q, q_t, k_t, values = sb("q", [P, T, P]), sb("q_t", [P, N]), sb("k_t", [P, N]), sb("values", [P, T, P])
        running, queries, heads_out = sb("running", [P, N]), sb("queries", [P, 4, N]), sb("heads_out", [P, T, P])
        top, ktop = sb("top", [P, T * HX]), sb("ktop", [P, B])
        seen = sb("seen", [P, P])
        products(k, "l2a_proj", [
            (VECTOR, wide(k, W("wqkv")[:, P:2 * P], k.XT), lambda v, out: nc.vector.tensor_copy(k_t[:], out)),
            (SCALAR, by_tile(k, k.XT, W("wqkv")[:, 0:P], P),
             lambda act, out: nc.scalar.copy(q[:].rearrange("p t n -> p (t n)"), out)),
            (SCALAR, by_tile(k, k.XT, W("wqkv")[:, 2 * P:3 * P], P),
             lambda act, out: nc.scalar.copy(values[:].rearrange("p t n -> p (t n)"), out)),
        ])
        with ExitStack() as inner:
            q_ps = k.ps("l2a_q_ps", [P, N], inner)
            q_shifted, q_exp, k_shifted, k_exp, q_soft, q_turned = k.sems(
                "l2a", "q_shifted q_exp k_shifted k_exp q_soft q_turned")
            heads = q[:].rearrange("p t (h d) -> p (t h) d", h=HX)
            with nc.Block() as block:

                @block.vector
                def _(v):
                    link = k.vchain
                    link(v, nc.vector.tensor_reduce(top[:], heads, AX.X, ALU.max))
                    nc.vector.tensor_tensor(heads, heads, bc(top[:].unsqueeze(2), [P, T * HX, DX]), ALU.subtract)\
                        .then_inc(q_shifted, 1)
                    batches = k_t[:].rearrange("p (b s) -> p b s", b=B)
                    link(v, nc.vector.tensor_reduce(ktop[:], batches, AX.X, ALU.max))
                    nc.vector.tensor_tensor(batches, batches, bc(ktop[:].unsqueeze(2), [P, B, S]), ALU.subtract)\
                        .then_inc(k_shifted, 1)
                    v.wait_ge(q_exp, 1)
                    link(v, nc.vector.tensor_reduce(top[:], heads, AX.X, ALU.add))
                    link(v, nc.vector.reciprocal(top[:], top[:]))
                    link(v, nc.vector.tensor_scalar(top[:], top[:], DX ** -0.5, None, ALU.mult))
                    nc.vector.tensor_tensor(heads, heads, bc(top[:].unsqueeze(2), [P, T * HX, DX]), ALU.mult)\
                        .then_inc(q_soft, 1)
                    v.wait_ge(k_exp, 1)
                    for b in range(B):
                        one = slice(b * S, (b + 1) * S)
                        link(v, nc.vector.tensor_tensor_scan(running[:, one], k_t[:, one], k_t[:, one], 0.0, ALU.add,
                                                             ALU.max))
                    link(v, nc.vector.tensor_scalar(running[:], running[:], 1e-9, None, ALU.add))
                    link(v, nc.vector.reciprocal(running[:], running[:]))
                    v.wait_ge(q_turned, 1)
                    link(v, nc.vector.tensor_tensor(q_t[:], q_ps[:], running[:], ALU.mult))
                    for j in range(4):
                        link(v, nc.vector.tensor_scalar(queries[:, j, :], q_t[:], k.own_of_four[:, j:j + 1], None,
                                                        ALU.mult))

                @block.scalar
                def _(act):
                    act.wait_ge(q_shifted, 1)
                    nc.scalar.activation(q[:], q[:], ACT.Exp).then_inc(q_exp, 1)
                    act.wait_ge(k_shifted, 1)
                    nc.scalar.activation(k_t[:], k_t[:], ACT.Exp).then_inc(k_exp, 1)

                @block.tensor
                def _(pe):
                    pe.wait_ge(q_soft, 1)
                    for t in range(T):
                        mm = nc.tensor.transpose(q_ps[:, t * P:(t + 1) * P], q[:, t, :], k.ident[:])
                    mm.then_inc(q_turned, 1)

                @block.gpsimd
                def _(g):
                    k.gchain(g, nc.gpsimd.memset(seen[:], 1.0))
                    nc.gpsimd.affine_select(out=seen[:], in_=seen[:], compare_op=ALU.is_ge, fill=0.0,
                                            base=0, pattern=[[1, P]], channel_multiplier=-1)

        cross = sb("cross", [P, B, P])
        l2_attn_cross(k, k_t, q_t, values, cross)
        with ExitStack() as inner:
            weights_ps = k.ps("l2a_weights_ps", [P, 2, TB, 4, P], inner)
            out_ps = k.ps("l2a_out_ps", [P, 2, BANK], inner)
            weights = k.sb("l2a_weights", [P, 2, TB, 4, P], F32, inner)
            ready, masked, out_ready, out_used = k.sems("l2u", "ready masked out_ready out_used")
            units = [(b, g) for b in range(B) for g in range(4)]
            out_of = lambda n: out_ps[:, n % 2, 0:TB * 4 * DX]
            with nc.Block() as block:

                @block.tensor
                def _(pe):
                    def weigh(n):
                        b, g = units[n]
                        rows = slice(32 * g, 32 * g + 32)
                        if n >= 2:
                            pe.wait_ge(masked, n - 1)
                        for i in range(TB):
                            tile = slice((TB * b + i) * P, (TB * b + i + 1) * P)
                            mm = nc.tensor.matmul(weights_ps[:, n % 2, i], k_t[rows, tile], queries[rows, :, tile],
                                                  start=True, stop=True)
                        mm.then_inc(ready, 1)
                    weigh(0)
                    for n, (b, g) in enumerate(units):
                        if n + 1 < len(units):
                            weigh(n + 1)
                        pe.wait_ge(masked, n + 1)
                        if n >= 2:
                            pe.wait_ge(out_used, n - 1)
                        for i in range(TB):
                            for j in range(4):
                                mm = nc.tensor.matmul(out_of(n)[:, (i * 4 + j) * DX:(i * 4 + j + 1) * DX],
                                                      weights[:, n % 2, i, j, :],
                                                      values[:, TB * b + i, (4 * g + j) * DX:(4 * g + j + 1) * DX],
                                                      start=True, stop=True)
                        mm.then_inc(out_ready, 1)

                @block.vector
                def _(v):
                    for n in range(len(units)):
                        v.wait_ge(ready, n + 1)
                        if n >= 2:
                            v.wait_ge(out_ready, n - 1)
                        nc.vector.tensor_tensor(weights[:, n % 2].rearrange("p i j t -> p (i j) t"),
                                                weights_ps[:, n % 2].rearrange("p i j t -> p (i j) t"),
                                                bc(seen[:].unsqueeze(1), [P, TB * 4, P]), ALU.mult).then_inc(masked, 1)

                @block.scalar
                def _(act):
                    for n, (b, g) in enumerate(units):
                        act.wait_ge(out_ready, n + 1)
                        nc.scalar.copy(heads_out[:, TB * b:TB * b + TB, 32 * g:32 * g + 32],
                                       out_of(n).rearrange("p (i c) -> p i c", i=TB)).then_inc(out_used, 1)
        with nc.Block() as block:

            @block.vector
            def _(v):
                second = heads_out[:].rearrange("p (b i) n -> p b i n", i=TB)[:, :, TB - 1, :]
                nc.vector.tensor_tensor(second, second, cross[:], ALU.add)
        close_sublayer(k, "l2a_close", heads_out[:], [W("wout")], 1)


def l2_attn_cross(k, k_t, q_t, values, cross):
    assert TB == 2
    nc = k.nc
    with ExitStack() as ctx:
        rows_ps, state_ps, cross_ps = (k.ps("l2c_" + x, [P, B, P], ctx) for x in ("rows_ps", "state_ps", "cross_ps"))
        rows, state = (k.sb("l2c_" + x, [P, B, P], F32, ctx) for x in ("rows", "state"))
        turned, rows_ready, products_ready, state_ready, cross_ready = k.sems(
            "l2c", "turned rows_ready products_ready state_ready cross_ready")
        with nc.Block() as block:

            @block.tensor
            def _(pe):
                for b in range(B):
                    mm = nc.tensor.transpose(rows_ps[:, b, :], k_t[:, b * S:b * S + P], k.ident[:])
                mm.then_inc(turned, 1)
                pe.wait_ge(rows_ready, 1)
                for b in range(B):
                    mm = nc.tensor.matmul(state_ps[:, b, :], rows[:, b, :], values[:, TB * b, :], start=True, stop=True)
                mm.then_inc(products_ready, 1)
                pe.wait_ge(state_ready, 1)
                for b in range(B):
                    mm = nc.tensor.matmul(cross_ps[:, b, :], q_t[:, b * S + P:(b + 1) * S], state[:, b, :], start=True,
                                          stop=True)
                mm.then_inc(cross_ready, 1)

            @block.scalar
            def _(act):
                act.wait_ge(turned, 1)
                nc.scalar.copy(rows[:], rows_ps[:]).then_inc(rows_ready, 1)
                act.wait_ge(cross_ready, 1)
                nc.scalar.copy(cross[:], cross_ps[:])

            @block.vector
            def _(v):
                v.wait_ge(products_ready, 1)
                for b in range(B):
                    last = nc.vector.tensor_tensor(state[:, b, :].rearrange("p (h d) -> p h d", h=HX),
                                                   state_ps[:, b, :].rearrange("p (h d) -> p h d", h=HX),
                                                   bc(k.own_head.unsqueeze(2), [P, HX, DX]), ALU.mult)
                last.then_inc(state_ready, 1)



L2X = Pack("l2_xattn")
for _key, _width in (("w1", 1), ("w2", 1), ("w3", 1), ("b_sim", 1), ("w_qv", 4 * P), ("b_qv", P)):
    L2X.put(_key, _width)


def l2_xattn_layout(i):
    g = lambda key: np.asarray(i["L2_xattn_" + key])
    w = g("w_sim").reshape(3, P)
    return L2X.build({"w1": column(w[0]), "w2": column(w[1]), "w3": column(w[2]), "b_sim": on_all(g("b_sim")),
                      "w_qv": tile_rows(g("W_qv")), "b_qv": on_all(g("b_qv"))})


def l2_xattn(k):
    nc = k.nc
    w = k.weights["l2_xattn"]
    W = lambda key: L2X.view(w, key)
    with ExitStack() as ctx:
        sb = lambda name, shape, dt=F32: k.sb("l2x_" + name, shape, dt, ctx)
        keys = sb("keys", [P, B * SC])
        w2_all = sb("w2_all", [P, P])
        sim, weights_t = sb("sim", [P, T, SC]), sb("weights_t", [SC, N])
        top, total = sb("top", [P, T]), sb("total", [P, T])
        tops_t, top8, tops_row, tops_pair = sb("tops_t", [T, P]), sb("top8", [T, 1]), sb("tops_row", [1, T]), sb("tops_pair", [1, B, TB])
        back, pooled, share = sb("back", [P, T]), sb("pooled", [P, B]), sb("share", [P, B])
        attended, product_t, pooled_t = sb("attended", [P, N]), sb("product_t", [P, N]), sb("pooled_t", [P, N])
        psum = ctx.enter_context(ExitStack())
        sim_ps = k.ps("l2x_sim_ps", [P, T, SC], psum)
        turned_ps = k.ps("l2x_turned_ps", [SC, N], psum)
        attended_ps = k.ps("l2x_attended_ps", [P, N], psum)
        small_ps = k.ps("l2x_small_ps", [P, 3, BANK], psum)
        (keys_ready, sim_ready, sim_taken, shifted, exp_ready, soft_ready, turned_ready, turned_copied,
         attended_ready, tops_turned, tops_reduced, row_ready, pairs_ready, spread_ready, back_shifted, back_exp,
         pooled_ready) = k.sems(
            "l2x", "keys_ready sim_ready sim_taken shifted exp_ready soft_ready turned_ready turned_copied "
            "attended_ready tops_turned tops_reduced row_ready pairs_ready spread_ready back_shifted back_exp "
            "pooled_ready")
        full = [P, T, SC]
        with nc.Block() as block:

            @block.tensor
            def _(pe):
                pe.wait_ge(keys_ready, 1)
                for t in range(T):
                    b = t // TB
                    nc.tensor.matmul(sim_ps[:, t, :], k.XT[:, t * P:(t + 1) * P], keys[:, b * SC:(b + 1) * SC],
                                     start=True, stop=False)
                    mm = nc.tensor.matmul(sim_ps[:, t, :], w2_all[:], k.ctx_t[:, b * SC:(b + 1) * SC], start=False,
                                          stop=True)
                mm.then_inc(sim_ready, 1)
                pe.wait_ge(sim_taken, 1)
                nc.tensor.transpose(small_ps[0:T, 0, 0:P], top[:], k.ident[:]).then_inc(tops_turned, 1)
                pe.wait_ge(tops_reduced, 1)
                nc.tensor.transpose(small_ps[0:1, 1, 0:T], top8[:], k.ident[0:T, 0:T]).then_inc(row_ready, 1)
                pe.wait_ge(pairs_ready, 1)
                nc.tensor.matmul(small_ps[:, 2, 0:T], k.ones[0:1, :], tops_pair[:].rearrange("p b i -> p (b i)"),
                                 start=True, stop=True).then_inc(spread_ready, 1)
                pe.wait_ge(soft_ready, 1)
                for t in range(T):
                    mm = nc.tensor.transpose(turned_ps[:, t * P:(t + 1) * P], sim[:, t, :], k.ident[:])
                mm.then_inc(turned_ready, 1)
                pe.wait_ge(turned_copied, 1)
                for b in range(B):
                    mm = nc.tensor.matmul(attended_ps[:, b * S:(b + 1) * S], k.ctx_rows[:, b, :],
                                          weights_t[:, b * S:(b + 1) * S], start=True, stop=True)
                mm.then_inc(attended_ready, 1)
                pe.wait_ge(back_exp, 1)
                for b in range(B):
                    for i in range(TB):
                        nc.tensor.matmul(small_ps[:, 0, b:b + 1], k.X[:, TB * b + i, :],
                                         back[:, TB * b + i:TB * b + i + 1], start=(i == 0), stop=(i == 1))
                    for i in range(TB):
                        mm = nc.tensor.matmul(small_ps[:, 1, b:b + 1], k.ones[:],
                                              back[:, TB * b + i:TB * b + i + 1], start=(i == 0), stop=(i == 1))
                mm.then_inc(pooled_ready, 1)

            @block.scalar
            def _(act):
                act.wait_ge(shifted, 1)
                nc.scalar.activation(sim[:], sim[:], ACT.Exp).then_inc(exp_ready, 1)
                act.wait_ge(back_shifted, 1)
                nc.scalar.activation(back[:], back[:], ACT.Exp).then_inc(back_exp, 1)
                act.wait_ge(turned_ready, 1)
                nc.scalar.copy(weights_t[:], turned_ps[:]).then_inc(turned_copied, 1)

            @block.vector
            def _(v):
                link = k.vchain
                link(v, nc.vector.tensor_copy(w2_all[:], bc(W("w2"), [P, P])))
                nc.vector.tensor_scalar(keys[:], k.ctx_t[:], W("w3"), W("w1"), ALU.mult, ALU.add)\
                    .then_inc(keys_ready, 1)
                v.wait_ge(sim_ready, 1)
                link(v, nc.vector.tensor_scalar(sim[:], sim_ps[:], W("b_sim"), None, ALU.add))
                nc.vector.tensor_reduce(top[:], sim[:], AX.X, ALU.max).then_inc(sim_taken, 1)
                v.wait_ge(sim_taken, 1)
                nc.vector.tensor_tensor(sim[:], sim[:], bc(top[:].unsqueeze(2), full), ALU.subtract)\
                    .then_inc(shifted, 1)
                v.wait_ge(tops_turned, 1)
                nc.vector.tensor_reduce(top8[:], small_ps[0:T, 0, 0:P], AX.X, ALU.max).then_inc(tops_reduced, 1)
                v.wait_ge(row_ready, 1)
                row = small_ps[0:1, 1, 0:T].rearrange("p (b i) -> p b i", b=B)
                link(v, nc.vector.tensor_copy(tops_row[:], small_ps[0:1, 1, 0:T]))
                pairs = tops_row[:].rearrange("p (b i) -> p b i", b=B)
                nc.vector.tensor_tensor(tops_pair[:], bc(pairs[:, :, 0:1], [1, B, TB]), bc(pairs[:, :, 1:2], [1, B, TB]),
                                        ALU.max).then_inc(pairs_ready, 1)
                v.wait_ge(spread_ready, 1)
                nc.vector.tensor_tensor(back[:], top[:], small_ps[:, 2, 0:T], ALU.subtract).then_inc(back_shifted, 1)
                v.wait_ge(exp_ready, 1)
                link(v, nc.vector.tensor_reduce(total[:], sim[:], AX.X, ALU.add))
                link(v, nc.vector.reciprocal(total[:], total[:]))
                nc.vector.tensor_tensor(sim[:], sim[:], bc(total[:].unsqueeze(2), full), ALU.mult)\
                    .then_inc(soft_ready, 1)
                v.wait_ge(pooled_ready, 1)
                link(v, nc.vector.reciprocal(share[:], small_ps[:, 1, 0:B]))
                link(v, nc.vector.tensor_tensor(pooled[:], small_ps[:, 0, 0:B], share[:], ALU.mult))
                link(v, nc.vector.tensor_tensor(pooled_t[:].rearrange("p (b s) -> p b s", b=B),
                                                k.XT[:].rearrange("p (b s) -> p b s", b=B),
                                                bc(pooled[:].unsqueeze(2), [P, B, S]), ALU.mult))
                v.wait_ge(attended_ready, 1)
                link(v, nc.vector.tensor_copy(attended[:], attended_ps[:]))
                link(v, nc.vector.tensor_tensor(product_t[:], k.XT[:], attended[:], ALU.mult))
        features = [k.XT, attended, product_t, pooled_t]
        psum.close()
        close_sublayer(k, "l2x_close", None, [W("w_qv")[:, c * P:(c + 1) * P] for c in range(4)], 4, bias=W("b_qv"),
                       features_t=features)



SLOTS, F2 = 8 * 64, 4 * P
TS = SLOTS // P
L2F = Pack("l2_ffn")
for _key, _width in (("w1", F2), ("w2", F2), ("slots", TS * P), ("gain_x", P), ("gain_slot", P)):
    L2F.put(_key, _width)


def l2_ffn_layout(i):
    g = lambda key: np.asarray(i["L2_ffn_" + key])
    return L2F.build({"w1": g("w1"), "w2": tile_rows(g("w2")), "slots": tile_rows(g("slot_embeds").reshape(SLOTS, P)),
                      "gain_x": on_all(g("gamma_x")), "gain_slot": on_all(g("gamma_slot"))})


def l2_ffn(k):
    nc = k.nc
    w = k.weights["l2_ffn"]
    W = lambda key: L2F.view(w, key)
    TA = T + TS
    with ExitStack() as ctx:
        sb = lambda name, shape, dt=F32: k.sb("l2f_" + name, shape, dt, ctx)
        rows = sb("rows", [P, TA, P + 1])
        xn_t, slots_t = sb("xn_t", [P, N]), sb("slots_t", [P, SLOTS])
        hidden_in, processed = sb("hidden_in", [P, B * TS, P]), sb("processed", [P, B * TS, P + 1])
        hidden_in_t, hidden = sb("hidden_in_t", [P, B * SLOTS]), sb("hidden", [P, F2 // P, B * SLOTS])
        combined = sb("combined", [P, T, P])
        with ExitStack() as inner:
            squares = k.sb("l2f_squares", [P, TA, P], F32, inner)
            norms, half = k.sb("l2f_norms", [P, TA], F32, inner), k.sb("l2f_half", [P, TA], F32, inner)
            summed, rooted = k.sems("l2f", "summed rooted")
            with nc.Block() as block:

                @block.gpsimd
                def _(g):
                    nc.gpsimd.memset(rows[:, :, P:P + 1], 1.0)
                    nc.gpsimd.memset(processed[:, :, P:P + 1], 1.0)
                    k.gchain(g, nc.gpsimd.memset(half[:], 0.5))
                    g.wait_ge(summed, 1)
                    nc.gpsimd.tensor_tensor(norms[:], norms[:], half[:], ALU.pow).then_inc(rooted, 1)

                @block.vector
                def _(v):
                    link = k.vchain
                    slots = W("slots").rearrange("p (t n) -> p t n", t=TS)
                    nc.vector.tensor_tensor(squares[:, 0:T, :], k.X[:], k.X[:], ALU.mult)
                    link(v, nc.vector.tensor_tensor(squares[:, T:TA, :], slots, slots, ALU.mult))
                    nc.vector.tensor_reduce(norms[:], squares[:], AX.X, ALU.add).then_inc(summed, 1)
                    v.wait_ge(rooted, 1)
                    link(v, nc.vector.tensor_scalar(norms[:], norms[:], 1e-12, None, ALU.max))
                    link(v, nc.vector.reciprocal(norms[:], norms[:]))
                    link(v, nc.vector.tensor_scalar(norms[:], norms[:], float(P) ** 0.5, None, ALU.mult))
                    for at, src, gain in ((slice(0, T), k.X[:], "gain_x"), (slice(T, TA), slots, "gain_slot")):
                        shape = [P, at.stop - at.start, P]
                        link(v, nc.vector.tensor_tensor(squares[:, at, :], src, bc(norms[:, at].unsqueeze(2), shape),
                                                        ALU.mult))
                        link(v, nc.vector.tensor_tensor(rows[:, at, 0:P], squares[:, at, :],
                                                        bc(W(gain).unsqueeze(1), shape), ALU.mult))

        def turn(source, first, count, width=P):
            def issue(pe, out):
                for t in range(count):
                    mm = nc.tensor.transpose(out[:, t * P:(t + 1) * P], source[:, first + t, 0:width], k.ident[:])
                return mm
            return issue
        copy = lambda dst, cols=N: lambda act, out: nc.scalar.copy(dst, out[:, 0:cols])
        products(k, "l2f_turn", [(SCALAR, turn(rows, 0, T), copy(xn_t[:])),
                                 (SCALAR, turn(rows, T, TS), copy(slots_t[:], SLOTS))])

        def dispatch(b, pair):
            def score(out):
                for o in range(2):
                    mm = nc.tensor.matmul(out[:, o, 0:S], slots_t[:, (2 * pair + o) * P:(2 * pair + o + 1) * P],
                                          xn_t[:, b * S:(b + 1) * S], start=True, stop=True)
                return mm

            def product(out, probs_t):
                for o in range(2):
                    for c in range(TB):
                        x = o * TB + c
                        mm = nc.tensor.matmul(out[:, o * (P + 1):(o + 1) * (P + 1)], probs_t[:, x * P:(x + 1) * P],
                                              rows[:, TB * b + c, :], start=(c == 0), stop=(c == TB - 1))
                return mm
            first = b * TS + 2 * pair
            return 2 * S, 2, score, product, hidden_in[:, first:first + 2, :], None

        attention(k, "l2f_dispatch", [dispatch(b, pair) for b in range(B) for pair in range(TS // 2)], 1.0)
        products(k, "l2f_turn2", [(SCALAR, turn(hidden_in, 8 * c, 8), copy(hidden_in_t[:, c * N:(c + 1) * N]))
                                  for c in range(2)])
        products(k, "l2f_up", [(SCALAR, wide(k, W("w1")[:, f * P:(f + 1) * P], hidden_in_t[:, c * N:(c + 1) * N]),
                                activated(k, hidden[:, f, c * N:(c + 1) * N], ACT.Gelu))
                               for c in range(2) for f in range(F2 // P)])

        def down(c):
            def issue(pe, out):
                for t in range(8):
                    at = (8 * c + t) * P
                    for f in range(F2 // P):
                        mm = nc.tensor.matmul(out[:, t * P:(t + 1) * P], hidden[:, f, at:at + P],
                                              W("w2")[:, f * P:(f + 1) * P], start=(f == 0), stop=(f == F2 // P - 1))
                return mm
            return issue
        products(k, "l2f_down", [(VECTOR, down(c), lambda v, out, c=c: nc.vector.tensor_copy(
            processed[:, 8 * c:8 * c + 8, 0:P], out.rearrange("p (t n) -> p t n", n=P))) for c in range(2)])

        def combine(b):
            def score(out):
                for o in range(TB):
                    t = TB * b + o
                    mm = nc.tensor.matmul(out[:, o, :], xn_t[:, t * P:(t + 1) * P], slots_t[:], start=True, stop=True)
                return mm

            def product(out, probs_t):
                for o in range(TB):
                    for c in range(TS):
                        x = o * TS + c
                        mm = nc.tensor.matmul(out[:, o * (P + 1):(o + 1) * (P + 1)], probs_t[:, x * P:(x + 1) * P],
                                              processed[:, b * TS + c, :], start=(c == 0), stop=(c == TS - 1))
                return mm
            return 2 * BANK, 2, score, product, combined[:, TB * b:TB * b + TB, :], None

        attention(k, "l2f_combine", [combine(b) for b in range(B)], 1.0)
        norm_and_turn(k, "l2f_out", k.X[:], k.X[:], k.XT[:], addends=(combined[:],))



L3A = Pack("l3_attn")
for _key, _width in (("wq", P), ("wk", P), ("wv", P), ("wo", P), ("bo", P), ("alpha", 1), ("temperature", 1),
                     ("gamma", P), ("beta", P), ("other_rows", DX * DX)):
    L3A.put(_key, _width)


def l3_attn_layout(i):
    g = lambda key: np.asarray(i["L3_attn_" + key])
    return L3A.build({"wq": g("Wq").T, "wk": g("Wk").T, "wv": g("Wv").T, "wo": g("Wo").T, "bo": on_all(g("bo")),
                      "alpha": on_all(g("alpha")), "temperature": on_all(g("temperature")), "gamma": on_all(g("gamma")),
                      "beta": on_all(g("beta")),
                      "other_rows": np.broadcast_to(1.0 - np.eye(DX).reshape(1, -1), (P, DX * DX))})


def l3_attn(k):
    nc = k.nc
    w = k.weights["l3_attn"]
    W = lambda key: L3A.view(w, key)
    M = B * HX
    with ExitStack() as ctx:
        sb = lambda name, shape, dt=F32: k.sb("l3a_" + name, shape, dt, ctx)
        x_in, inner, inner_t = sb("x_in", [P, T, P]), sb("inner", [P, T, P]), sb("inner_t", [P, N])
        q_t, kv, out_t = sb("q_t", [P, N]), sb("kv", [P, T, 2 * P]), sb("out_t", [P, N])
        products(k, "l3a_proj", [
            (SCALAR, by_tile(k, k.XT, W("wk"), P), lambda act, out: nc.scalar.copy(
                kv[:, :, 0:P], out.rearrange("p (t n) -> p t n", n=P))),
            (VECTOR, by_tile(k, k.XT, W("wv"), P), lambda v, out: nc.vector.tensor_copy(
                kv[:, :, P:2 * P], out.rearrange("p (t n) -> p t n", n=P))),
            (SCALAR, wide(k, W("wq"), k.XT), activated(k, q_t[:])),
            ])
        with ExitStack() as att:
            psum = k.ps("l3a_gram_ps", [P, B, 2 * P], att)
            out_ps = k.ps("l3a_out_ps", [P, N], att)
            tmp = k.sb("l3a_tmp", [P, 2 * B, HX, DX], F32, att)
            own = k.sb("l3a_own", [P, B, 2, DX], F32, att)
            system = k.sb("l3a_system", [M, DX, 2 * DX], F32, att)
            row = k.sb("l3a_row", [M, 2 * DX], F32, att)
            factor, pivot = k.sb("l3a_factor", [M, DX], F32, att), k.sb("l3a_pivot", [M, 1], F32, att)
            outer = k.sb("l3a_outer", [M, DX, 2 * DX], F32, att)
            solved, top = k.sb("l3a_solved", [M, DX, DX], F32, att), k.sb("l3a_top", [M, DX], F32, att)
            maps = k.sb("l3a_maps", [P, B, DX], F32, att)
            maps_wide = k.sb("l3a_maps_wide", [P, B, HX, DX], F32, att)
            gram_dram = nc.dram_tensor("l3a_gram", (P, B * 2 * DX), F32, kind="Internal").ap()
            maps_dram = nc.dram_tensor("l3a_maps_dram", (M, DX * DX), F32, kind="Internal").ap()
            (gram_ready, own_ready, gram_stored, gram_loaded, shifted, exp_ready, solved_ready, maps_stored,
             maps_loaded, maps_ready, out_ready) = k.sems(
                "l3a", "gram_ready own_ready gram_stored gram_loaded shifted exp_ready solved_ready maps_stored "
                "maps_loaded maps_ready out_ready")
            with nc.Block() as block:

                @block.tensor
                def _(pe):
                    for b in range(B):
                        for i in range(TB):
                            mm = nc.tensor.matmul(psum[:, b, :], kv[:, TB * b + i, 0:P], kv[:, TB * b + i, :],
                                                  start=(i == 0), stop=(i == TB - 1))
                    mm.then_inc(gram_ready, 1)
                    pe.wait_ge(maps_ready, 1)
                    for b in range(B):
                        mm = nc.tensor.matmul(out_ps[:, b * S:(b + 1) * S], maps_wide[:, b].rearrange("p h e -> p (h e)"),
                                              q_t[:, b * S:(b + 1) * S], start=True, stop=True)
                    mm.then_inc(out_ready, 1)

                @block.scalar
                def _(act):
                    act.wait_ge(shifted, 1)
                    nc.scalar.activation(solved[:], solved[:], ACT.Exp).then_inc(exp_ready, 1)
                    act.wait_ge(out_ready, 1)
                    nc.scalar.copy(out_t[:], out_ps[:])

                @block.sync
                def _(sp):
                    sp.wait_ge(own_ready, 1)
                    sp.dma_start(gram_dram, own[:].rearrange("p b s e -> p (b s e)")).then_inc(gram_stored, 16)
                    sp.wait_ge(gram_stored, 16)
                    for b in range(B):
                        sp.dma_start(system[b * HX:(b + 1) * HX],
                                     gram_dram.rearrange("(h d) (b e) -> b h d e", d=DX, b=B)[b]).then_inc(gram_loaded, 16)
                    sp.wait_ge(solved_ready, 1)
                    sp.dma_start(maps_dram, solved[:].rearrange("m d e -> m (d e)")).then_inc(maps_stored, 16)
                    sp.wait_ge(maps_stored, 16)
                    for b in range(B):
                        sp.dma_start(maps[:, b, :], maps_dram[b * HX:(b + 1) * HX, :]
                                     .rearrange("h (d e) -> (h d) e", d=DX)).then_inc(maps_loaded, 16)

                @block.vector
                def _(v):
                    link = k.vchain
                    nc.vector.tensor_copy(x_in[:], k.X[:])
                    v.wait_ge(gram_ready, 1)
                    link(v, nc.vector.tensor_tensor(
                        tmp[:], psum[:].rearrange("p b (s h e) -> p (b s) h e", s=2, h=HX),
                        bc(k.own_head.unsqueeze(1).unsqueeze(3), [P, 2 * B, HX, DX]), ALU.mult))
                    nc.vector.tensor_reduce(own[:].rearrange("p b s e -> p (b s) e"),
                                            tmp[:].rearrange("p x h e -> p x e h"), AX.X, ALU.add)\
                        .then_inc(own_ready, 1)
                    v.wait_ge(gram_loaded, 16 * B)
                    flat = system[:].rearrange("m d e -> m (d e)")
                    diagonal = flat[:, 0:DX * 2 * DX:2 * DX + 1]
                    link(v, nc.vector.tensor_scalar(diagonal, diagonal, W("alpha")[0:M], None, ALU.add))
                    others = W("other_rows").rearrange("p (a b) -> p a b", a=DX)[0:M]
                    for p in range(DX):
                        link(v, nc.vector.reciprocal(pivot[:], system[:, p, p:p + 1]))
                        link(v, nc.vector.tensor_scalar(row[:], system[:, p, :], pivot[:], None, ALU.mult))
                        link(v, nc.vector.tensor_tensor(factor[:], system[:, :, p], others[:, p, :], ALU.mult))
                        link(v, nc.vector.tensor_tensor(outer[:], bc(factor[:].unsqueeze(2), [M, DX, 2 * DX]),
                                                        bc(row[:].unsqueeze(1), [M, DX, 2 * DX]), ALU.mult))
                        link(v, nc.vector.tensor_tensor(system[:], system[:], outer[:], ALU.subtract))
                        link(v, nc.vector.tensor_copy(system[:, p, :], row[:]))
                    link(v, nc.vector.reciprocal(pivot[:], W("temperature")[0:M]))
                    link(v, nc.vector.tensor_scalar(solved[:], system[:, :, DX:2 * DX], pivot[:], None, ALU.mult))
                    by_e = solved[:].rearrange("m d e -> m e d")
                    spread = lambda: bc(top[:].unsqueeze(1), [M, DX, DX])
                    link(v, nc.vector.tensor_reduce(top[:], by_e, AX.X, ALU.max))
                    nc.vector.tensor_tensor(solved[:], solved[:], spread(), ALU.subtract).then_inc(shifted, 1)
                    v.wait_ge(exp_ready, 1)
                    link(v, nc.vector.tensor_reduce(top[:], by_e, AX.X, ALU.add))
                    link(v, nc.vector.reciprocal(top[:], top[:]))
                    nc.vector.tensor_tensor(solved[:], solved[:], spread(), ALU.mult).then_inc(solved_ready, 1)
                    v.wait_ge(maps_loaded, 16 * B)
                    for b in range(B):
                        ins = nc.vector.tensor_tensor(maps_wide[:, b], bc(maps[:, b, :].unsqueeze(1), [P, HX, DX]),
                                                      bc(k.own_head.unsqueeze(2), [P, HX, DX]), ALU.mult)
                    ins.then_inc(maps_ready, 1)
        close_sublayer(k, "l3a_close", None, [W("wo")], 1, bias=W("bo"), features_t=[out_t],
                       to=(inner[:], inner_t[:]), gain=W("gamma"), shift=W("beta"))
        norm_and_turn(k, "l3a_out", inner[:], k.X[:], k.XT[:], addends=(x_in[:],))



H3, D3 = 16, 64
PAIRS = H3 * D3 // P
L3X = Pack("l3_xattn")
for _key, _width in (("wq", H3 * D3), ("wk", H3 * D3), ("wv", H3 * D3), ("wo", PAIRS * P), ("bq", PAIRS),
                     ("bk", PAIRS), ("bv", H3 * D3), ("bo", P)):
    L3X.put(_key, _width)


def l3_xattn_layout(i):
    g = lambda key: np.asarray(i["L3_xattn_" + key])
    wide_of = lambda x: g(x).transpose(1, 0, 2).reshape(P, H3 * D3)
    return L3X.build({"wq": wide_of("Wq"), "wk": wide_of("Wk"), "wv": wide_of("Wv"), "wo": tile_rows(g("Wo")),
                      "bq": g("bq").reshape(PAIRS, P).T, "bk": g("bk").reshape(PAIRS, P).T,
                      "bv": on_all(g("bv").reshape(-1)), "bo": on_all(g("bo"))})


def l3_xattn(k):
    nc = k.nc
    w = k.weights["l3_xattn"]
    W = lambda key: L3X.view(w, key)
    with ExitStack() as ctx:
        sb = lambda name, shape, dt=F32: k.sb("l3x_" + name, shape, dt, ctx)
        heads_out = sb("heads_out", [P, T, H3 * D3])
        with ExitStack() as att:
            sb = lambda name, shape, dt=F32: k.sb("l3x_" + name, shape, dt, att)
            q_t = sb("q_t", [P, PAIRS, N])
            keys = sb("keys", [P, PAIRS, B, 2, SC])
            values = sb("values", [P, B, H3, D3])
            v_tmp = sb("v_tmp", [P, H3, D3])
            keep, add = sb("keep", [P, T, SC]), sb("add", [P, T, SC])
            with nc.Block() as block:

                @block.gpsimd
                def _(g):
                    nc.gpsimd.memset(keys[:], 0.0)

                @block.vector
                def _(v):
                    k.vchain(v, nc.vector.tensor_scalar(keep[:], k.mask3[:], 0.0, None, ALU.is_equal))
                    nc.vector.tensor_scalar(add[:], keep[:], 1.0, 1e9 * D3 ** 0.5, ALU.subtract, ALU.mult)

            def four_keys(c):
                def issue(pe, out):
                    for j in range(4):
                        x = 4 * c + j
                        mm = nc.tensor.matmul(out[:, j * B * SC:(j + 1) * B * SC], W("wk")[:, x * P:(x + 1) * P],
                                              k.ctx_t[:], start=True, stop=True)
                    return mm
                return issue

            def take_keys(c):
                def take(act, out):
                    for j in range(4):
                        x = 4 * c + j
                        for half in range(2):
                            part = slice(half * D3, (half + 1) * D3)
                            ins = nc.scalar.activation(
                                keys[part, x, :, half, :],
                                out[part, j * B * SC:(j + 1) * B * SC].rearrange("p (b s) -> p b s", b=B),
                                ACT.Identity, bias=W("bk")[part, x:x + 1])
                    return ins
                return take

            def take_values(b):
                def take(v, out):
                    k.vchain(v, nc.vector.tensor_tensor(v_tmp[:].rearrange("p h d -> p (h d)"), out, W("bv"), ALU.add))
                    return nc.vector.tensor_tensor(values[:, b], v_tmp[:],
                                                   bc(k.own_parity.unsqueeze(2), [P, H3, D3]), ALU.mult)
                return take

            products(k, "l3x_proj", [(SCALAR, four_keys(c), take_keys(c)) for c in range(2)] + [
                (VECTOR, wide(k, k.ctx_twice[:, b].rearrange("p a s -> p (a s)"), W("wv")), take_values(b))
                for b in range(B)] + [
                (SCALAR, wide(k, W("wq")[:, x * P:(x + 1) * P], k.XT),
                 activated(k, q_t[:, x, :], bias=W("bq")[:, x:x + 1])) for x in range(PAIRS)])

            def unit(t):
                b = t // TB

                def score(out):
                    for x in range(PAIRS):
                        mm = nc.tensor.matmul(out[:, x // 4, (x % 4) * P:(x % 4 + 1) * P],
                                              q_t[:, x, t * P:(t + 1) * P], keys[:, x, b], start=True, stop=True)
                    return mm

                def product(out, probs_t):
                    for x in range(PAIRS):
                        mm = nc.tensor.matmul(out[:, x * P:(x + 1) * P], probs_t[:, x * P:(x + 1) * P],
                                              values[:, b, 2 * x:2 * x + 2, :], start=True, stop=True)
                    return mm
                return (2 * BANK, H3, score, product, heads_out[:, t].rearrange("p (h d) -> p h d", h=H3),
                        (keep[:, t, :], add[:, t, :]))

            attention(k, "l3x_att", [unit(t) for t in range(T)], D3 ** -0.5, wide_out=True)
        close_sublayer(k, "l3x_close", heads_out[:], [W("wo")[:, c * P:(c + 1) * P] for c in range(PAIRS)], PAIRS,
                       bias=W("bo"))



DEPTH, HL, DL, WINDOW = 2, 8, 64, 64
INNER = HL * DL
HID = int(P * 4 * 2 / 3)
CHUNKS = [(0, P), (P, P), (2 * P, HID - 2 * P)]
L3F = Pack("l3_ffn")
for _l in range(DEPTH):
    for _key, _width in (("wqkv", 3 * INNER), ("wo", INNER), ("w1", 2 * HID), ("w2", 3 * P), ("b1", 6), ("b2", P),
                         ("ln_g", P), ("ln_b", P), ("q_scale", DL), ("q_swapped", DL), ("k_scale", DL),
                         ("k_swapped", DL)):
        L3F.put(_key + str(_l), _width)
for _key in ("cos_q", "sin_q", "cos_k", "sin_k"):
    L3F.put(_key, TB * DL)


def l3_ffn_layout(i):
    g = lambda key, l: np.asarray(i["L3_ffn_" + key])[l]
    swap = np.r_[DL // 2:DL, 0:DL // 2]
    parts = {}

    def padded(a, n):
        out = np.zeros((n,) + a.shape[1:], a.dtype)
        out[:a.shape[0]] = a
        return out
    for l in range(DEPTH):
        b1 = g("b1", l)
        columns = [padded(b1[half * HID + first:half * HID + first + n], P) for half in range(2) for first, n in CHUNKS]
        parts.update({f"wqkv{l}": g("wqkv", l), f"wo{l}": tile_rows(g("wo", l)), f"w1{l}": g("w1", l),
                      f"w2{l}": tile_rows(padded(g("w2", l), 3 * P)), f"b1{l}": np.stack(columns, axis=1),
                      f"b2{l}": on_all(g("b2", l)), f"ln_g{l}": on_all(g("ln_g", l)), f"ln_b{l}": on_all(g("ln_b", l)),
                      f"q_scale{l}": on_all(g("q_scale", l)), f"q_swapped{l}": on_all(g("q_scale", l)[swap]),
                      f"k_scale{l}": on_all(g("k_scale", l)), f"k_swapped{l}": on_all(g("k_scale", l)[swap])})
    f = np.float32
    half = np.arange(0, DL, 2, dtype=f)
    t = np.arange(S, dtype=f)
    freqs = t[:, None] * (f(1.0) / f(10000.0) ** (half / f(DL)))[None, :]
    freqs = np.concatenate([freqs, freqs], axis=1).astype(np.float64)
    base = (half + 0.4 * DL) / (1.4 * DL)
    scale = base[None, :].astype(np.float64) ** ((t - S // 2) / (WINDOW // 2))[:, None]
    scale = np.concatenate([scale, scale], axis=1)
    sign = np.r_[-np.ones(DL // 2), np.ones(DL // 2)]
    for key, table in (("cos_q", np.cos(freqs) * scale), ("sin_q", np.sin(freqs) * scale * sign),
                       ("cos_k", np.cos(freqs) / scale), ("sin_k", np.sin(freqs) / scale * sign)):
        parts[key] = tile_rows(table.astype(f))
    return L3F.build(parts)


def shift_tokens(k, dst, extra=None):
    nc = k.nc
    H = P // 2
    with nc.Block() as block:

        @block.vector
        def _(v):
            nc.vector.tensor_copy(dst[0:H, :], k.XT[0:H, :])
            nc.vector.memset(dst[H:P].rearrange("p (b s) -> p b s", b=B)[:, :, 0:1], 0.0)

        @block.scalar
        def _(act):
            nc.scalar.copy(dst[H:P].rearrange("p (b s) -> p b s", b=B)[:, :, 1:S],
                           k.XT[H:P].rearrange("p (b s) -> p b s", b=B)[:, :, 0:S - 1])


def l3_ffn(k):
    nc = k.nc
    with ExitStack() as ctx:
        x_in = k.sb("l3f_x_in", [P, T, P], F32, ctx)
        shifted = k.sb("l3f_shifted", [P, N], F32, ctx)
        far_own, far_before = (k.sb("l3f_" + x, [P, P], BF16, ctx) for x in ("far_own", "far_before"))
        with nc.Block() as block:

            @block.vector
            def _(v):
                nc.vector.tensor_copy(x_in[:], k.X[:])

            @block.gpsimd
            def _(g):
                nc.gpsimd.memset(far_own[:], 0.0)
                k.gchain(g, nc.gpsimd.memset(far_before[:], 0.0))
                k.gchain(g, nc.gpsimd.affine_select(out=far_own[:], in_=far_own[:], compare_op=ALU.is_ge, fill=1.0,
                                                    base=0, pattern=[[1, P]], channel_multiplier=-1))
                nc.gpsimd.affine_select(out=far_own[:], in_=far_own[:], compare_op=ALU.is_ge, fill=1.0,
                                        base=WINDOW, pattern=[[-1, P]], channel_multiplier=1)
                nc.gpsimd.affine_select(out=far_before[:], in_=far_before[:], compare_op=ALU.is_ge, fill=1.0,
                                        base=WINDOW - P, pattern=[[-1, P]], channel_multiplier=1)
        for l in range(DEPTH):
            l3_ffn_attention(k, l, shifted, far_own, far_before)
            l3_ffn_net(k, l, shifted, x_in)


def l3_ffn_attention(k, l, shifted, far_own, far_before):
    nc = k.nc
    w = k.weights["l3_ffn"]
    W = lambda key: L3F.view(w, f"{key}{l}")
    table = lambda key: L3F.view(w, key).rearrange("p (i d) -> p i d", i=TB)
    tag = f"l3f{l}"
    with ExitStack() as ctx:
        sb = lambda name, shape, dt=F32: k.sb(f"{tag}_{name}", shape, dt, ctx)
        heads_out = sb("heads_out", [P, T, INNER])
        with ExitStack() as att:
            sb = lambda name, shape, dt=F32: k.sb(f"{tag}_{name}", shape, dt, att)
            values = sb("values", [P, T, HL, DL + 1])
            q_t, k_t = sb("q_t", [P, HL // 2, N]), sb("k_t", [P, HL // 2, N])
            with ExitStack() as unturned:
                rows = {"q": k.sb(f"{tag}_q", [P, T, INNER], F32, unturned), "k": k.sb(f"{tag}_k", [P, T, INNER], F32, unturned)}
                shift_tokens(k, shifted)

                def two_tiles(part, c):
                    def issue(pe, out):
                        for j in range(2):
                            t = 2 * c + j
                            mm = nc.tensor.matmul(out[:, j * INNER:(j + 1) * INNER], shifted[:, t * P:(t + 1) * P],
                                                  W("wqkv")[:, part * INNER:(part + 1) * INNER], start=True, stop=True)
                        return mm
                    return issue
                both = lambda out: out.rearrange("p (t n) -> p t n", t=2)
                products(k, tag + "_qkv", [e for c in range(T // 2) for e in (
                    (SCALAR, two_tiles(0, c), lambda act, out, c=c: nc.scalar.copy(rows["q"][:, 2 * c:2 * c + 2], both(out))),
                    (VECTOR, two_tiles(1, c), lambda v, out, c=c: nc.vector.tensor_copy(rows["k"][:, 2 * c:2 * c + 2],
                                                                                      both(out))),
                    (SCALAR, two_tiles(2, c), lambda act, out, c=c: nc.scalar.copy(
                        values[:, 2 * c:2 * c + 2, :, 0:DL].rearrange("p t h d -> p (t h) d"),
                        out.rearrange("p (x d) -> p x d", d=DL))))])
                l3_ffn_rotate(k, tag, W, table, rows, {"q": q_t, "k": k_t}, values, heads_out)

            def unit(t, g):
                b, i = divmod(t, TB)
                width = (i + 1) * P

                def score(out):
                    for o in range(2):
                        for y in range(2):
                            at = out[:, o, y * width:(y + 1) * width]
                            if i:
                                nc.tensor.matmul(at[:, 0:P], far_before[:], k.masker[:], start=True, stop=False,
                                                 skip_group_check=True)
                            nc.tensor.matmul(at[:, i * P:(i + 1) * P], far_own[:], k.masker[:], start=(i == 0),
                                             stop=False, skip_group_check=True)
                            part = slice(o * DL, (o + 1) * DL)
                            mm = nc.tensor.matmul(at, q_t[part, 2 * g + y, t * P:(t + 1) * P],
                                                  k_t[part, 2 * g + y, b * S:b * S + width], start=False, stop=True,
                                                  skip_group_check=True)
                    return mm

                def product(out, probs_t):
                    for o in range(2):
                        for y in range(2):
                            for c in range(i + 1):
                                x = (o * 2 + y) * (i + 1) + c
                                mm = nc.tensor.matmul(out[:, (o * 2 + y) * (DL + 1):(o * 2 + y + 1) * (DL + 1)],
                                                      probs_t[:, x * P:(x + 1) * P],
                                                      values[:, TB * b + c, 4 * g + 2 * y + o, :], start=(c == 0),
                                                      stop=(c == i))
                    return mm
                dest = heads_out[:, t, 4 * g * DL:4 * (g + 1) * DL].rearrange("p (y o d) -> p o y d", y=2, o=2)
                return 4 * width, 4, score, product, dest, None

            attention(k, tag + "_att", [unit(t, g) for t in range(T) for g in range(2)], 8.0)
        close_sublayer(k, tag + "_mid", heads_out[:], [W("wo")[:, c * P:(c + 1) * P] for c in range(INNER // P)],
                       INNER // P, norm=False)


def l3_ffn_rotate(k, tag, W, table, rows, turned, values, parts):
    nc = k.nc
    tiles = [(x, t) for x in "qk" for t in range(T)]
    halves = ((slice(0, DL // 2), slice(DL // 2, DL)), (slice(DL // 2, DL), slice(0, DL // 2)))
    with ExitStack() as ctx:
        sb = lambda name, shape: k.sb(f"{tag}r_{name}", shape, F32, ctx)
        length = sb("length", [P, 2, T * HL])
        tables = {x: sb("table_" + x, [P, TB, DL]) for x in ("cos_q", "sin_q", "cos_k", "sin_k")}
        turned_ps = k.ps(f"{tag}r_turned_ps", [P, 4, BANK], ctx)
        squared, summed, rooted, tables_ready, part_ready, tile_ready, turned_ready, turned_copied = k.sems(
            tag + "r", "squared summed rooted tables_ready part_ready tile_ready turned_ready turned_copied")
        squares = {x: turned[x][:].rearrange("p a n -> p (a n)").rearrange("p (a d) -> p a d", d=DL) for x in "qk"}
        heads = {x: rows[x][:].rearrange("p t (h d) -> p (t h) d", d=DL) for x in "qk"}
        part_of = lambda t: parts[:, t].rearrange("p (h d) -> p h d", h=HL)
        with nc.Block() as block:

            @block.gpsimd
            def _(g):
                nc.gpsimd.memset(values[:, :, :, DL:DL + 1], 1.0)
                g.wait_ge(tables_ready, 1)
                for n, (x, t) in enumerate(tiles):
                    if n >= T:
                        g.wait_ge(tile_ready, n - T + 1)
                    one = rows[x][:, t].rearrange("p (h d) -> p h d", h=HL)
                    for to, of in halves:
                        last = nc.gpsimd.tensor_tensor(part_of(t)[:, :, to], one[:, :, of], bc(
                            tables["sin_" + x][:, t % TB, to].unsqueeze(1), [P, HL, DL // 2]), ALU.mult)
                    last.then_inc(part_ready, 1)

            @block.scalar
            def _(act):
                for x in "qk":
                    nc.scalar.activation(squares[x], heads[x], ACT.Square).then_inc(squared, 1)
                act.wait_ge(summed, 1)
                nc.scalar.activation(length[:], length[:], ACT.Sqrt).then_inc(rooted, 1)
                for n, (x, t) in enumerate(tiles):
                    act.wait_ge(turned_ready, n + 1)
                    nc.scalar.copy(turned[x][:, :, t * P:(t + 1) * P],
                                   turned_ps[:, n % 4].rearrange("p (a n) -> p a n", n=P)).then_inc(turned_copied, 1)

            @block.vector
            def _(v):
                link = k.vchain
                for x in "qk":
                    for trig, by in (("cos_", "_scale"), ("sin_", "_swapped")):
                        last = nc.vector.tensor_tensor(tables[trig + x][:], table(trig + x),
                                                       bc(W(x + by).unsqueeze(1), [P, TB, DL]), ALU.mult)
                last.then_inc(tables_ready, 1)
                v.wait_ge(tables_ready, 1)
                for n, x in enumerate("qk"):
                    v.wait_ge(squared, n + 1)
                    last = nc.vector.tensor_reduce(length[:, n, :], squares[x], AX.X, ALU.add)
                last.then_inc(summed, 1)
                v.wait_ge(rooted, 1)
                link(v, nc.vector.tensor_scalar(length[:], length[:], 1e-12, None, ALU.max))
                link(v, nc.vector.reciprocal(length[:], length[:]))
                for n, (x, t) in enumerate(tiles):
                    one = rows[x][:, t].rearrange("p (h d) -> p h d", h=HL)
                    v.wait_ge(part_ready, n + 1)
                    link(v, nc.vector.tensor_tensor(one, one, bc(tables["cos_" + x][:, t % TB].unsqueeze(1),
                                                                 [P, HL, DL]), ALU.mult))
                    link(v, nc.vector.tensor_tensor(one, one, part_of(t), ALU.add))
                    lengths = length[:, "qk".index(x), t * HL:(t + 1) * HL].unsqueeze(2)
                    nc.vector.tensor_tensor(one, one, bc(lengths, [P, HL, DL]), ALU.mult).then_inc(tile_ready, 1)

            @block.tensor
            def _(pe):
                for n, (x, t) in enumerate(tiles):
                    pe.wait_ge(tile_ready, n + 1)
                    if n >= 4:
                        pe.wait_ge(turned_copied, n - 3)
                    for a in range(HL // 2):
                        mm = nc.tensor.transpose(turned_ps[:, n % 4, a * P:(a + 1) * P],
                                                 rows[x][:, t, a * P:(a + 1) * P], k.ident[:])
                    mm.then_inc(turned_ready, 1)


def l3_ffn_net(k, l, shifted, x_in):
    nc = k.nc
    w = k.weights["l3_ffn"]
    W = lambda key: L3F.view(w, f"{key}{l}")
    tag = f"l3n{l}"
    with ExitStack() as ctx:
        sb = lambda name, shape, dt=F32: k.sb(f"{tag}_{name}", shape, dt, ctx)
        rows, normed = sb("rows", [P, T, P]), sb("normed", [P, N])
        act_part, hidden = sb("act_part", [P, 3, N]), sb("hidden", [P, 3, N])
        shift_tokens(k, shifted)

        def token_major(pe, out):
            for t in range(T):
                mm = nc.tensor.transpose(out[:, t * P:(t + 1) * P], shifted[:, t * P:(t + 1) * P], k.ident[:])
            return mm
        products(k, tag + "_rows", [(SCALAR, token_major, activated(k, rows[:].rearrange("p t n -> p (t n)")))])
        norm_and_turn(k, tag + "_norm", rows[:], rows[:], normed[:], W("ln_g"), W("ln_b"))
        products(k, tag + "_g", [(SCALAR, wide(k, W("w1")[:, HID + first:HID + first + n], normed, n),
                                  activated(k, act_part[0:n, c, :], ACT.Gelu, W("b1")[0:n, 3 + c:4 + c], n))
                                 for c, (first, n) in enumerate(CHUNKS)])
        products(k, tag + "_a", [(VECTOR, wide(k, W("w1")[:, first:first + n], normed, n),
                                  lambda v, out, c=c, n=n: nc.vector.scalar_tensor_tensor(
                                      hidden[0:n, c, :], out[0:n, :], W("b1")[0:n, c:c + 1], act_part[0:n, c, :],
                                      ALU.add, ALU.mult))
                                 for c, (first, n) in enumerate(CHUNKS)])
        end = l == DEPTH - 1
        close_sublayer(k, tag + "_close", None, [W("w2")[0:n, c * P:(c + 1) * P] for c, (_, n) in enumerate(CHUNKS)], 3,
                       bias=W("b2"), features_t=[hidden[0:n, c, :] for c, (_, n) in enumerate(CHUNKS)],
                       addend=x_in[:] if end else None, norm=end)


MARKS = Pack("marks")
for _key, _width in (("own_head", HX), ("own_of_four", 4), ("own_parity", HX)):
    MARKS.put(_key, _width)


def marks_layout(i):
    head = np.arange(P)[:, None] // DX
    return MARKS.build({"own_head": head == np.arange(HX), "own_of_four": head % 4 == np.arange(4),
                        "own_parity": np.arange(P)[:, None] // SC == np.arange(HX) % 2})


def other_layouts(i):
    ctx_t = np.asarray(i["ctx_1024"]).transpose(2, 0, 1)
    return {
        "ctx_t": np.ascontiguousarray(ctx_t.reshape(P, B * SC)),
        "ctx_twice": np.ascontiguousarray(np.stack([ctx_t, ctx_t], axis=2)),
        "ctx_rows": np.ascontiguousarray(np.asarray(i["ctx_1024"]).transpose(1, 0, 2)),
        "l1_experts": l1_experts_layout(i),
        "marks": marks_layout(i),
        "mask3": np.ascontiguousarray(np.asarray(i["mask_BxSxS2_bk1"]).reshape(T, P, SC)
                                      .transpose(1, 0, 2).astype(np.int32)),
        "mask0": np.ascontiguousarray(np.asarray(i["mask_1x1xSxS2_ik1"]).reshape(TB, P, SC).transpose(1, 0, 2)),
        "l0_experts": l0_experts_layout(i),
    }



WEIGHTS = {"l0_attn": (L0A, l0_attn_layout), "l0_xattn": (L0X, l0_xattn_layout), "l0_ffn": (L0F, l0_ffn_layout),
           "l1_attn": (L1A, l1_attn_layout), "l1_xattn": (L1X, l1_xattn_layout), "l1_ffn": (L1F, l1_ffn_layout),
           "l2_attn": (L2A, l2_attn_layout), "l2_xattn": (L2X, l2_xattn_layout), "l2_ffn": (L2F, l2_ffn_layout),
           "l3_attn": (L3A, l3_attn_layout), "l3_xattn": (L3X, l3_xattn_layout), "l3_ffn": (L3F, l3_ffn_layout)}
SUBLAYERS = [l0_attn, l0_xattn, l0_ffn, l1_attn, l1_xattn, l1_ffn, l2_attn, l2_xattn, l2_ffn, l3_attn, l3_xattn,
             l3_ffn]
LARGE, LARGE_LATER = "l0_attn", "l3_xattn"
SMALL = ["l0_xattn", "l0_ffn", "l1_attn", "l1_xattn", "l1_ffn", "l2_attn", "l2_xattn", "l2_ffn"]
SMALL_LATER = "l3_ffn"
LARGE_OVER, SMALL_OVER = 1, 9
LARGE_LATER_USED, SMALL_LATER_USED = 10, 11


def place_weights(k):
    widths = {name: pack.width for name, (pack, _) in WEIGHTS.items()}
    large = k.sb("large_weights", [P, max(widths[LARGE], widths[LARGE_LATER])])
    small = k.sb("small_weights", [P, max(sum(widths[x] for x in SMALL), widths[SMALL_LATER])])
    k.weights = {x: large[:, 0:widths[x]] for x in (LARGE, LARGE_LATER)}
    k.weights["l3_attn"] = k.sb("l3_attn_weights", [P, widths["l3_attn"]])[:]
    k.weights[SMALL_LATER] = small[:, 0:widths[SMALL_LATER]]
    at = 0
    for x in SMALL:
        k.weights[x] = small[:, at:at + widths[x]]
        at += widths[x]


def first_loads(k, others):
    nc, dram = k.nc, k.dram
    k.loaded_first, k.loaded_projections, k.loaded_rest, k.loaded_large, k.loaded_small = k.sems(
        "loaded", "first projections rest large small")
    w, source = k.weights[LARGE], dram["w_" + LARGE]
    heads, out = L0A.at["wq"][0], L0A.at["wo"][0]
    rest = [(w[:, out:], source[:, out:])] + others + [(k.weights[x], dram["w_" + x]) for x in SMALL + ["l3_attn"]]
    k.rest_signals = 16 * len(rest)
    with nc.Block() as block:

        @block.sync
        def _(sp):
            sp.dma_start(k.XT[:], dram["xt"]).then_inc(k.loaded_first, 16)
            sp.dma_start(w[:, 0:heads], source[:, 0:heads]).then_inc(k.loaded_first, 16)
            sp.dma_start(w[:, heads:out], source[:, heads:out]).then_inc(k.loaded_projections, 16)
            for dst, src in rest:
                sp.dma_start(dst, src).then_inc(k.loaded_rest, 16)
            sp.wait_ge(k.loaded_first, 32)


def later_load(k, name, signal):
    with k.nc.Block() as block:

        @block.sync
        def _(sp):
            sp.wait_ge(k.loaded_projections, 16)
            sp.wait_ge(k.loaded_rest, k.rest_signals)
            sp.dma_start(k.weights[name], k.dram["w_" + name]).then_inc(signal, 16)


def arrived(k, signal):
    with k.nc.Block() as block:

        @block.sync
        def _(sp):
            sp.wait_ge(signal, 16)


def decoder(nc, dram):
    with ExitStack() as ctx:
        k = Core(nc, ctx, dram)
        k.quarter = k.sb("quarter", [P, 1])
        k.ctx_t = k.sb("ctx_t", [P, B * SC])
        k.ctx_twice = k.sb("ctx_twice", [P, B, 2, SC])
        k.ctx_rows = k.sb("ctx_rows", [SC, B, P])
        k.mask0 = k.sb("mask0", [P, TB, SC], I32)
        k.mask3 = k.sb("mask3", [P, T, SC], I32)
        k.marks = k.sb("marks", [P, MARKS.width])
        k.own_head, k.own_of_four, k.own_parity = (MARKS.view(k.marks, x)
                                                   for x in ("own_head", "own_of_four", "own_parity"))
        place_weights(k)
        constants(k)
        first_loads(k, [
            (k.X[:], dram["x"].rearrange("b (i p) d -> p (b i) d", p=P)), (k.marks[:], dram["marks"]),
            (k.ctx_t[:], dram["ctx_t"]), (k.ctx_twice[:], dram["ctx_twice"]), (k.ctx_rows[:], dram["ctx_rows"]),
            (k.mask0[:], dram["mask0"]), (k.mask3[:], dram["mask3"])])
        for n, sublayer in enumerate(SUBLAYERS):
            if n == LARGE_OVER:
                later_load(k, LARGE_LATER, k.loaded_large)
            if n == SMALL_OVER:
                later_load(k, SMALL_LATER, k.loaded_small)
            if n == LARGE_LATER_USED:
                arrived(k, k.loaded_large)
            if n == SMALL_LATER_USED:
                arrived(k, k.loaded_small)
            sublayer(k)
        stored = k.sem("stored")
        with nc.Block() as block:

            @block.sync
            def _(sp):
                sp.dma_start(dram["out"].rearrange("b (i p) d -> p (b i) d", p=P), k.X[:]).then_inc(stored, 16)
                sp.wait_ge(stored, 16)


def kernel(**inputs):
    from concourse import bacc
    from concourse.bass_utils import run_bass_kernel_spmd

    x = np.asarray(inputs["x"])
    arrays = {"x": x, "xt": np.ascontiguousarray(x.reshape(N, P).T)}
    arrays.update({"w_" + name: layout(inputs) for name, (_, layout) in WEIGHTS.items()})
    arrays.update(other_layouts(inputs))
    nc = bacc.Bacc("TRN2", target_bir_lowering=False, num_devices=1)
    dram = {name: nc.dram_tensor("in_" + name, a.shape, mybir.dt.from_np(a.dtype), kind="ExternalInput").ap()
            for name, a in arrays.items()}
    dram["out"] = nc.dram_tensor("out", (B, S, P), F32, kind="ExternalOutput").ap()
    decoder(nc, dram)
    result = run_bass_kernel_spmd(nc, [{"in_" + name: a for name, a in arrays.items()}], core_ids=[0])
    return result.results[0]["out"]
```
